# Optimizing a Trainium2 kernel written in Bass

```python
import numpy as np
import jax
import jax.numpy as jnp

def _softmax(x, axis=-1):
    return jax.nn.softmax(x, axis=axis)

def _gelu(x):
    return jax.nn.gelu(x, approximate=True)

def _silu(x):
    return jax.nn.silu(x)

def _sigmoid(x):
    return jax.nn.sigmoid(x)

def _layernorm(x, axis=-1, eps=1e-05):
    m = jnp.mean(x, axis=axis, keepdims=True)
    v = jnp.var(x, axis=axis, keepdims=True)
    return (x - m) / jnp.sqrt(v + eps)

def _scatter_add(tgt, idx, src, axis=0):
    return tgt.at[idx].add(src)

def _segment_sum(src, seg, n):
    return jax.ops.segment_sum(src, seg, n)
kernel_name = 'mk_gnn_resnorm_d4_gnn_r32_a871b1'

def setup_inputs(seed: int=0):
    np.random.seed(seed)
    _w = jnp.asarray

    def _rec_inputs():
        import jax
        import jax.numpy as jnp
        _gk = jax.random.key(seed)
        x = -0.0001006 + 1 * jax.random.normal(jax.random.fold_in(_gk, 1), (50000, 96), jnp.float32)
        src = jax.random.randint(jax.random.fold_in(_gk, 2), (50000,), 0, 50000, jnp.int32)
        dst = jax.random.randint(jax.random.fold_in(_gk, 3), (50000,), 0, 50000, jnp.int32)
        _o = jnp.argsort(dst, stable=True)
        src = src[_o]
        dst = dst[_o]
        edge_attr_32 = 0.000196303 + 1.00016 * jax.random.normal(jax.random.fold_in(_gk, 12), (50000, 32), jnp.float32)
        edge_attr_4 = 0.000714719 + 1.00021 * jax.random.normal(jax.random.fold_in(_gk, 13), (50000, 4), jnp.float32)
        return (x, src, dst, edge_attr_32, edge_attr_4)
    x, src, dst, edge_attr_32, edge_attr_4 = _rec_inputs()

    def _L0_gnn_setup():
        import jax, jax.numpy as jnp
        import numpy as np
        N_NODES = 50000
        N_EDGES = 25000
        D = 96
        DEPTH = 2
        key = jax.random.key(seed)
        ks = jax.random.split(key, 8)
        scale = 1.0 / np.sqrt(D)
        x = jax.random.normal(ks[0], (N_NODES, D), dtype=jnp.float32)
        W0 = jax.random.normal(ks[1], (DEPTH, D, D), dtype=jnp.float32) * scale
        b0 = jnp.zeros((DEPTH, D), dtype=jnp.float32)
        W1 = jax.random.normal(ks[2], (DEPTH, D, D), dtype=jnp.float32) * scale
        b1 = jnp.zeros((DEPTH, D), dtype=jnp.float32)
        W2 = jax.random.normal(ks[3], (DEPTH, 2 * D, D), dtype=jnp.float32) * (1.0 / np.sqrt(2 * D))
        b2 = jnp.zeros((DEPTH, D), dtype=jnp.float32)
        edge_src = jax.random.randint(ks[4], (N_EDGES,), 0, N_NODES, dtype=jnp.int64 if jax.config.jax_enable_x64 else jnp.int32)
        edge_dst = jnp.sort(jax.random.randint(ks[5], (N_EDGES,), 0, N_NODES, dtype=jnp.int64 if jax.config.jax_enable_x64 else jnp.int32))
        return {'x': x, 'W0': W0, 'b0': b0, 'W1': W1, 'b1': b1, 'W2': W2, 'b2': b2, 'edge_src': edge_src, 'edge_dst': edge_dst}
    _L0_gnn_all = _L0_gnn_setup()
    _L0_gnn_in = {k: v for k, v in _L0_gnn_all.items() if k in ('W0', 'b0', 'W1', 'b1', 'W2', 'b2')}
    del _L0_gnn_all

    def _L1_gnn_setup():
        import jax, jax.numpy as jnp
        import numpy as np
        N_NODES = 50000
        N_EDGES = 25000
        D_MODEL = 96
        HEADS = 4
        key = jax.random.key(seed)
        ks = jax.random.split(key, 6)
        scale = 1.0 / np.sqrt(D_MODEL)
        return {'embeds': jax.random.normal(ks[0], (N_NODES, D_MODEL), dtype=jnp.float32), 'qW': jax.random.normal(ks[1], (D_MODEL, D_MODEL), dtype=jnp.float32) * scale, 'kW': jax.random.normal(ks[2], (D_MODEL, D_MODEL), dtype=jnp.float32) * scale, 'vW': jax.random.normal(ks[3], (D_MODEL, D_MODEL), dtype=jnp.float32) * scale, 'rows': jax.random.randint(ks[4], (N_EDGES,), 0, N_NODES, dtype=jnp.int32), 'cols': jax.random.randint(ks[5], (N_EDGES,), 0, N_NODES, dtype=jnp.int32)}
    _L1_gnn_all = _L1_gnn_setup()
    _L1_gnn_in = {k: v for k, v in _L1_gnn_all.items() if k in ('qW', 'kW', 'vW')}
    del _L1_gnn_all

    def _L2_gnn_setup():
        import jax, jax.numpy as jnp
        import numpy as np
        EPS = 1e-05

        def _mlp(h, W, b, gamma, beta):
            h = jax.nn.relu(h @ W + b)
            mu = jnp.mean(h, axis=0)
            var = jnp.mean(jnp.square(h - mu), axis=0)
            return gamma * (h - mu) * jax.lax.rsqrt(var + EPS) + beta
        key = jax.random.key(seed)
        ks = jax.random.split(key, 10)
        N, E, C_in, C_out, E_dim = (50000, 25000, 96, 96, 4)
        x = jax.random.normal(ks[0], (N, C_in), dtype=jnp.float32)
        edge_index = jax.random.randint(ks[1], (2, E), 0, N, dtype=jnp.int64)
        edge_attr = jax.random.normal(ks[2], (E, E_dim), dtype=jnp.float32)
        s = lambda fan_in: 1.0 / np.sqrt(fan_in)
        W_node = jax.random.uniform(ks[3], (C_in, C_out), jnp.float32, -s(C_in), s(C_in))
        b_node = jnp.zeros((C_out,), jnp.float32)
        g_node = jnp.ones((C_out,), jnp.float32)
        beta_node = jnp.zeros((C_out,), jnp.float32)
        W_edge = jax.random.uniform(ks[4], (E_dim, C_out), jnp.float32, -s(E_dim), s(E_dim))
        b_edge = jnp.zeros((C_out,), jnp.float32)
        g_edge = jnp.ones((C_out,), jnp.float32)
        beta_edge = jnp.zeros((C_out,), jnp.float32)
        M_in = 2 * C_in + C_out
        W_msg = jax.random.uniform(ks[5], (M_in, C_out), jnp.float32, -s(M_in), s(M_in))
        b_msg = jnp.zeros((C_out,), jnp.float32)
        g_msg = jnp.ones((C_out,), jnp.float32)
        beta_msg = jnp.zeros((C_out,), jnp.float32)
        return dict(x=x, edge_index=edge_index, edge_attr=edge_attr, W_node=W_node, b_node=b_node, g_node=g_node, beta_node=beta_node, W_edge=W_edge, b_edge=b_edge, g_edge=g_edge, beta_edge=beta_edge, W_msg=W_msg, b_msg=b_msg, g_msg=g_msg, beta_msg=beta_msg)
    _L2_gnn_all = _L2_gnn_setup()
    _L2_gnn_in = {k: v for k, v in _L2_gnn_all.items() if k in ('W_node', 'b_node', 'g_node', 'beta_node', 'W_edge', 'b_edge', 'g_edge', 'beta_edge', 'W_msg', 'b_msg', 'g_msg', 'beta_msg')}
    del _L2_gnn_all

    def _L3_gnn_setup():
        import jax, jax.numpy as jnp
        import numpy as np
        N_NODES = 50000
        N_EDGES = 25000
        IN_DIM = 96
        OUT_DIM = 96
        EDGE_DIM = 32
        BN_EPS = 1e-05
        key = jax.random.key(seed)
        ks = jax.random.split(key, 12)
        x = jax.random.normal(ks[0], (N_NODES, IN_DIM), dtype=jnp.float32)
        edge_index = jax.random.randint(ks[1], (2, N_EDGES), 0, N_NODES, dtype=jnp.int64)
        edge_attr = jax.random.normal(ks[2], (N_EDGES, EDGE_DIM), dtype=jnp.float32)
        We = jax.random.normal(ks[3], (EDGE_DIM, IN_DIM), dtype=jnp.float32) / np.sqrt(EDGE_DIM)
        be = jnp.zeros((IN_DIM,), dtype=jnp.float32)
        W1 = jax.random.normal(ks[4], (IN_DIM, OUT_DIM), dtype=jnp.float32) / np.sqrt(IN_DIM)
        b1 = jnp.zeros((OUT_DIM,), dtype=jnp.float32)
        W2 = jax.random.normal(ks[5], (OUT_DIM, OUT_DIM), dtype=jnp.float32) / np.sqrt(OUT_DIM)
        b2 = jnp.zeros((OUT_DIM,), dtype=jnp.float32)
        gamma = jnp.ones((OUT_DIM,), dtype=jnp.float32)
        beta = jnp.zeros((OUT_DIM,), dtype=jnp.float32)
        return {'x': x, 'edge_index': edge_index, 'edge_attr': edge_attr, 'We': We, 'be': be, 'W1': W1, 'b1': b1, 'W2': W2, 'b2': b2, 'gamma': gamma, 'beta': beta}
    _L3_gnn_all = _L3_gnn_setup()
    _L3_gnn_in = {k: v for k, v in _L3_gnn_all.items() if k in ('We', 'be', 'W1', 'b1', 'W2', 'b2', 'gamma', 'beta')}
    del _L3_gnn_all
    return {'x': x, 'src': src, 'dst': dst, 'edge_attr_32': edge_attr_32, 'edge_attr_4': edge_attr_4, 'L0_gnn_W0': _L0_gnn_in['W0'], 'L0_gnn_b0': _L0_gnn_in['b0'], 'L0_gnn_W1': _L0_gnn_in['W1'], 'L0_gnn_b1': _L0_gnn_in['b1'], 'L0_gnn_W2': _L0_gnn_in['W2'], 'L0_gnn_b2': _L0_gnn_in['b2'], 'L1_gnn_qW': _L1_gnn_in['qW'], 'L1_gnn_kW': _L1_gnn_in['kW'], 'L1_gnn_vW': _L1_gnn_in['vW'], 'L2_gnn_W_node': _L2_gnn_in['W_node'], 'L2_gnn_b_node': _L2_gnn_in['b_node'], 'L2_gnn_g_node': _L2_gnn_in['g_node'], 'L2_gnn_beta_node': _L2_gnn_in['beta_node'], 'L2_gnn_W_edge': _L2_gnn_in['W_edge'], 'L2_gnn_b_edge': _L2_gnn_in['b_edge'], 'L2_gnn_g_edge': _L2_gnn_in['g_edge'], 'L2_gnn_beta_edge': _L2_gnn_in['beta_edge'], 'L2_gnn_W_msg': _L2_gnn_in['W_msg'], 'L2_gnn_b_msg': _L2_gnn_in['b_msg'], 'L2_gnn_g_msg': _L2_gnn_in['g_msg'], 'L2_gnn_beta_msg': _L2_gnn_in['beta_msg'], 'L3_gnn_We': _L3_gnn_in['We'], 'L3_gnn_be': _L3_gnn_in['be'], 'L3_gnn_W1': _L3_gnn_in['W1'], 'L3_gnn_b1': _L3_gnn_in['b1'], 'L3_gnn_W2': _L3_gnn_in['W2'], 'L3_gnn_b2': _L3_gnn_in['b2'], 'L3_gnn_gamma': _L3_gnn_in['gamma'], 'L3_gnn_beta': _L3_gnn_in['beta']}

def reference(x, src, dst, edge_attr_32, edge_attr_4, L0_gnn_W0, L0_gnn_b0, L0_gnn_W1, L0_gnn_b1, L0_gnn_W2, L0_gnn_b2, L1_gnn_qW, L1_gnn_kW, L1_gnn_vW, L2_gnn_W_node, L2_gnn_b_node, L2_gnn_g_node, L2_gnn_beta_node, L2_gnn_W_edge, L2_gnn_b_edge, L2_gnn_g_edge, L2_gnn_beta_edge, L2_gnn_W_msg, L2_gnn_b_msg, L2_gnn_g_msg, L2_gnn_beta_msg, L3_gnn_We, L3_gnn_be, L3_gnn_W1, L3_gnn_b1, L3_gnn_W2, L3_gnn_b2, L3_gnn_gamma, L3_gnn_beta):
    import jax
    import jax.numpy as jnp

    def _L0_gnn_ref(x, W0, b0, W1, b1, W2, b2, edge_src, edge_dst):
        import jax, jax.numpy as jnp
        import numpy as np
        N_NODES = 50000
        N_EDGES = 25000
        D = 96
        DEPTH = 2
        n = x.shape[0]
        depth = W0.shape[0]
        for i in range(depth):
            h_self = x @ W1[i] + b1[i]
            h_nb = x @ W0[i] + b0[i]
            agg = jax.ops.segment_sum(h_nb[edge_src], edge_dst, num_segments=n)
            x = jnp.concatenate([h_self, agg], axis=-1) @ W2[i] + b2[i]
            x = x / jnp.std(x, axis=-1, ddof=1, keepdims=True)
        return x

    def _L1_gnn_ref(embeds, qW, kW, vW, rows, cols):
        import jax, jax.numpy as jnp
        import numpy as np
        N_NODES = 50000
        N_EDGES = 25000
        D_MODEL = 96
        HEADS = 4
        nvar, d = embeds.shape
        dh = d // HEADS
        e = rows.shape[0]
        q = (embeds[rows] @ qW).reshape(e, HEADS, dh)
        k = (embeds[cols] @ kW).reshape(e, HEADS, dh)
        v = (embeds[cols] @ vW).reshape(e, HEADS, dh)
        scores = jnp.clip(jnp.einsum('ehd,ehd->eh', q, k), -10.0, 10.0)
        exp_s = jnp.exp(scores)
        norms = jax.ops.segment_sum(exp_s, rows, num_segments=nvar)[rows]
        w = exp_s / (norms + 1e-08)
        res = jax.ops.segment_sum(w[:, :, None] * v, rows, num_segments=nvar).reshape(nvar, d)
        return embeds + res

    def _L2_gnn_ref(x, edge_index, edge_attr, W_node, b_node, g_node, beta_node, W_edge, b_edge, g_edge, beta_edge, W_msg, b_msg, g_msg, beta_msg):
        import jax, jax.numpy as jnp
        import numpy as np
        EPS = 1e-05

        def _mlp(h, W, b, gamma, beta):
            h = jax.nn.relu(h @ W + b)
            mu = jnp.mean(h, axis=0)
            var = jnp.mean(jnp.square(h - mu), axis=0)
            return gamma * (h - mu) * jax.lax.rsqrt(var + EPS) + beta
        node_feat = _mlp(x, W_node, b_node, g_node, beta_node)
        edge_feat = _mlp(edge_attr, W_edge, b_edge, g_edge, beta_edge)
        row, col = (edge_index[0], edge_index[1])
        message = jnp.concatenate([x[row], x[col], edge_feat], axis=1)
        message = _mlp(message, W_msg, b_msg, g_msg, beta_msg)
        agg = jax.ops.segment_sum(message, col, num_segments=node_feat.shape[0])
        return agg + node_feat

    def _L3_gnn_ref(x, edge_index, edge_attr, We, be, W1, b1, W2, b2, gamma, beta):
        import jax, jax.numpy as jnp
        import numpy as np
        N_NODES = 50000
        N_EDGES = 25000
        IN_DIM = 96
        OUT_DIM = 96
        EDGE_DIM = 32
        BN_EPS = 1e-05
        src = edge_index[0]
        dst = edge_index[1]
        msg = jax.nn.relu(x[src] + edge_attr @ We + be)
        aggr = jax.ops.segment_sum(msg, dst, num_segments=x.shape[0])
        h = x + aggr
        h = jax.nn.relu(h @ W1 + b1) @ W2 + b2
        mean = jnp.mean(h, axis=0)
        var = jnp.mean(jnp.square(h - mean), axis=0)
        h = (h - mean) * jax.lax.rsqrt(var + BN_EPS) * gamma + beta
        return jax.nn.relu(h)
    edge_index = jnp.stack([src, dst])
    x = _layernorm(x + _L0_gnn_ref(x, L0_gnn_W0, L0_gnn_b0, L0_gnn_W1, L0_gnn_b1, L0_gnn_W2, L0_gnn_b2, src, dst), axis=-1)
    x = _layernorm(x + _L1_gnn_ref(x, L1_gnn_qW, L1_gnn_kW, L1_gnn_vW, src, dst), axis=-1)
    x = _layernorm(x + _L2_gnn_ref(x, edge_index, edge_attr_4, L2_gnn_W_node, L2_gnn_b_node, L2_gnn_g_node, L2_gnn_beta_node, L2_gnn_W_edge, L2_gnn_b_edge, L2_gnn_g_edge, L2_gnn_beta_edge, L2_gnn_W_msg, L2_gnn_b_msg, L2_gnn_g_msg, L2_gnn_beta_msg), axis=-1)
    x = _layernorm(x + _L3_gnn_ref(x, edge_index, edge_attr_32, L3_gnn_We, L3_gnn_be, L3_gnn_W1, L3_gnn_b1, L3_gnn_W2, L3_gnn_b2, L3_gnn_gamma, L3_gnn_beta), axis=-1)
    return x

_drawn_inputs = setup_inputs


def setup_inputs(seed=0):
    import zlib

    import numpy as np

    out = dict(_drawn_inputs(seed))
    spreads = {'L0_gnn_b0': (0.0, 0.1),
     'L0_gnn_b1': (0.0, 0.1),
     'L0_gnn_b2': (0.0, 0.1),
     'L2_gnn_b_node': (0.0, 0.1),
     'L2_gnn_g_node': (1.0, 0.2),
     'L2_gnn_beta_node': (0.0, 0.1),
     'L2_gnn_b_edge': (0.0, 0.1),
     'L2_gnn_g_edge': (1.0, 0.2),
     'L2_gnn_beta_edge': (0.0, 0.418),
     'L2_gnn_b_msg': (0.0, 0.1),
     'L2_gnn_g_msg': (1.0, 0.2),
     'L2_gnn_beta_msg': (0.0, 0.1),
     'L3_gnn_be': (0.0, 0.1),
     'L3_gnn_b1': (0.0, 0.1),
     'L3_gnn_b2': (0.0, 0.8),
     'L3_gnn_gamma': (1.0, 0.2),
     'L3_gnn_beta': (0.0, 0.1)}
    factors = {}
    for name, (base, spread) in spreads.items():
        noise = np.random.default_rng([zlib.crc32(name.encode()), seed]).standard_normal(out[name].shape)
        drawn = base * np.exp(spread * noise) if base else spread * noise
        out[name] = jnp.asarray(drawn.astype(out[name].dtype))
    for name, factor in factors.items():
        out[name] = (out[name] * factor).astype(out[name].dtype)
    return out
```

```python
import concourse.bass as bass
from concourse import mybir
from contextlib import ExitStack

F32 = mybir.dt.float32
I32 = mybir.dt.int32
ALU = mybir.AluOpType
ACT = mybir.ActivationFunctionType
AX = mybir.AxisListType

N = 50000
D = 96
W = D + 1
HEADS = 4
DH = D // HEADS
M = D + HEADS
P = 128
TILES = N // P
TAIL = N - TILES * P
GT = 3
GR = 10
LAPS = TILES // (GT * GR)
GROUPS = LAPS * GR
RING = 5
PAIRS = GROUPS // 2
STEP = 8
SLOTS = TILES + 2
DUMP = N
EPS = 1e-5
FULL = (GT, P)
LAST = (1, TAIL)


class Phase(ExitStack):

    count = 0

    def __init__(self, nc):
        super().__init__()
        self.nc = nc
        Phase.count += 1
        self.tag = f"p{Phase.count}_"
        self.sems = []

    def sbuf(self, name, shape, dt):
        return self.enter_context(self.nc.sbuf_tensor(self.tag + name, shape, dt))

    def psum(self, name, shape, dt):
        return self.enter_context(self.nc.psum_tensor(self.tag + name, shape, dt))

    def semaphore(self, name):
        self.sems.append(self.nc.alloc_semaphore(self.tag + name))
        return self.sems[-1]

    def __exit__(self, *error):
        super().__exit__(*error)
        if error[0] is None:
            self.nc.clear_and_free_semaphores(self.sems)
            self.nc.all_engine_barrier(sem_only=True)


START = 16


class Count:

    def __init__(self, ctx, nc, name, unit=1):
        self.sem = ctx.semaphore(name)
        self.unit = unit
        nc.sync.sem_inc(self.sem, START * unit)

    def done(self, g):
        return (g + (START + 1)) * self.unit

    def free(self, g, ring):
        return (g + (START + 1 - ring)) * self.unit


class DmaRing:

    def __init__(self, ctx, nc, name, dmas=1, pool=False):
        self.sems = [ctx.semaphore(f"{name}{s}") for s in range(RING)]
        self.inc = 16 * dmas
        self.first = 1 if pool else 2
        if not pool:
            for s in self.sems:
                nc.sync.sem_inc(s, self.inc)

    def sem(self, k):
        return self.sems[k % RING]

    def done(self, i, k):
        return (i * (GR // RING) + (k // RING + self.first)) * self.inc

    def free(self, i, k):
        return (i * (GR // RING) + (k // RING + 1)) * self.inc


def wait_apart(eng, steady, *waits):
    held = [v if isinstance(v, int) else eng.snap(eng.to_reg(v)) for _, v in waits]
    eng.wait_ge(steady, 1)
    for (sem, _), value in zip(waits, held):
        eng.wait_ge(sem, value)


def laps(eng, stages):
    most = max(lead for lead, _ in stages)

    def beside(g):
        for lead, step in stages:
            if 0 <= g + lead <= GROUPS:
                step((g + lead) // GR, (g + lead) % GR, *(LAST if g + lead == GROUPS else FULL))

    for g in range(-most, 0):
        beside(g)
    with eng.Fori(0, LAPS - 1) as i:
        for k in range(GR):
            for lead, step in stages:
                step(i + (k + lead) // GR, (k + lead) % GR, *FULL)
    for g in range(GROUPS - GR, GROUPS + 1):
        beside(g)


def group_rows(dram, g, T, rows):
    if rows == TAIL:
        return dram[TILES * P:N, :].rearrange("(t p) f -> p t f", t=1)
    return dram[bass.ds(g * (GT * P), GT * P), :].rearrange("(t p) f -> p t f", p=P)


def group_cols(dram, g, rows):
    if rows == TAIL:
        return dram[:, TILES * P:N]
    return dram[:, bass.ds(g * (GT * P), GT * P)]


class Chip:
    pass


def gnn(nc, given, out):
    with ExitStack() as ctx:
        def sb(name, shape, dt=F32):
            return ctx.enter_context(nc.sbuf_tensor(name, shape, dt))

        def dram(name, shape, dt=F32):
            return nc.dram_tensor(name, shape, dt, kind="Internal").ap()

        c = Chip()
        c.iota256 = sb("iota256", [P, 2 * P])
        c.tile_base = sb("tile_base", [P, SLOTS])
        c.ident = sb("ident", [P, P])
        c.ones = sb("ones", [P, P])
        c.zeros = sb("zeros", [P, GT, W])
        c.dst_f = sb("dst_f", [P, TILES + 1])
        c.steps = sb("steps", [1, (GROUPS + 2) * STEP], I32)
        c.w_src = sb("w_src", [W, D])
        c.w_dst = sb("w_dst", [D, D])
        c.w_feat = sb("w_feat", [D, D])
        c.w_edge4 = sb("w_edge4", [5, D])
        c.w_node = sb("w_node", [D, D])
        c.w_edge32 = sb("w_edge32", [33, D])
        c.w1 = sb("w1", [D, D])
        c.w2 = sb("w2", [W, D])
        c.cols = sb("cols", [D, 10])
        c.stat = sb("stat", [D, GROUPS + 1, 6])
        c.stat_msg = sb("stat_msg", [D, GROUPS + 1, 6])
        c.hop_tab = dram("steps_dram", [(PAIRS + 1), 2 * STEP], I32)
        c.att = dram("att", [P * SLOTS, M])
        x1, x2, x3, x4 = (dram(f"x{l}", [N, D]) for l in range(1, 5))
        x0 = given["x"]
        c.src, c.src_cols, c.dst, c.dst_cols = (given[k] for k in ("src", "src_cols", "dst", "dst_cols"))

        with ExitStack() as early:
            def sb_early(name, shape, dt=F32):
                return early.enter_context(nc.sbuf_tensor(name, shape, dt))

            c.lower = sb_early("lower", [P, P])
            c.src_f = sb_early("src_f", [P, TILES + 1])
            c.to_dump = sb_early("to_dump", [P, TILES + 1])
            c.mix_self = [sb_early(f"mix_self{l}", [W, D]) for l in range(2)]
            c.mix_near = [sb_early(f"mix_near{l}", [W, D]) for l in range(2)]
            c.qkv = sb_early("qkv", [D, 3 * D])
            with nc.sbuf_tensor("node_tab", [P, SLOTS, W], F32) as c.node_tab:
                load_and_index(nc, c, given)
                edge_norm(nc, c, given)
                gather_sum(nc, c, x0)
                mix_nodes(nc, c, x0, x1, 0, None)
                gather_sum(nc, c, x1)
                mix_nodes(nc, c, x1, x2, 1, x0)
            attention_edges(nc, c, x2)
            attention_nodes(nc, c, x2, x3)
        with nc.sbuf_tensor("node_tab2", [P, SLOTS, W], F32) as c.node_tab:
            clear_table(nc, c)
            message_edges(nc, c, x3, given["edge4_t"])
            message_nodes(nc, c, x3, x4)
            gather_sum(nc, c, x4, given["edge32_t"])
            mlp_nodes(nc, c, x4)
            out_nodes(nc, c, x4, out)


COLS = ["b_node", "g_node", "beta_node", "g_edge", "beta_edge", "g_msg", "beta_msg", "b1", "gamma", "beta"]


def column(c, name):
    k = COLS.index(name)
    return c.cols[:, k:k + 1]


def load_and_index(nc, c, given):
    with Phase(nc) as ctx:
        def sb(name, shape, dt=F32):
            return ctx.sbuf(name, shape, dt)

        def sem(name):
            return ctx.semaphore(name)

        src_i = sb("src_i", [P, TILES + 1], I32)
        dst_i = sb("dst_i", [P, TILES + 1], I32)
        hops = sb("hops", [PAIRS + 1, 2 * GT * P], I32)
        hops_f = sb("hops_f", [PAIRS + 1, 2 * GT, P])
        low = sb("low", [PAIRS + 1, 2 * GT])
        more = sb("more", [PAIRS + 1, 2 * GT])
        anymore = sb("anymore", [PAIRS + 1, 2])
        step_rows = sb("step_rows", [PAIRS + 1, 2, STEP], I32)
        self_t = [sb(f"self_t{l}", [W, W]) for l in range(2)]
        near_t = [sb(f"near_t{l}", [D, W]) for l in range(2)]
        w2_self = [sb(f"w2_self{l}", [W, D]) for l in range(2)]
        w2_near = [sb(f"w2_near{l}", [D, D]) for l in range(2)]
        mix = ctx.psum("mix", [P, 4, 512], F32)
        filled = sem("filled")
        masks = sem("masks")
        idx_loaded = sem("idx_loaded")
        w_loaded = sem("w_loaded")
        step = sem("step")
        table_zero = sem("table_zero")
        att_zero = sem("att_zero")
        steps_out = sem("steps_out")
        steps_in = sem("steps_in")
        mixed = sem("mixed")
        block = ctx.enter_context(nc.Block())
        weights = ([(self_t[l][:], given[f"self_t{l}"]) for l in range(2)]
                   + [(near_t[l][:], given[f"near_t{l}"]) for l in range(2)]
                   + [(w2_self[l][:], given[f"w2_self{l}"]) for l in range(2)]
                   + [(w2_near[l][:], given[f"w2_near{l}"]) for l in range(2)]
                   + [(c.w_src[:], given["w_src"]), (c.w_dst[:], given["w_dst"]), (c.w_feat[:], given["w_feat"]),
                      (c.w_edge4[:], given["w_edge4"]), (c.qkv[:], given["qkv"]), (c.w_node[:], given["w_node"]),
                      (c.w_edge32[:], given["w_edge32"]), (c.w1[:], given["w1"]), (c.w2[:], given["w2"]),
                      (c.cols[:], given["cols"])])
        tail = slice(TILES * P, N)
        src, dst = given["src"], given["dst"]

        @block.sync
        def _(sp):
            sp.wait_ge(filled, 4)
            loads = [(hops[0:PAIRS, :], dst[0:TILES * P].rearrange("(i f) -> i f", i=PAIRS)),
                     (hops[PAIRS:PAIRS + 1, 0:P], dst[N - P:N].rearrange("(o f) -> o f", o=1)),
                     (dst_i[:, 0:TILES], given["dst_cols"]),
                     (dst_i[0:TAIL, TILES:TILES + 1], dst[tail].rearrange("(p o) -> p o", o=1)),
                     (src_i[:, 0:TILES], given["src_cols"]),
                     (src_i[0:TAIL, TILES:TILES + 1], src[tail].rearrange("(p o) -> p o", o=1))]
            for to, frm in loads:
                sp.dma_start(to, frm).then_inc(idx_loaded, 16)
            for to, frm in weights:
                sp.dma_start(to, frm).then_inc(w_loaded, 16)
            sp.wait_ge(table_zero, 1)
            att = c.att.rearrange("(p a) f -> p (a f)", p=P)
            half = SLOTS * M // 2
            for h in range(2):
                sp.dma_start(att[:, h * half:(h + 1) * half],
                             c.node_tab[:].rearrange("p a f -> p (a f)")[:, 0:half]).then_inc(att_zero, 16)
            sp.wait_ge(step, 12)
            sp.dma_start(c.hop_tab, step_rows[:].rearrange("p a b -> p (a b)")).then_inc(steps_out, 16)
            sp.wait_ge(steps_out, 16)
            sp.dma_start(c.steps[:], c.hop_tab.rearrange("(o i) k -> o (i k)", o=1)).then_inc(steps_in, 16)
            sp.wait_ge(steps_in, 16)
            sp.wait_ge(att_zero, 32)

        @block.gpsimd
        def _(pool):
            nc.gpsimd.iota(c.iota256[:], pattern=[[1, 2 * P]], base=0, channel_multiplier=0,
                           allow_small_or_imprecise_dtypes=True)
            nc.gpsimd.iota(c.tile_base[:], pattern=[[P, SLOTS]], base=0, channel_multiplier=0,
                           allow_small_or_imprecise_dtypes=True)
            nc.gpsimd.iota(c.to_dump[:], pattern=[[0, TILES + 1]], base=DUMP, channel_multiplier=1,
                           allow_small_or_imprecise_dtypes=True).then_inc(masks, 1)
            nc.gpsimd.memset(c.ident[:], 0.0).then_inc(masks, 1)
            nc.gpsimd.memset(c.lower[:], 1.0).then_inc(masks, 1)
            pool.wait_ge(masks, 3)
            nc.gpsimd.affine_select(out=c.ident[:], in_=c.ident[:], compare_op=ALU.not_equal, fill=1.0,
                                    base=0, pattern=[[-1, P]], channel_multiplier=1)
            nc.gpsimd.affine_select(out=c.lower[:], in_=c.lower[:], compare_op=ALU.is_gt, fill=0.0,
                                    base=0, pattern=[[-1, P]], channel_multiplier=1)

        @block.tensor
        def _(pe):
            pe.wait_ge(w_loaded, 16 * len(weights))
            for l in range(2):
                nc.tensor.matmul(mix[0:W, 2 * l, 0:D], self_t[l][:], w2_self[l][:], start=True, stop=True)\
                    .then_inc(mixed, 1)
                nc.tensor.matmul(mix[0:W, 2 * l + 1, 0:D], near_t[l][:], w2_near[l][:], start=True, stop=True)\
                    .then_inc(mixed, 1)

        @block.scalar
        def _(act):
            for l in range(2):
                act.wait_ge(mixed, 2 * l + 2)
                nc.scalar.copy(c.mix_self[l][:], mix[0:W, 2 * l, 0:D])
                nc.scalar.copy(c.mix_near[l][:], mix[0:W, 2 * l + 1, 0:D])

        @block.vector
        def _(dve):
            nc.vector.memset(hops[:], 0).then_inc(filled, 1)
            nc.vector.memset(step_rows[:], 0).then_inc(filled, 1)
            nc.vector.memset(dst_i[:, TILES:TILES + 1], 0).then_inc(filled, 1)
            nc.vector.memset(src_i[:, TILES:TILES + 1], 0).then_inc(filled, 1)
            nc.vector.memset(c.zeros[:], 0.0)
            nc.vector.memset(c.ones[:], 1.0)
            nc.vector.memset(c.node_tab[:], 0.0).then_inc(table_zero, 1)
            dve.wait_ge(filled, 4)
            dve.wait_ge(idx_loaded, 16 * 6)
            count = 0

            def then(ins):
                nonlocal count
                count += 1
                ins.then_inc(step, 1)
                dve.wait_ge(step, count)

            then(nc.vector.tensor_copy(c.dst_f[:], dst_i[:]))
            then(nc.vector.tensor_copy(c.src_f[:], src_i[:]))
            dve.wait_ge(masks, 3)
            then(nc.vector.tensor_tensor(c.to_dump[:], c.to_dump[:], c.src_f[:], ALU.subtract))
            then(nc.vector.tensor_scalar(hops[:], hops[:], 7, None, ALU.arith_shift_right))
            then(nc.vector.tensor_copy(hops_f[:].rearrange("p a b -> p (a b)"), hops[:]))
            then(nc.vector.tensor_reduce(low[:], hops_f[:], AX.X, ALU.min))
            then(nc.vector.tensor_reduce(more[:], hops_f[:], AX.X, ALU.max))
            then(nc.vector.tensor_tensor(more[:], more[:], low[:], ALU.subtract))
            then(nc.vector.tensor_scalar(more[:], more[:], -1.0, 0.0, ALU.add, ALU.max))
            then(nc.vector.tensor_reduce(anymore[:], more[:].rearrange("p (a b) -> p a b", a=2), AX.X, ALU.max))
            nc.vector.tensor_copy(step_rows[:, :, 0:GT], low[:].rearrange("p (a b) -> p a b", a=2))
            nc.vector.tensor_copy(step_rows[:, :, 4:4 + GT], more[:].rearrange("p (a b) -> p a b", a=2))\
                .then_inc(step, 1)
            nc.vector.tensor_copy(step_rows[:, :, 3:4], anymore[:].rearrange("p (a b) -> p a b", b=1))\
                .then_inc(step, 1)


class Norm:

    def __init__(self, ctx, nc, name):
        self.nc = nc
        self.mv = ctx.sbuf(f"{name}_mv", [D, 2], F32)
        self.inv = ctx.sbuf(f"{name}_inv", [D, 1], F32)
        self.root = ctx.sbuf(f"{name}_root", [D, 1], F32)
        self.stepped = ctx.semaphore(f"{name}_stepped")
        self.rooted = ctx.semaphore(f"{name}_rooted")

    def on_vector(self, dve, stat, gamma, beta, terms):
        nc, mv, inv = self.nc, self.mv, self.inv
        nc.vector.bn_aggr(mv[:], stat[:].rearrange("p a b -> p (a b)")).then_inc(self.stepped, 1)
        dve.wait_ge(self.stepped, 1)
        nc.vector.tensor_scalar(inv[:], mv[:, 1:2], EPS, None, ALU.add).then_inc(self.stepped, 1)
        dve.wait_ge(self.stepped, 2)
        nc.vector.reciprocal(inv[:], inv[:]).then_inc(self.stepped, 1)
        dve.wait_ge(self.rooted, 1)
        nc.vector.tensor_tensor(terms[:, 0:1], self.root[:], gamma, ALU.mult).then_inc(self.stepped, 1)
        dve.wait_ge(self.stepped, 4)
        nc.vector.tensor_tensor(terms[:, 1:2], mv[:, 0:1], terms[:, 0:1], ALU.mult).then_inc(self.stepped, 1)
        dve.wait_ge(self.stepped, 5)
        nc.vector.tensor_tensor(terms[:, 1:2], beta, terms[:, 1:2], ALU.subtract).then_inc(self.stepped, 1)
        dve.wait_ge(self.stepped, 6)

    def on_scalar(self, act):
        act.wait_ge(self.stepped, 3)
        self.nc.scalar.activation(self.root[:], self.inv[:], ACT.Sqrt).then_inc(self.rooted, 1)


def flat(ap):
    return ap.rearrange("p a b -> p (a b)")


def record(stat, g):
    return flat(stat[:, bass.ds(g, 1), :])


def edge_norm(nc, c, given):
    with Phase(nc) as ctx:
        def sb(name, shape, dt=F32):
            return ctx.sbuf(name, shape, dt)

        def sem(name):
            return ctx.semaphore(name)

        feats = sb("feats", [5, RING, GT * P])
        h = sb("h", [D, 2, GT * P])
        terms = sb("terms", [D, 2])
        shift_l = sb("shift_l", [D, W])
        h_ps = ctx.psum("h_ps", [P, 2, 512], F32)
        fold_ps = ctx.psum("fold_ps", [P, 512], F32)
        norm = Norm(ctx, nc, "edge")
        feats_in = DmaRing(ctx, nc, "feats_in")
        multiplied = Count(ctx, nc, "multiplied")
        rectified = Count(ctx, nc, "rectified")
        counted = Count(ctx, nc, "counted")
        ones_set = sem("ones_set")
        shift_set = sem("shift_set")
        folded = sem("folded")
        block = ctx.enter_context(nc.Block())

        @block.sync
        def _(sp):
            def load(i, k, T, rows):
                g = i * GR + k
                wait_apart(nc.sync, ones_set, (multiplied.sem, multiplied.free(g, RING)))
                sp.dma_start(feats[0:4, k % RING, 0:T * rows], group_cols(given["edge4_t"], g, rows))\
                    .then_inc(feats_in.sem(k), 16)
            sp.wait_ge(ones_set, 1)
            laps(nc.sync, [(0, load)])

        @block.tensor
        def _(pe):
            def multiply(i, k, T, rows):
                g = i * GR + k
                pe.wait_ge(feats_in.sem(k), feats_in.done(i, k))
                pe.wait_ge(rectified.sem, rectified.free(g, 2))
                nc.tensor.matmul(h_ps[0:D, k % 2, 0:T * rows], c.w_edge4[:], feats[:, k % RING, 0:T * rows],
                                 start=True, stop=True).then_inc(multiplied.sem, 1)
            laps(nc.tensor, [(0, multiply)])
            pe.wait_ge(shift_set, 2)
            nc.tensor.matmul(fold_ps[0:W, 0:D], c.ident[0:W, 0:W], c.w_src[:], start=True, stop=False)
            nc.tensor.matmul(fold_ps[0:W, 0:D], shift_l[:], c.w_feat[:], start=False, stop=True).then_inc(folded, 1)

        @block.scalar
        def _(act):
            def rectify(i, k, T, rows):
                g = i * GR + k
                act.wait_ge(multiplied.sem, multiplied.done(g))
                act.wait_ge(counted.sem, counted.free(g, 2))
                nc.scalar.activation(h[:, k % 2, 0:T * rows], h_ps[0:D, k % 2, 0:T * rows], ACT.Relu)\
                    .then_inc(rectified.sem, 1)
            laps(nc.scalar, [(0, rectify)])
            norm.on_scalar(act)

        @block.vector
        def _(dve):
            nc.vector.memset(feats[:], 1.0).then_inc(ones_set, 1)
            nc.vector.memset(shift_l[:], 0.0).then_inc(shift_set, 1)

            def count(i, k, T, rows):
                g = i * GR + k
                dve.wait_ge(rectified.sem, rectified.done(g))
                nc.vector.bn_stats(record(c.stat, g), h[:, k % 2, 0:T * rows]).then_inc(counted.sem, 1)
            laps(nc.vector, [(0, count)])
            dve.wait_ge(counted.sem, counted.done(GROUPS))
            norm.on_vector(dve, c.stat, column(c, "g_edge"), column(c, "beta_edge"), terms)
            dve.wait_ge(shift_set, 1)
            nc.vector.tensor_copy(shift_l[:, D:W], terms[:, 1:2]).then_inc(shift_set, 1)
            dve.wait_ge(folded, 1)
            nc.vector.tensor_copy(c.w_src[:], fold_ps[0:W, 0:D])
            nc.vector.tensor_scalar(c.w_feat[:], c.w_feat[:], terms[:, 0:1], None, ALU.mult)


def clear_table(nc, c):
    with Phase(nc) as ctx:
        block = ctx.enter_context(nc.Block())
        half = SLOTS * 5 // 8

        @block.vector
        def _(dve):
            nc.vector.memset(flat(c.node_tab[:, 0:half, :]), 0.0)

        @block.gpsimd
        def _(pool):
            nc.gpsimd.memset(flat(c.node_tab[:, half:SLOTS, :]), 0.0)


class NodeSum:

    def __init__(self, ctx, nc, c):
        self.nc, self.c, self.tag = nc, c, ctx.tag
        self.hot = ctx.sbuf("hot", [P, GT, 2 * P], F32)
        self.far_hot = ctx.sbuf("far_hot", [P, P], F32)
        self.acc = ctx.psum("acc", [P, 2, 512], F32)
        self.far_acc = ctx.psum("far_acc", [P, 512], F32)
        self.hot_made = Count(ctx, nc, "hot_made")
        self.summed = Count(ctx, nc, "summed")
        self.added = Count(ctx, nc, "added")
        self.far_matched = ctx.semaphore("far_matched")
        self.far_summed = ctx.semaphore("far_summed")
        self.far_added = ctx.semaphore("far_added")

    def on_tensor(self, pe, rows_of, wait_rows):
        nc, c = self.nc, self.c
        far = nc.tensor.alloc_register(self.tag + "far_steps_pe")
        any_far = nc.tensor.alloc_register(self.tag + "any_far_pe")
        more = [nc.tensor.alloc_register(self.tag + f"more_pe{j}") for j in range(4)]
        nc.tensor.reg_mov(far, 0)

        def step(i, k, T, rows):
            g = i * GR + k
            nc.tensor.reg_load(any_far, c.steps[0:1, bass.ds(g * STEP + 3, 1)])
            some = nc.tensor.snap(any_far, min_val=0, max_val=TILES)
            wait_rows(i, k)
            with nc.tensor.If(some > 0):
                nc.tensor.reg_load(more, c.steps[0:1, bass.ds(g * STEP + 4, 4)])
                for j in range(T):
                    count = nc.tensor.snap(more[j], min_val=0, max_val=TILES)
                    with nc.tensor.If(count > 0):
                        with nc.tensor.Fori(0, count):
                            nc.tensor.reg_add(far, far, 1)
                            now = nc.tensor.snap(far)
                            pe.wait_ge(self.far_matched, now)
                            nc.tensor.matmul(self.far_acc[:, 0:W], self.far_hot[0:rows, :], rows_of(k, j, rows),
                                             start=True, stop=True).then_inc(self.far_summed, 1)
                            pe.wait_ge(self.far_added, now)
            for j in range(T):
                t = g * GT + j
                pe.wait_ge(self.hot_made.sem, self.hot_made.done(t))
                pe.wait_ge(self.added.sem, self.added.free(t, 2))
                for h in range(2):
                    last = nc.tensor.matmul(self.acc[:, (GT * k + j) % 2, h * W:(h + 1) * W],
                                            self.hot[0:rows, j, h * P:(h + 1) * P], rows_of(k, j, rows),
                                            start=True, stop=True)
                last.then_inc(self.summed.sem, 1)
        return step

    def on_vector(self, dve):
        nc, c = self.nc, self.c
        far = nc.vector.alloc_register(self.tag + "far_steps_dve")
        near = [[nc.vector.alloc_register(self.tag + f"near_dve{s}_{j}") for j in range(4)] for s in range(2)]
        more = [nc.vector.alloc_register(self.tag + f"more_dve{j}") for j in range(4)]
        nc.vector.reg_mov(far, 0)
        first = {}

        def match(g, j, rows, base):
            t = g * GT + j
            dve.wait_ge(self.summed.sem, self.summed.free(t, GT))
            nc.vector.tensor_scalar(self.hot[0:rows, j, :], c.iota256[0:rows, :], c.tile_base[0:rows, bass.ds(base, 1)],
                                    c.dst_f[0:rows, bass.ds(t, 1)], ALU.add, ALU.is_equal).then_inc(self.hot_made.sem, 1)

        def add(g, k, j):
            t = g * GT + j
            dve.wait_ge(self.added.sem, self.added.free(t, 1))
            dve.wait_ge(self.summed.sem, self.summed.done(t))
            at = c.node_tab[:, bass.ds(first[j], 2), :]
            nc.vector.tensor_tensor(at, at, self.acc[:, (GT * k + j) % 2, 0:2 * W].rearrange("p (a b) -> p a b", a=2),
                                    ALU.add).then_inc(self.added.sem, 1)

        def start(i, k, T, rows):
            g = i * GR + k
            nc.vector.reg_load(near[k % 2], c.steps[0:1, bass.ds(g * STEP, 4)])
            match(g, 0, rows, nc.vector.snap(near[k % 2][0], min_val=0, max_val=TILES))

        def middle(i, k, T, rows):
            g = i * GR + k
            regs = near[k % 2]
            for j in range(T):
                first[j] = nc.vector.snap(regs[j], min_val=0, max_val=TILES)
            with nc.vector.If(nc.vector.snap(regs[3], min_val=0, max_val=TILES) > 0):
                nc.vector.reg_load(more, c.steps[0:1, bass.ds(g * STEP + 4, 4)])
                for j in range(T):
                    count = nc.vector.snap(more[j], min_val=0, max_val=TILES)
                    with nc.vector.If(count > 0):
                        with nc.vector.Fori(0, count) as n:
                            nc.vector.reg_add(far, far, 1)
                            now = nc.vector.snap(far)
                            tile = nc.s_assert_within(first[j] + 2 + n, 2, TILES)
                            t = g * GT + j
                            dve.wait_ge(self.added.sem, self.added.free(g * GT, 1))
                            nc.vector.tensor_scalar(self.far_hot[0:rows, :], c.iota256[0:rows, 0:P],
                                                    c.tile_base[0:rows, bass.ds(tile, 1)],
                                                    c.dst_f[0:rows, bass.ds(t, 1)], ALU.add, ALU.is_equal)\
                                .then_inc(self.far_matched, 1)
                            dve.wait_ge(self.far_summed, now)
                            at = c.node_tab[:, bass.ds(tile, 1), :]
                            nc.vector.tensor_tensor(at, at, self.far_acc[:, 0:W].rearrange("p (a b) -> p a b", a=1),
                                                    ALU.add).then_inc(self.far_added, 1)
                            dve.wait_ge(self.far_added, now)
            for j in range(1, T):
                match(g, j, rows, first[j])
                add(g, k, j - 1)

        def end(i, k, T, rows):
            add(i * GR + k, k, T - 1)
        return start, middle, end


def gather_sum(nc, c, x, edge32_t=None):
    with Phase(nc) as ctx:
        def sb(name, shape, dt=F32):
            return ctx.sbuf(name, shape, dt)

        def sem(name):
            return ctx.semaphore(name)

        rows_in = sb("rows_in", [P, RING, GT, W])
        idx = sb("idx", [P, RING, GT], I32)
        idx_in = DmaRing(ctx, nc, "idx_in")
        gathered = DmaRing(ctx, nc, "gathered", GT, pool=True)
        ones_set = sem("ones_set")
        node_sum = NodeSum(ctx, nc, c)
        if edge32_t is not None:
            feats = sb("feats", [33, RING, GT * P])
            msg = sb("msg", [P, 2, GT, W])
            pre_ps = ctx.psum("pre_ps", [P, 2, 512], F32)
            feats_in = DmaRing(ctx, nc, "feats_in")
            pre_made = Count(ctx, nc, "pre_made")
            msg_made = Count(ctx, nc, "msg_made")
        block = ctx.enter_context(nc.Block())

        @block.sync
        def _(sp):
            def load(i, k, T, rows):
                g = i * GR + k
                if edge32_t is not None:
                    wait_apart(nc.sync, ones_set, (pre_made.sem, pre_made.free(g, RING)))
                else:
                    wait_apart(nc.sync, ones_set, (node_sum.summed.sem,
                                                   node_sum.summed.free(g * GT + GT - 1, GT * RING)))
                sp.dma_start(idx[0:rows, k % RING, 0:T], idx_cols(c.src_cols, c.src, g, rows))\
                    .then_inc(idx_in.sem(k), 16)
                if edge32_t is not None:
                    sp.dma_start(feats[0:32, k % RING, 0:T * rows], group_cols(edge32_t, g, rows))\
                        .then_inc(feats_in.sem(k), 16)
            sp.wait_ge(ones_set, 1)
            laps(nc.sync, [(0, load)])

        @block.gpsimd
        def _(pool):
            used = pre_made if edge32_t is not None else node_sum.summed
            per_group = 1 if edge32_t is not None else GT
            take = PoolTakes(nc, ctx.tag)
            idx_at = take.ring(idx_in.done(0, 0), idx_in)
            used_at = take.counter(used.free(per_group - 1, per_group * RING), per_group)

            def gather(i, k, T, rows):
                take.next_group(k, [used_at])
                idx_value, used_value = take.value(idx_at), take.value(used_at)
                pool.wait_ge(ones_set, 1)
                pool.wait_ge(idx_in.sem(k), idx_value)
                pool.wait_ge(used.sem, used_value)
                for j in range(T):
                    gather_tile(nc, rows_in[0:rows, k % RING, j, 0:D], x, idx[0:rows, k % RING, j:j + 1])\
                        .then_inc(gathered.sem(k), 16 * GT if T == 1 else 16)
            laps(nc.gpsimd, [(0, gather)])

        @block.tensor
        def _(pe):
            pe.wait_ge(ones_set, 1)

            def pre(i, k, T, rows):
                g = i * GR + k
                pe.wait_ge(feats_in.sem(k), feats_in.done(i, k))
                pe.wait_ge(gathered.sem(k), gathered.done(i, k))
                pe.wait_ge(msg_made.sem, msg_made.free(g, 2))
                for j in range(T):
                    to = pre_ps[0:rows, k % 2, j * D:(j + 1) * D]
                    nc.tensor.matmul(to, feats[:, k % RING, j * P:j * P + rows], c.w_edge32[:], start=True, stop=False)
                    last = nc.tensor.matmul(to, c.ident[0:rows, 0:rows], rows_in[0:rows, k % RING, j, 0:D],
                                            start=False, stop=True)
                last.then_inc(pre_made.sem, 1)

            if edge32_t is not None:
                add_up = node_sum.on_tensor(pe, lambda k, j, rows: msg[0:rows, k % 2, j, :],
                                            lambda i, k: pe.wait_ge(msg_made.sem, msg_made.done(i * GR + k)))
            else:
                add_up = node_sum.on_tensor(pe, lambda k, j, rows: rows_in[0:rows, k % RING, j, :],
                                            lambda i, k: pe.wait_ge(gathered.sem(k), gathered.done(i, k)))

            laps(nc.tensor, [(1, pre), (0, add_up)] if edge32_t is not None else [(0, add_up)])

        if edge32_t is not None:
            @block.scalar
            def _(act):
                def rectify(i, k, T, rows):
                    g = i * GR + k
                    act.wait_ge(pre_made.sem, pre_made.done(g))
                    act.wait_ge(node_sum.summed.sem, node_sum.summed.free(g * GT + GT - 1, 2 * GT))
                    nc.scalar.activation(msg[0:rows, k % 2, 0:T, 0:D],
                                         pre_ps[0:rows, k % 2, 0:T * D].rearrange("p (a b) -> p a b", a=T),
                                         ACT.Relu).then_inc(msg_made.sem, 1)
                laps(nc.scalar, [(0, rectify)])

        @block.vector
        def _(dve):
            if edge32_t is not None:
                nc.vector.memset(feats[:], 1.0)
                nc.vector.memset(msg[:, :, :, D:W], 1.0)
            nc.vector.memset(rows_in[:, :, :, D:W], 1.0).then_inc(ones_set, 1)
            start, middle, end = node_sum.on_vector(dve)
            laps(nc.vector, [(0, middle), (1, start), (0, end)])


def idx_cols(cols, whole, g, rows):
    if rows == TAIL:
        return whole[TILES * P:N].rearrange("(p o) -> p o", o=1)
    return cols[:, bass.ds(g * GT, GT)]


def gather_tile(nc, to, table, idx):
    return nc.gpsimd.indirect_dma_start(out=to, out_offset=None, in_=table,
                                        in_offset=bass.IndirectOffsetOnAxis(ap=idx, axis=0))


class PoolTakes:

    def __init__(self, nc, tag):
        self.nc, self.tag = nc, tag
        self.rings = []
        self.made = 0

    def counter(self, first, by):
        self.made += 1
        reg = self.nc.gpsimd.alloc_register(f"{self.tag}take{self.made}")
        self.nc.gpsimd.reg_mov(reg, first - by)
        return reg, by

    def ring(self, first, ring):
        self.rings.append(self.counter(first, ring.inc))
        return self.rings[-1]

    def next_group(self, k, counters):
        for reg, by in counters + (self.rings if k % RING == 0 else []):
            self.nc.gpsimd.reg_add(reg, reg, by)

    def value(self, at):
        return self.nc.gpsimd.snap(at[0])


class RowNorm:

    def __init__(self, ctx, nc, name, steady, factor=1.0, eps=EPS):
        def sb(what, shape):
            return ctx.sbuf(f"{name}_{what}", shape, F32)
        self.nc, self.factor, self.eps, self.steady = nc, factor, eps, steady
        self.stat = sb("stat", [P, 2, GT, 6])
        self.mv = sb("mv", [P, 2, GT, 2])
        self.inv = sb("inv", [P, 2, GT])
        self.root = sb("root", [P, 2, GT])
        self.bias = sb("bias", [P, 2, GT])
        self.stat_made = Count(ctx, nc, f"{name}_stat_made")
        self.mv_made = Count(ctx, nc, f"{name}_mv_made")
        self.var_made = Count(ctx, nc, f"{name}_var_made")
        self.inv_made = Count(ctx, nc, f"{name}_inv_made")
        self.root_made = Count(ctx, nc, f"{name}_root_made")
        self.bias_made = Count(ctx, nc, f"{name}_bias_made")

    def moments(self, dve, g, b, T, rows, tile):
        nc = self.nc
        for j in range(T):
            last = nc.vector.bn_stats(self.stat[0:rows, b, j, :], tile(j))
        last.then_inc(self.stat_made.sem, 1)
        wait_apart(nc.vector, self.steady, (self.stat_made.sem, self.stat_made.done(g)))
        for j in range(T):
            last = nc.vector.bn_aggr(self.mv[0:rows, b, j, :], self.stat[0:rows, b, j, :])
        last.then_inc(self.mv_made.sem, 1)
        dve.wait_ge(self.mv_made.sem, self.mv_made.done(g))
        inv = self.inv[0:rows, b, 0:T]
        nc.vector.tensor_scalar(inv, self.mv[0:rows, b, 0:T, 1], self.factor, self.eps, ALU.mult, ALU.add)\
            .then_inc(self.var_made.sem, 1)
        dve.wait_ge(self.var_made.sem, self.var_made.done(g))
        nc.vector.reciprocal(inv, inv).then_inc(self.inv_made.sem, 1)

    def take_root(self, act, g, b, T, rows):
        act.wait_ge(self.inv_made.sem, self.inv_made.done(g))
        self.nc.scalar.activation(self.root[0:rows, b, 0:T], self.inv[0:rows, b, 0:T], ACT.Sqrt)\
            .then_inc(self.root_made.sem, 1)

    def make_bias(self, dve, g, b, T, rows):
        dve.wait_ge(self.root_made.sem, self.root_made.done(g))
        self.nc.vector.scalar_tensor_tensor(self.bias[0:rows, b, 0:T], self.mv[0:rows, b, 0:T, 0], -1.0,
                                            self.root[0:rows, b, 0:T], ALU.mult, ALU.mult)\
            .then_inc(self.bias_made.sem, 1)

    def apply(self, act, g, b, T, rows, tile, to, biased=True):
        if biased:
            act.wait_ge(self.bias_made.sem, self.bias_made.done(g))
        else:
            act.wait_ge(self.root_made.sem, self.root_made.done(g))
        for j in range(T):
            bias = self.bias[0:rows, b, j:j + 1] if biased else 0.0
            last = self.nc.scalar.activation(to(j), tile(j), ACT.Identity if biased else ACT.Copy, bias=bias,
                                             scale=self.root[0:rows, b, j:j + 1])
        return last


def take_sums(nc, c, steady, taken, used, sums, g, k, T):
    wait_apart(nc.gpsimd, steady, (used.sem, used.free(g, 2)))
    tiles = GT if T == GT else 2
    at = c.node_tab[:, bass.ds(g * GT, tiles), :]
    nc.gpsimd.tensor_copy(sums[:, k % 2, 0:tiles, :], at).then_inc(taken.sem, 1)
    wait_apart(nc.gpsimd, steady, (taken.sem, taken.done(g)))
    nc.gpsimd.tensor_copy(at, c.zeros[:, 0:tiles, :])


def transposed(nc, to, T, rows, cols, tile, ident):
    for j in range(T):
        last = nc.tensor.transpose(to[0:cols, j * P:j * P + rows], tile(j), ident[0:rows, 0:rows])
    return last


def mix_nodes(nc, c, x, x_out, layer, first):
    with Phase(nc) as ctx:
        def sb(name, shape, dt=F32):
            return ctx.sbuf(name, shape, dt)

        x_in = sb("x_in", [P, RING, GT, W])
        sums = sb("sums", [P, 2, GT, W])
        x_t = sb("x_t", [W, 2, GT * P])
        s_t = sb("s_t", [W, 2, GT * P])
        res = sb("res", [P, RING, GT, D])
        x_t_ps = ctx.psum("x_t_ps", [P, 2, 512], F32)
        s_t_ps = ctx.psum("s_t_ps", [P, 2, 512], F32)
        y_ps = ctx.psum("y_ps", [P, 2, 512], F32)
        ones_set = ctx.semaphore("ones_set")
        loaded = DmaRing(ctx, nc, "loaded")
        stored = DmaRing(ctx, nc, "stored")
        taken = Count(ctx, nc, "taken")
        x_turned = Count(ctx, nc, "x_turned")
        s_turned = Count(ctx, nc, "s_turned")
        x_copied = Count(ctx, nc, "x_copied")
        s_copied = Count(ctx, nc, "s_copied")
        mixed = Count(ctx, nc, "mixed")
        res_made = Count(ctx, nc, "res_made")
        spread = RowNorm(ctx, nc, "spread", ones_set, factor=D / (D - 1), eps=0.0)
        if first is not None:
            first_in = sb("first_in", [P, RING, GT, D])
            z = sb("z", [P, 2, GT, D])
            first_loaded = DmaRing(ctx, nc, "first_loaded")
            z_made = Count(ctx, nc, "z_made")
            norm = RowNorm(ctx, nc, "norm", ones_set)
        block = ctx.enter_context(nc.Block())

        @block.sync
        def _(sp):
            def load(i, k, T, rows):
                g = i * GR + k
                wait_apart(nc.sync, ones_set, (x_turned.sem, x_turned.free(g, RING)))
                sp.dma_start(x_in[0:rows, k % RING, 0:T, 0:D], group_rows(x, g, T, rows)).then_inc(loaded.sem(k), 16)
                if first is not None:
                    wait_apart(nc.sync, ones_set, (z_made.sem, z_made.free(g, RING)))
                    sp.dma_start(first_in[0:rows, k % RING, 0:T, :], group_rows(first, g, T, rows))\
                        .then_inc(first_loaded.sem(k), 16)

            def store(i, k, T, rows):
                g = i * GR + k
                wait_apart(nc.sync, ones_set, (res_made.sem, res_made.done(g)))
                sp.dma_start(group_rows(x_out, g, T, rows), res[0:rows, k % RING, 0:T, :]).then_inc(stored.sem(k), 16)
            sp.wait_ge(ones_set, 1)
            laps(nc.sync, [(3, load), (0, store)])
            wait_stores(sp, stored)

        @block.gpsimd
        def _(pool):
            def take(i, k, T, rows):
                take_sums(nc, c, ones_set, taken, s_turned, sums, i * GR + k, k, T)
            laps(nc.gpsimd, [(0, take)])

        @block.tensor
        def _(pe):
            def turn(i, k, T, rows):
                g = i * GR + k
                pe.wait_ge(loaded.sem(k), loaded.done(i, k))
                pe.wait_ge(x_copied.sem, x_copied.free(g, 2))
                transposed(nc, x_t_ps[:, k % 2, :], T, rows, W, lambda j: x_in[0:rows, k % RING, j, :], c.ident)\
                    .then_inc(x_turned.sem, 1)
                pe.wait_ge(taken.sem, taken.done(g))
                pe.wait_ge(s_copied.sem, s_copied.free(g, 2))
                transposed(nc, s_t_ps[:, k % 2, :], T, rows, W, lambda j: sums[0:rows, k % 2, j, :], c.ident)\
                    .then_inc(s_turned.sem, 1)

            def mix(i, k, T, rows):
                g = i * GR + k
                pe.wait_ge(x_copied.sem, x_copied.done(g))
                pe.wait_ge(s_copied.sem, s_copied.done(g))
                used = res_made if first is None else z_made
                pe.wait_ge(used.sem, used.free(g, 2))
                for j in range(T):
                    to = y_ps[0:rows, k % 2, j * D:(j + 1) * D]
                    nc.tensor.matmul(to, x_t[:, k % 2, j * P:j * P + rows], c.mix_self[layer][:], start=True, stop=False)
                    last = nc.tensor.matmul(to, s_t[:, k % 2, j * P:j * P + rows], c.mix_near[layer][:],
                                            start=False, stop=True)
                last.then_inc(mixed.sem, 1)
            pe.wait_ge(ones_set, 1)
            laps(nc.tensor, [(1, turn), (0, mix)])

        @block.scalar
        def _(act):
            def copy_x(i, k, T, rows):
                g = i * GR + k
                act.wait_ge(x_turned.sem, x_turned.done(g))
                act.wait_ge(mixed.sem, mixed.free(g, 2))
                nc.scalar.copy(x_t[:, k % 2, 0:(T - 1) * P + rows], x_t_ps[0:W, k % 2, 0:(T - 1) * P + rows])\
                    .then_inc(x_copied.sem, 1)

            def root(i, k, T, rows):
                spread.take_root(act, i * GR + k, k % 2, T, rows)

            def scale(i, k, T, rows):
                g = i * GR + k
                act.wait_ge(stored.sem(k), stored.free(i, k))
                spread.apply(act, g, k % 2, T, rows, lambda j: y_ps[0:rows, k % 2, j * D:(j + 1) * D],
                             lambda j: res[0:rows, k % RING, j, :], biased=False).then_inc(res_made.sem, 1)

            def root2(i, k, T, rows):
                norm.take_root(act, i * GR + k, k % 2, T, rows)

            def normalise(i, k, T, rows):
                g = i * GR + k
                act.wait_ge(stored.sem(k), stored.free(i, k))
                norm.apply(act, g, k % 2, T, rows, lambda j: z[0:rows, k % 2, j, :],
                           lambda j: res[0:rows, k % RING, j, :]).then_inc(res_made.sem, 1)
            if first is None:
                laps(nc.scalar, [(2, copy_x), (1, root), (0, scale)])
            else:
                laps(nc.scalar, [(3, copy_x), (2, root), (1, root2), (0, normalise)])

        @block.vector
        def _(dve):
            def copy_s(i, k, T, rows):
                g = i * GR + k
                dve.wait_ge(s_turned.sem, s_turned.done(g))
                dve.wait_ge(mixed.sem, mixed.free(g, 2))
                nc.vector.tensor_copy(s_t[:, k % 2, 0:(T - 1) * P + rows], s_t_ps[0:W, k % 2, 0:(T - 1) * P + rows])\
                    .then_inc(s_copied.sem, 1)

            def measure(i, k, T, rows):
                g = i * GR + k
                dve.wait_ge(mixed.sem, mixed.done(g))
                dve.wait_ge(spread.root_made.sem, spread.root_made.free(g, 2))
                spread.moments(dve, g, k % 2, T, rows, lambda j: y_ps[0:rows, k % 2, j * D:(j + 1) * D])

            def join(i, k, T, rows):
                g = i * GR + k
                dve.wait_ge(spread.root_made.sem, spread.root_made.done(g))
                dve.wait_ge(first_loaded.sem(k), first_loaded.done(i, k))
                dve.wait_ge(res_made.sem, res_made.free(g, 2))
                for j in range(T):
                    last = nc.vector.scalar_tensor_tensor(z[0:rows, k % 2, j, :], y_ps[0:rows, k % 2, j * D:(j + 1) * D],
                                                          spread.root[0:rows, k % 2, j:j + 1],
                                                          first_in[0:rows, k % RING, j, :], ALU.mult, ALU.add)
                last.then_inc(z_made.sem, 1)
                dve.wait_ge(z_made.sem, z_made.done(g))
                norm.moments(dve, g, k % 2, T, rows, lambda j: z[0:rows, k % 2, j, :])

            def bias(i, k, T, rows):
                norm.make_bias(dve, i * GR + k, k % 2, T, rows)
            nc.vector.memset(x_in[:, :, :, D:W], 1.0).then_inc(ones_set, 1)
            if first is None:
                laps(nc.vector, [(2, copy_s), (1, measure)])
            else:
                laps(nc.vector, [(3, copy_s), (2, measure), (1, join), (0, bias)])


def attention_edges(nc, c, x):
    with Phase(nc) as ctx:
        def sb(name, shape, dt=F32):
            return ctx.sbuf(name, shape, dt)

        def ps(name):
            return ctx.psum(name, [P, 512], F32)

        idx = sb("idx", [P, RING, 2, GT], I32)
        sources = sb("sources", [P, RING, GT * P], I32)
        rows_s = sb("rows_s", [P, RING, GT, D])
        rows_d = sb("rows_d", [P, RING, GT, D])
        s_t = sb("s_t", [D, 2, GT * P])
        d_t = sb("d_t", [D, 2, GT * P])
        q = sb("q", [P, GT, D])
        qk = sb("qk", [P, GT, D])
        score = sb("score", [P, GT * HEADS])
        weight = sb("weight", [P, 2, GT * HEADS])
        pay = sb("pay", [P, 2, GT, M])
        same = sb("same", [P, RING, GT, P])
        before = sb("before", [P, GT, P])
        repeats = sb("repeats", [P, RING, GT])
        target_f = sb("target_f", [P, RING, GT])
        target = sb("target", [P, RING, GT], I32)
        total = sb("total", [P, 2, GT, M])
        s_t_ps, d_t_ps, q_ps, k_ps, v_ps, total_ps = (ps(n) for n in ("s_t_ps", "d_t_ps", "q_ps", "k_ps", "v_ps", "total_ps"))
        ready = ctx.semaphore("ready")
        idx_in = DmaRing(ctx, nc, "idx_in", 3)
        gathered = DmaRing(ctx, nc, "gathered", 2 * GT, pool=True)
        scattered = ctx.semaphore("scattered")
        landed = Count(ctx, nc, "landed")
        turned = Count(ctx, nc, "turned")
        s_copied = Count(ctx, nc, "s_copied")
        d_copied = Count(ctx, nc, "d_copied")
        projected = Count(ctx, nc, "projected")
        q_copied = Count(ctx, nc, "q_copied")
        qk_made = Count(ctx, nc, "qk_made")
        scored = Count(ctx, nc, "scored")
        clipped = Count(ctx, nc, "clipped")
        weighed = Count(ctx, nc, "weighed")
        paid = Count(ctx, nc, "paid")
        matched = Count(ctx, nc, "matched")
        counted = Count(ctx, nc, "counted")
        aimed_f = Count(ctx, nc, "aimed_f")
        aimed = Count(ctx, nc, "aimed")
        totalled = Count(ctx, nc, "totalled")
        total_copied = Count(ctx, nc, "total_copied")
        block = ctx.enter_context(nc.Block())

        @block.sync
        def _(sp):
            def load(i, k, T, rows):
                g = i * GR + k
                wait_apart(nc.sync, ready, (turned.sem, turned.free(g, RING)), (matched.sem, matched.free(g, RING)))
                sp.dma_start(idx[0:rows, k % RING, 0, 0:T], idx_cols(c.src_cols, c.src, g, rows))\
                    .then_inc(idx_in.sem(k), 16)
                sp.dma_start(idx[0:rows, k % RING, 1, 0:T], idx_cols(c.dst_cols, c.dst, g, rows))\
                    .then_inc(idx_in.sem(k), 16)
                n = T * rows
                row = (c.src[TILES * P:N] if rows == TAIL else c.src[bass.ds(g * (GT * P), GT * P)])
                sp.dma_start(sources[0:rows, k % RING, 0:n], row.rearrange("(o f) -> o f", o=1).to_broadcast([rows, n]))\
                    .then_inc(idx_in.sem(k), 16)
            sp.wait_ge(ready, 1)
            laps(nc.sync, [(0, load)])

        @block.gpsimd
        def _(pool):
            take = PoolTakes(nc, ctx.tag)
            idx_at = take.ring(idx_in.done(0, 0), idx_in)
            turned_at = take.counter(turned.free(0, RING), 1)
            total_at = take.counter(total_copied.done(0), 1)
            added = nc.gpsimd.alloc_register("added")
            nc.gpsimd.reg_mov(added, 0)

            def gather(i, k, T, rows):
                take.next_group(k, [turned_at])
                idx_value, turned_value = take.value(idx_at), take.value(turned_at)
                pool.wait_ge(ready, 1)
                pool.wait_ge(idx_in.sem(k), idx_value)
                pool.wait_ge(turned.sem, turned_value)
                for side, to in enumerate((rows_s, rows_d)):
                    for j in range(T):
                        gather_tile(nc, to[0:rows, k % RING, j, :], x, idx[0:rows, k % RING, side, j:j + 1])\
                            .then_inc(gathered.sem(k), 16 * GT if T == 1 else 16)

            def scatter(i, k, T, rows):
                take.next_group(1, [total_at])
                total_value = take.value(total_at)
                for j in range(T):
                    added_value = nc.gpsimd.snap(added)
                    pool.wait_ge(ready, 1)
                    pool.wait_ge(scattered, added_value)
                    if j == 0:
                        pool.wait_ge(total_copied.sem, total_value)
                    nc.gpsimd.sem_inc(landed.sem, 1)
                    nc.gpsimd.indirect_dma_start(
                        out=c.att, out_offset=bass.IndirectOffsetOnAxis(ap=target[0:rows, k % RING, j:j + 1], axis=0),
                        in_=total[0:rows, k % 2, j, :], in_offset=None, compute_op=ALU.add).then_inc(scattered, 16)
                    nc.gpsimd.reg_add(added, added, 16)
            laps(nc.gpsimd, [(3, gather), (0, scatter)])
            pool.wait_ge(scattered, 16 * (TILES + 1))

        @block.tensor
        def _(pe):
            def turn(i, k, T, rows):
                g = i * GR + k
                pe.wait_ge(gathered.sem(k), gathered.done(i, k))
                pe.wait_ge(s_copied.sem, s_copied.free(g, 1))
                transposed(nc, s_t_ps, T, rows, D, lambda j: rows_s[0:rows, k % RING, j, :], c.ident)
                pe.wait_ge(d_copied.sem, d_copied.free(g, 1))
                transposed(nc, d_t_ps, T, rows, D, lambda j: rows_d[0:rows, k % RING, j, :], c.ident)\
                    .then_inc(turned.sem, 1)

            def project(i, k, T, rows):
                g = i * GR + k
                pe.wait_ge(s_copied.sem, s_copied.done(g))
                pe.wait_ge(d_copied.sem, d_copied.done(g))
                pe.wait_ge(paid.sem, paid.free(g, 1))
                for j in range(T):
                    for n, (to, side) in enumerate(((q_ps, s_t), (k_ps, d_t), (v_ps, d_t))):
                        last = nc.tensor.matmul(to[0:rows, j * D:(j + 1) * D], side[:, k % 2, j * P:j * P + rows],
                                                c.qkv[:, n * D:(n + 1) * D], start=True, stop=True)
                last.then_inc(projected.sem, 1)

            def sum_up(i, k, T, rows):
                g = i * GR + k
                pe.wait_ge(paid.sem, paid.done(g))
                pe.wait_ge(total_copied.sem, total_copied.free(g, 1))
                for j in range(T):
                    last = nc.tensor.matmul(total_ps[0:rows, j * M:(j + 1) * M], same[0:rows, k % RING, j, 0:rows],
                                            pay[0:rows, k % 2, j, :], start=True, stop=True)
                last.then_inc(totalled.sem, 1)
            pe.wait_ge(ready, 1)
            laps(nc.tensor, [(2, turn), (1, project), (0, sum_up)])

        @block.scalar
        def _(act):
            def copy_s(i, k, T, rows):
                g = i * GR + k
                act.wait_ge(turned.sem, turned.done(g))
                act.wait_ge(projected.sem, projected.free(g, 2))
                n = (T - 1) * P + rows
                nc.scalar.copy(s_t[:, k % 2, 0:n], s_t_ps[0:D, 0:n]).then_inc(s_copied.sem, 1)

            def copy_q(i, k, T, rows):
                g = i * GR + k
                act.wait_ge(projected.sem, projected.done(g))
                act.wait_ge(qk_made.sem, qk_made.free(g, 1))
                nc.scalar.copy(flat(q[0:rows, 0:T, :]), q_ps[0:rows, 0:T * D]).then_inc(q_copied.sem, 1)

            def weigh(i, k, T, rows):
                g = i * GR + k
                act.wait_ge(clipped.sem, clipped.done(g))
                act.wait_ge(paid.sem, paid.free(g, 2))
                nc.scalar.activation(weight[0:rows, k % 2, 0:T * HEADS], score[0:rows, 0:T * HEADS], ACT.Exp)\
                    .then_inc(weighed.sem, 1)

            def copy_total(i, k, T, rows):
                g = i * GR + k
                act.wait_ge(totalled.sem, totalled.done(g))
                act.wait_ge(aimed.sem, aimed.done(g))
                act.wait_ge(landed.sem, landed.free(g * GT, GT))
                nc.scalar.copy(flat(total[0:rows, k % 2, 0:T, :]), total_ps[0:rows, 0:T * M]).then_inc(total_copied.sem, 1)

            laps(nc.scalar, [(2, copy_s), (1, copy_q), (1, weigh), (0, copy_total)])

        @block.vector
        def _(dve):
            def match(i, k, T, rows):
                g = i * GR + k
                dve.wait_ge(idx_in.sem(k), idx_in.done(i, k))
                dve.wait_ge(totalled.sem, totalled.free(g, RING))
                for j in range(T):
                    last = nc.vector.tensor_scalar(same[0:rows, k % RING, j, 0:rows],
                                                   sources[0:rows, k % RING, j * P:j * P + rows],
                                                   c.src_f[0:rows, bass.ds(g * GT + j, 1)], None, ALU.is_equal)
                last.then_inc(matched.sem, 1)
                dve.wait_ge(matched.sem, matched.done(g))
                dve.wait_ge(total_copied.sem, total_copied.free(g, RING))
                for j in range(T):
                    last = nc.vector.scalar_tensor_tensor(before[0:rows, j, 0:rows], same[0:rows, k % RING, j, 0:rows], 1.0,
                                                          c.lower[0:rows, 0:rows], ALU.mult, ALU.mult,
                                                          accum_out=repeats[0:rows, k % RING, j:j + 1])
                last.then_inc(counted.sem, 1)
                dve.wait_ge(counted.sem, counted.done(g))
                nc.vector.scalar_tensor_tensor(target_f[0:rows, k % RING, 0:T], repeats[0:rows, k % RING, 0:T], 0.0,
                                               c.to_dump[0:rows, bass.ds(g * GT, T)], ALU.is_gt, ALU.mult)\
                    .then_inc(aimed_f.sem, 1)
                dve.wait_ge(aimed_f.sem, aimed_f.done(g))
                dve.wait_ge(landed.sem, landed.free(g * GT, GT * (RING - 1)))
                nc.vector.tensor_tensor(target[0:rows, k % RING, 0:T], target_f[0:rows, k % RING, 0:T],
                                        c.src_f[0:rows, bass.ds(g * GT, T)], ALU.add).then_inc(aimed.sem, 1)

            def copy_d(i, k, T, rows):
                g = i * GR + k
                dve.wait_ge(turned.sem, turned.done(g))
                dve.wait_ge(projected.sem, projected.free(g, 2))
                n = (T - 1) * P + rows
                nc.vector.tensor_copy(d_t[:, k % 2, 0:n], d_t_ps[0:D, 0:n]).then_inc(d_copied.sem, 1)

            def score_edges(i, k, T, rows):
                g = i * GR + k
                dve.wait_ge(q_copied.sem, q_copied.done(g))
                dve.wait_ge(scored.sem, scored.free(g, 1))
                nc.vector.tensor_tensor(flat(qk[0:rows, 0:T, :]), flat(q[0:rows, 0:T, :]), k_ps[0:rows, 0:T * D],
                                        ALU.mult).then_inc(qk_made.sem, 1)
                dve.wait_ge(qk_made.sem, qk_made.done(g))
                dve.wait_ge(weighed.sem, weighed.free(g, 1))
                nc.vector.tensor_reduce(score[0:rows, 0:T * HEADS],
                                        flat(qk[0:rows, 0:T, :]).rearrange("p (h f) -> p h f", f=DH), AX.X, ALU.add)\
                    .then_inc(scored.sem, 1)
                dve.wait_ge(scored.sem, scored.done(g))
                nc.vector.tensor_scalar(score[0:rows, 0:T * HEADS], score[0:rows, 0:T * HEADS], -10.0, 10.0,
                                        ALU.max, ALU.min).then_inc(clipped.sem, 1)

            def pay_edges(i, k, T, rows):
                g = i * GR + k
                dve.wait_ge(weighed.sem, weighed.done(g))
                dve.wait_ge(totalled.sem, totalled.free(g, 2))
                w = weight[0:rows, k % 2, 0:T * HEADS]
                nc.vector.tensor_copy(pay[0:rows, k % 2, 0:T, D:M], w.rearrange("p (t h) -> p t h", h=HEADS))
                for j in range(T):
                    last = nc.vector.tensor_tensor(
                        pay[0:rows, k % 2, j, 0:D].rearrange("p (h f) -> p h f", f=DH),
                        v_ps[0:rows, j * D:(j + 1) * D].rearrange("p (h f) -> p h f", f=DH),
                        w[:, j * HEADS:(j + 1) * HEADS].rearrange("p (h o) -> p h o", o=1).to_broadcast([rows, HEADS, DH]),
                        ALU.mult)
                last.then_inc(paid.sem, 1)
            nc.vector.memset(before[:], 0.0).then_inc(ready, 1)
            laps(nc.vector, [(2, match), (2, copy_d), (1, score_edges), (1, pay_edges)])


def attention_nodes(nc, c, x, x_out):
    with Phase(nc) as ctx:
        def sb(name, shape, dt=F32):
            return ctx.sbuf(name, shape, dt)

        att_in = sb("att_in", [P, RING, GT, M])
        x_in = sb("x_in", [P, RING, GT, D])
        share = sb("share", [P, 2, GT, HEADS])
        seen = sb("seen", [P, 2, GT, D])
        z = sb("z", [P, 2, GT, D])
        res = sb("res", [P, RING, GT, D])
        x_t = sb("x_t", [D, 2, GT * P])
        f = sb("f", [D, 2, GT * P])
        x_t_ps = ctx.psum("x_t_ps", [P, 2, 512], F32)
        f_ps = ctx.psum("f_ps", [P, 2, 512], F32)
        ready = ctx.semaphore("ready")
        loaded = DmaRing(ctx, nc, "loaded", 2)
        stored = DmaRing(ctx, nc, "stored")
        floored = Count(ctx, nc, "floored")
        shared = Count(ctx, nc, "shared")
        seen_made = Count(ctx, nc, "seen_made")
        z_made = Count(ctx, nc, "z_made")
        res_made = Count(ctx, nc, "res_made")
        turned = Count(ctx, nc, "turned")
        copied = Count(ctx, nc, "copied")
        projected = Count(ctx, nc, "projected")
        rectified = Count(ctx, nc, "rectified")
        counted = Count(ctx, nc, "counted")
        norm = RowNorm(ctx, nc, "norm", ready)
        block = ctx.enter_context(nc.Block())

        @block.sync
        def _(sp):
            def load(i, k, T, rows):
                g = i * GR + k
                wait_apart(nc.sync, ready, (z_made.sem, z_made.free(g, RING)))
                sp.dma_start(att_in[0:rows, k % RING, 0:T, :], group_rows(c.att, g, T, rows)).then_inc(loaded.sem(k), 16)
                sp.dma_start(x_in[0:rows, k % RING, 0:T, :], group_rows(x, g, T, rows)).then_inc(loaded.sem(k), 16)

            def store(i, k, T, rows):
                g = i * GR + k
                wait_apart(nc.sync, ready, (res_made.sem, res_made.done(g)))
                sp.dma_start(group_rows(x_out, g, T, rows), res[0:rows, k % RING, 0:T, :]).then_inc(stored.sem(k), 16)
            sp.wait_ge(ready, 1)
            laps(nc.sync, [(3, load), (0, store)])
            wait_stores(sp, stored)

        @block.tensor
        def _(pe):
            def turn(i, k, T, rows):
                g = i * GR + k
                pe.wait_ge(res_made.sem, res_made.done(g))
                pe.wait_ge(copied.sem, copied.free(g, 2))
                transposed(nc, x_t_ps[:, k % 2, :], T, rows, D, lambda j: res[0:rows, k % RING, j, :], c.ident)\
                    .then_inc(turned.sem, 1)

            def project(i, k, T, rows):
                g = i * GR + k
                pe.wait_ge(copied.sem, copied.done(g))
                pe.wait_ge(rectified.sem, rectified.free(g, 2))
                nc.tensor.matmul(f_ps[0:D, k % 2, 0:T * rows], c.w_node[:], x_t[:, k % 2, 0:T * rows],
                                 start=True, stop=True).then_inc(projected.sem, 1)
            laps(nc.tensor, [(1, turn), (0, project)])

        @block.scalar
        def _(act):
            def root(i, k, T, rows):
                norm.take_root(act, i * GR + k, k % 2, T, rows)

            def normalise(i, k, T, rows):
                g = i * GR + k
                act.wait_ge(stored.sem(k), stored.free(i, k))
                act.wait_ge(turned.sem, turned.free(g, RING))
                norm.apply(act, g, k % 2, T, rows, lambda j: z[0:rows, k % 2, j, :],
                           lambda j: res[0:rows, k % RING, j, :]).then_inc(res_made.sem, 1)

            def copy_x(i, k, T, rows):
                g = i * GR + k
                act.wait_ge(turned.sem, turned.done(g))
                act.wait_ge(projected.sem, projected.free(g, 2))
                nc.scalar.copy(x_t[:, k % 2, 0:T * rows], x_t_ps[0:D, k % 2, 0:T * rows]).then_inc(copied.sem, 1)

            def rectify(i, k, T, rows):
                g = i * GR + k
                act.wait_ge(projected.sem, projected.done(g))
                act.wait_ge(counted.sem, counted.free(g, 2))
                nc.scalar.activation(f[:, k % 2, 0:T * rows], f_ps[0:D, k % 2, 0:T * rows], ACT.Relu,
                                     bias=column(c, "b_node")).then_inc(rectified.sem, 1)
            laps(nc.scalar, [(3, root), (2, normalise), (1, copy_x), (0, rectify)])

        @block.gpsimd
        def _(pool):
            def see(i, k, T, rows):
                g = i * GR + k
                pool.wait_ge(shared.sem, shared.done(g))
                pool.wait_ge(z_made.sem, z_made.free(g, 2))
                for j in range(T):
                    last = nc.gpsimd.tensor_tensor(
                        seen[0:rows, k % 2, j, :].rearrange("p (h f) -> p h f", f=DH),
                        att_in[0:rows, k % RING, j, 0:D].rearrange("p (h f) -> p h f", f=DH),
                        share[0:rows, k % 2, j, :].rearrange("p (h o) -> p h o", o=1).to_broadcast([rows, HEADS, DH]),
                        ALU.mult)
                last.then_inc(seen_made.sem, 1)
            laps(nc.gpsimd, [(0, see)])

        @block.vector
        def _(dve):
            nc.vector.memset(share[:], 0.0).then_inc(ready, 1)

            def divide(i, k, T, rows):
                g = i * GR + k
                dve.wait_ge(loaded.sem(k), loaded.done(i, k))
                dve.wait_ge(seen_made.sem, seen_made.free(g, 2))
                at = share[0:rows, k % 2, 0:T, :]
                nc.vector.tensor_scalar(at, att_in[0:rows, k % RING, 0:T, D:M], 1e-8, None, ALU.add)\
                    .then_inc(floored.sem, 1)
                dve.wait_ge(floored.sem, floored.done(g))
                nc.vector.reciprocal(at, at).then_inc(shared.sem, 1)

            def join(i, k, T, rows):
                g = i * GR + k
                dve.wait_ge(seen_made.sem, seen_made.done(g))
                dve.wait_ge(res_made.sem, res_made.free(g, 2))
                nc.vector.scalar_tensor_tensor(flat(z[0:rows, k % 2, 0:T, :]), flat(x_in[0:rows, k % RING, 0:T, :]), 2.0,
                                               flat(seen[0:rows, k % 2, 0:T, :]), ALU.mult, ALU.add)\
                    .then_inc(z_made.sem, 1)
                dve.wait_ge(z_made.sem, z_made.done(g))
                norm.moments(dve, g, k % 2, T, rows, lambda j: z[0:rows, k % 2, j, :])

            def bias(i, k, T, rows):
                norm.make_bias(dve, i * GR + k, k % 2, T, rows)

            def count(i, k, T, rows):
                g = i * GR + k
                dve.wait_ge(rectified.sem, rectified.done(g))
                nc.vector.bn_stats(record(c.stat, g), f[:, k % 2, 0:T * rows]).then_inc(counted.sem, 1)
            laps(nc.vector, [(4, divide), (3, join), (2, bias), (0, count)])


def message_edges(nc, c, x, edge4_t):
    with Phase(nc) as ctx:
        def sb(name, shape, dt=F32):
            return ctx.sbuf(name, shape, dt)

        idx = sb("idx", [P, RING, 2, GT], I32)
        rows_s = sb("rows_s", [P, RING, GT, D])
        rows_d = sb("rows_d", [P, RING, GT, D])
        feats = sb("feats", [5, RING, GT * P])
        s_t = sb("s_t", [W, 2, GT * P])
        d_t = sb("d_t", [D, 2, GT * P])
        f_t = sb("f_t", [D, 2, GT * P])
        m_t = sb("m_t", [D, 2, GT * P])
        msg = sb("msg", [P, 2, GT, W])
        s_t_ps, d_t_ps, f_t_ps, m_t_ps, msg_ps = (ctx.psum(n, [P, 512], F32)
                                                  for n in ("s_t_ps", "d_t_ps", "f_t_ps", "m_t_ps", "msg_ps"))
        ready = ctx.semaphore("ready")
        idx_in = DmaRing(ctx, nc, "idx_in", 3)
        gathered = DmaRing(ctx, nc, "gathered", 2 * GT, pool=True)
        turned = Count(ctx, nc, "turned")
        s_copied = Count(ctx, nc, "s_copied")
        d_copied = Count(ctx, nc, "d_copied")
        f_made = Count(ctx, nc, "f_made")
        multiplied = Count(ctx, nc, "multiplied")
        m_made = Count(ctx, nc, "m_made")
        counted = Count(ctx, nc, "counted")
        turned_back = Count(ctx, nc, "turned_back")
        msg_made = Count(ctx, nc, "msg_made")
        node_sum = NodeSum(ctx, nc, c)
        block = ctx.enter_context(nc.Block())

        @block.sync
        def _(sp):
            def load(i, k, T, rows):
                g = i * GR + k
                wait_apart(nc.sync, ready, (turned.sem, turned.free(g, RING)))
                sp.dma_start(idx[0:rows, k % RING, 0, 0:T], idx_cols(c.src_cols, c.src, g, rows))\
                    .then_inc(idx_in.sem(k), 16)
                sp.dma_start(idx[0:rows, k % RING, 1, 0:T], idx_cols(c.dst_cols, c.dst, g, rows))\
                    .then_inc(idx_in.sem(k), 16)
                sp.dma_start(feats[0:4, k % RING, 0:T * rows], group_cols(edge4_t, g, rows)).then_inc(idx_in.sem(k), 16)
            sp.wait_ge(ready, 1)
            laps(nc.sync, [(0, load)])

        @block.gpsimd
        def _(pool):
            take = PoolTakes(nc, ctx.tag)
            idx_at = take.ring(idx_in.done(0, 0), idx_in)
            turned_at = take.counter(turned.free(0, RING), 1)

            def gather(i, k, T, rows):
                take.next_group(k, [turned_at])
                idx_value, turned_value = take.value(idx_at), take.value(turned_at)
                pool.wait_ge(ready, 1)
                pool.wait_ge(idx_in.sem(k), idx_value)
                pool.wait_ge(turned.sem, turned_value)
                for side, to in enumerate((rows_s, rows_d)):
                    for j in range(T):
                        gather_tile(nc, to[0:rows, k % RING, j, :], x, idx[0:rows, k % RING, side, j:j + 1])\
                            .then_inc(gathered.sem(k), 16 * GT if T == 1 else 16)
            laps(nc.gpsimd, [(0, gather)])

        @block.tensor
        def _(pe):
            def turn(i, k, T, rows):
                g = i * GR + k
                pe.wait_ge(idx_in.sem(k), idx_in.done(i, k))
                pe.wait_ge(f_made.sem, f_made.free(g, 1))
                nc.tensor.matmul(f_t_ps[0:D, 0:T * rows], c.w_edge4[:], feats[:, k % RING, 0:T * rows],
                                 start=True, stop=True)
                pe.wait_ge(gathered.sem(k), gathered.done(i, k))
                pe.wait_ge(s_copied.sem, s_copied.free(g, 1))
                transposed(nc, s_t_ps, T, rows, D, lambda j: rows_s[0:rows, k % RING, j, :], c.ident)
                pe.wait_ge(d_copied.sem, d_copied.free(g, 1))
                transposed(nc, d_t_ps, T, rows, D, lambda j: rows_d[0:rows, k % RING, j, :], c.ident)\
                    .then_inc(turned.sem, 1)

            def multiply(i, k, T, rows):
                g = i * GR + k
                pe.wait_ge(s_copied.sem, s_copied.done(g))
                pe.wait_ge(d_copied.sem, d_copied.done(g))
                pe.wait_ge(f_made.sem, f_made.done(g))
                pe.wait_ge(m_made.sem, m_made.free(g, 1))
                n = T * rows
                to = m_t_ps[0:D, 0:n]
                nc.tensor.matmul(to, c.w_src[:], s_t[:, k % 2, 0:n], start=True, stop=False)
                nc.tensor.matmul(to, c.w_dst[:], d_t[:, k % 2, 0:n], start=False, stop=False)
                nc.tensor.matmul(to, c.w_feat[:], f_t[:, k % 2, 0:n], start=False, stop=True).then_inc(multiplied.sem, 1)

            def turn_back(i, k, T, rows):
                g = i * GR + k
                pe.wait_ge(m_made.sem, m_made.done(g))
                pe.wait_ge(msg_made.sem, msg_made.free(g, 1))
                for j in range(T):
                    last = nc.tensor.transpose(msg_ps[0:rows, j * D:(j + 1) * D], m_t[:, k % 2, j * P:j * P + rows],
                                               c.ident[0:D, 0:D])
                last.then_inc(turned_back.sem, 1)
            add_up = node_sum.on_tensor(pe, lambda k, j, rows: msg[0:rows, k % 2, j, :],
                                        lambda i, k: pe.wait_ge(msg_made.sem, msg_made.done(i * GR + k)))
            pe.wait_ge(ready, 1)
            laps(nc.tensor, [(3, turn), (2, multiply), (1, turn_back), (0, add_up)])

        @block.scalar
        def _(act):
            def copy_s(i, k, T, rows):
                g = i * GR + k
                act.wait_ge(turned.sem, turned.done(g))
                act.wait_ge(multiplied.sem, multiplied.free(g, 2))
                nc.scalar.copy(s_t[0:D, k % 2, 0:T * rows], s_t_ps[0:D, 0:T * rows]).then_inc(s_copied.sem, 1)
                nc.scalar.activation(f_t[:, k % 2, 0:T * rows], f_t_ps[0:D, 0:T * rows], ACT.Relu).then_inc(f_made.sem, 1)

            def rectify(i, k, T, rows):
                g = i * GR + k
                act.wait_ge(multiplied.sem, multiplied.done(g))
                act.wait_ge(counted.sem, counted.free(g, 2))
                act.wait_ge(turned_back.sem, turned_back.free(g, 2))
                nc.scalar.activation(m_t[:, k % 2, 0:T * rows], m_t_ps[0:D, 0:T * rows], ACT.Relu).then_inc(m_made.sem, 1)

            def copy_back(i, k, T, rows):
                g = i * GR + k
                act.wait_ge(turned_back.sem, turned_back.done(g))
                act.wait_ge(node_sum.summed.sem, node_sum.summed.free(g * GT + GT - 1, 2 * GT))
                nc.scalar.copy(msg[0:rows, k % 2, 0:T, 0:D],
                               msg_ps[0:rows, 0:T * D].rearrange("p (a b) -> p a b", a=T)).then_inc(msg_made.sem, 1)
            laps(nc.scalar, [(3, copy_s), (2, rectify), (1, copy_back)])

        @block.vector
        def _(dve):
            nc.vector.memset(feats[:], 1.0)
            nc.vector.memset(s_t[D:W, :, :], 1.0)
            nc.vector.memset(msg[:, :, :, D:W], 1.0).then_inc(ready, 1)

            def copy_d(i, k, T, rows):
                g = i * GR + k
                dve.wait_ge(turned.sem, turned.done(g))
                dve.wait_ge(multiplied.sem, multiplied.free(g, 2))
                nc.vector.tensor_copy(d_t[:, k % 2, 0:T * rows], d_t_ps[0:D, 0:T * rows]).then_inc(d_copied.sem, 1)

            def count(i, k, T, rows):
                g = i * GR + k
                dve.wait_ge(m_made.sem, m_made.done(g))
                nc.vector.bn_stats(record(c.stat_msg, g), m_t[:, k % 2, 0:T * rows]).then_inc(counted.sem, 1)
            start, middle, end = node_sum.on_vector(dve)
            laps(nc.vector, [(3, copy_d), (2, count), (0, middle), (1, start), (0, end)])


def message_nodes(nc, c, x, x_out):
    with Phase(nc) as ctx:
        def sb(name, shape, dt=F32):
            return ctx.sbuf(name, shape, dt)

        x_in = sb("x_in", [P, RING, GT, W])
        sums = sb("sums", [P, 2, GT, W])
        x_t = sb("x_t", [W, 2, GT * P])
        s_t = sb("s_t", [W, 2, GT * P])
        f_t = sb("f_t", [D, 2, GT * P])
        res = sb("res", [P, RING, GT, D])
        terms_n = sb("terms_n", [D, 2])
        terms_m = sb("terms_m", [D, 2])
        left_x = sb("left_x", [D, W])
        left_m = sb("left_m", [D, W])
        keep_x = sb("keep_x", [W, D])
        scale_m = sb("scale_m", [W, D])
        scale_n = sb("scale_n", [D, D])
        x_t_ps = ctx.psum("x_t_ps", [P, 2, 512], F32)
        s_t_ps = ctx.psum("s_t_ps", [P, 2, 512], F32)
        f_t_ps = ctx.psum("f_t_ps", [P, 512], F32)
        z_ps = ctx.psum("z_ps", [P, 2, 512], F32)
        small_ps = ctx.psum("small_ps", [P, 512], F32)
        ready = ctx.semaphore("ready")
        folding = ctx.semaphore("folding")
        folded = ctx.semaphore("folded")
        constants = ctx.semaphore("constants")
        norm_n = Norm(ctx, nc, "nodes")
        norm_m = Norm(ctx, nc, "messages")
        loaded = DmaRing(ctx, nc, "loaded")
        stored = DmaRing(ctx, nc, "stored")
        taken = Count(ctx, nc, "taken")
        x_turned = Count(ctx, nc, "x_turned")
        s_turned = Count(ctx, nc, "s_turned")
        x_copied = Count(ctx, nc, "x_copied")
        s_copied = Count(ctx, nc, "s_copied")
        projected = Count(ctx, nc, "projected")
        f_made = Count(ctx, nc, "f_made")
        joined = Count(ctx, nc, "joined")
        res_made = Count(ctx, nc, "res_made")
        norm = RowNorm(ctx, nc, "norm", ready)
        block = ctx.enter_context(nc.Block())

        @block.sync
        def _(sp):
            def load(i, k, T, rows):
                g = i * GR + k
                wait_apart(nc.sync, ready, (x_turned.sem, x_turned.free(g, RING)))
                sp.dma_start(x_in[0:rows, k % RING, 0:T, 0:D], group_rows(x, g, T, rows)).then_inc(loaded.sem(k), 16)

            def store(i, k, T, rows):
                g = i * GR + k
                wait_apart(nc.sync, ready, (res_made.sem, res_made.done(g)))
                sp.dma_start(group_rows(x_out, g, T, rows), res[0:rows, k % RING, 0:T, :]).then_inc(stored.sem(k), 16)
            sp.wait_ge(ready, 1)
            laps(nc.sync, [(4, load), (0, store)])
            wait_stores(sp, stored)

        @block.gpsimd
        def _(pool):
            def take(i, k, T, rows):
                take_sums(nc, c, ready, taken, s_turned, sums, i * GR + k, k, T)
            laps(nc.gpsimd, [(0, take)])

        @block.tensor
        def _(pe):
            pe.wait_ge(folding, 2)
            nc.tensor.matmul(small_ps[0:W, 0:D], left_x[:], c.ident[0:D, 0:D], start=True, stop=True)
            nc.tensor.matmul(small_ps[0:W, D:2 * D], left_m[:], c.ident[0:D, 0:D], start=True, stop=True)\
                .then_inc(folded, 1)
            pe.wait_ge(constants, 3)
            pe.wait_ge(ready, 1)

            def turn(i, k, T, rows):
                g = i * GR + k
                pe.wait_ge(loaded.sem(k), loaded.done(i, k))
                pe.wait_ge(x_copied.sem, x_copied.free(g, 2))
                transposed(nc, x_t_ps[:, k % 2, :], T, rows, W, lambda j: x_in[0:rows, k % RING, j, :], c.ident)\
                    .then_inc(x_turned.sem, 1)
                pe.wait_ge(taken.sem, taken.done(g))
                pe.wait_ge(s_copied.sem, s_copied.free(g, 2))
                transposed(nc, s_t_ps[:, k % 2, :], T, rows, W, lambda j: sums[0:rows, k % 2, j, :], c.ident)\
                    .then_inc(s_turned.sem, 1)

            def project(i, k, T, rows):
                g = i * GR + k
                pe.wait_ge(x_copied.sem, x_copied.done(g))
                pe.wait_ge(f_made.sem, f_made.free(g, 1))
                nc.tensor.matmul(f_t_ps[0:D, 0:T * rows], c.w_node[:], x_t[0:D, k % 2, 0:T * rows],
                                 start=True, stop=True).then_inc(projected.sem, 1)

            def join(i, k, T, rows):
                g = i * GR + k
                pe.wait_ge(s_copied.sem, s_copied.done(g))
                pe.wait_ge(f_made.sem, f_made.done(g))
                pe.wait_ge(res_made.sem, res_made.free(g, 2))
                for j in range(T):
                    to = z_ps[0:rows, k % 2, j * D:(j + 1) * D]
                    at = slice(j * P, j * P + rows)
                    nc.tensor.matmul(to, x_t[:, k % 2, at], keep_x[:], start=True, stop=False)
                    nc.tensor.matmul(to, s_t[:, k % 2, at], scale_m[:], start=False, stop=False)
                    last = nc.tensor.matmul(to, f_t[:, k % 2, at], scale_n[:], start=False, stop=True)
                last.then_inc(joined.sem, 1)
            laps(nc.tensor, [(3, turn), (2, project), (1, join)])

        @block.scalar
        def _(act):
            norm_n.on_scalar(act)
            norm_m.on_scalar(act)

            def copy_x(i, k, T, rows):
                g = i * GR + k
                act.wait_ge(x_turned.sem, x_turned.done(g))
                act.wait_ge(joined.sem, joined.free(g, 2))
                nc.scalar.copy(x_t[:, k % 2, 0:T * rows], x_t_ps[0:W, k % 2, 0:T * rows]).then_inc(x_copied.sem, 1)

            def rectify(i, k, T, rows):
                g = i * GR + k
                act.wait_ge(projected.sem, projected.done(g))
                act.wait_ge(joined.sem, joined.free(g, 2))
                nc.scalar.activation(f_t[:, k % 2, 0:T * rows], f_t_ps[0:D, 0:T * rows], ACT.Relu,
                                     bias=column(c, "b_node")).then_inc(f_made.sem, 1)

            def root(i, k, T, rows):
                norm.take_root(act, i * GR + k, k % 2, T, rows)

            def normalise(i, k, T, rows):
                g = i * GR + k
                act.wait_ge(stored.sem(k), stored.free(i, k))
                norm.apply(act, g, k % 2, T, rows, lambda j: z_ps[0:rows, k % 2, j * D:(j + 1) * D],
                           lambda j: res[0:rows, k % RING, j, :]).then_inc(res_made.sem, 1)
            laps(nc.scalar, [(3, copy_x), (2, rectify), (1, root), (0, normalise)])

        @block.vector
        def _(dve):
            nc.vector.memset(x_in[:, :, :, D:W], 1.0).then_inc(ready, 1)
            norm_n.on_vector(dve, c.stat, column(c, "g_node"), column(c, "beta_node"), terms_n)
            norm_m.on_vector(dve, c.stat_msg, column(c, "g_msg"), column(c, "beta_msg"), terms_m)
            eye = c.ident[0:D, 0:D]
            nc.vector.tensor_copy(left_x[:, 0:D], eye)
            nc.vector.tensor_copy(left_x[:, D:W], terms_n[:, 1:2]).then_inc(folding, 1)
            nc.vector.tensor_scalar(left_m[:, 0:D], eye, terms_m[:, 0:1], None, ALU.mult)
            nc.vector.tensor_copy(left_m[:, D:W], terms_m[:, 1:2]).then_inc(folding, 1)
            nc.vector.tensor_scalar(scale_n[:], eye, terms_n[:, 0:1], None, ALU.mult).then_inc(constants, 1)
            dve.wait_ge(folded, 1)
            nc.vector.tensor_copy(keep_x[:], small_ps[0:W, 0:D]).then_inc(constants, 1)
            nc.vector.tensor_copy(scale_m[:], small_ps[0:W, D:2 * D]).then_inc(constants, 1)

            def copy_s(i, k, T, rows):
                g = i * GR + k
                dve.wait_ge(s_turned.sem, s_turned.done(g))
                dve.wait_ge(joined.sem, joined.free(g, 2))
                nc.vector.tensor_copy(s_t[:, k % 2, 0:T * rows], s_t_ps[0:W, k % 2, 0:T * rows]).then_inc(s_copied.sem, 1)

            def measure(i, k, T, rows):
                g = i * GR + k
                dve.wait_ge(joined.sem, joined.done(g))
                dve.wait_ge(res_made.sem, res_made.free(g, 2))
                norm.moments(dve, g, k % 2, T, rows, lambda j: z_ps[0:rows, k % 2, j * D:(j + 1) * D])

            def bias(i, k, T, rows):
                norm.make_bias(dve, i * GR + k, k % 2, T, rows)
            laps(nc.vector, [(3, copy_s), (1, measure), (0, bias)])


def mlp_nodes(nc, c, x):
    with Phase(nc) as ctx:
        def sb(name, shape, dt=F32):
            return ctx.sbuf(name, shape, dt)

        x_in = sb("x_in", [P, RING, GT, D])
        h = sb("h", [P, 2, GT, D])
        h_t = sb("h_t", [D, 2, GT * P])
        r_t = sb("r_t", [W, 2, GT * P])
        h_t_ps = ctx.psum("h_t_ps", [P, 2, 512], F32)
        r_t_ps = ctx.psum("r_t_ps", [P, 2, 512], F32)
        h2_t_ps = ctx.psum("h2_t_ps", [P, 512], F32)
        h2_ps = ctx.psum("h2_ps", [P, 2, 512], F32)
        ready = ctx.semaphore("ready")
        loaded = DmaRing(ctx, nc, "loaded")
        h_made = Count(ctx, nc, "h_made")
        turned = Count(ctx, nc, "turned")
        copied = Count(ctx, nc, "copied")
        first = Count(ctx, nc, "first")
        rectified = Count(ctx, nc, "rectified")
        second_t = Count(ctx, nc, "second_t")
        second = Count(ctx, nc, "second")
        counted = Count(ctx, nc, "counted")
        kept = Count(ctx, nc, "kept")
        block = ctx.enter_context(nc.Block())

        @block.sync
        def _(sp):
            def load(i, k, T, rows):
                g = i * GR + k
                wait_apart(nc.sync, ready, (h_made.sem, h_made.free(g, RING)))
                sp.dma_start(x_in[0:rows, k % RING, 0:T, :], group_rows(x, g, T, rows)).then_inc(loaded.sem(k), 16)
            sp.wait_ge(ready, 1)
            laps(nc.sync, [(0, load)])

        @block.gpsimd
        def _(pool):
            def join(i, k, T, rows):
                g = i * GR + k
                wait_apart(nc.gpsimd, ready, (loaded.sem(k), loaded.done(i, k)), (turned.sem, turned.free(g, 2)))
                nc.gpsimd.tensor_tensor(h[0:rows, k % 2, 0:T, :], x_in[0:rows, k % RING, 0:T, :],
                                        c.node_tab[0:rows, bass.ds(g * GT, T), 0:D], ALU.add).then_inc(h_made.sem, 1)
            laps(nc.gpsimd, [(0, join)])

        @block.tensor
        def _(pe):
            def turn(i, k, T, rows):
                g = i * GR + k
                pe.wait_ge(h_made.sem, h_made.done(g))
                pe.wait_ge(copied.sem, copied.free(g, 2))
                transposed(nc, h_t_ps[:, k % 2, :], T, rows, D, lambda j: h[0:rows, k % 2, j, :], c.ident)\
                    .then_inc(turned.sem, 1)

            def one(i, k, T, rows):
                g = i * GR + k
                pe.wait_ge(copied.sem, copied.done(g))
                pe.wait_ge(rectified.sem, rectified.free(g, 2))
                nc.tensor.matmul(r_t_ps[0:D, k % 2, 0:T * rows], c.w1[:], h_t[:, k % 2, 0:T * rows],
                                 start=True, stop=True).then_inc(first.sem, 1)

            def two(i, k, T, rows):
                g = i * GR + k
                pe.wait_ge(rectified.sem, rectified.done(g))
                pe.wait_ge(counted.sem, counted.free(g, 1))
                nc.tensor.matmul(h2_t_ps[0:D, 0:T * rows], c.w2[:], r_t[:, k % 2, 0:T * rows],
                                 start=True, stop=True).then_inc(second_t.sem, 1)
                pe.wait_ge(kept.sem, kept.free(g, 2))
                for j in range(T):
                    last = nc.tensor.matmul(h2_ps[0:rows, k % 2, j * D:(j + 1) * D], r_t[:, k % 2, j * P:j * P + rows],
                                            c.w2[:], start=True, stop=True)
                last.then_inc(second.sem, 1)
            pe.wait_ge(ready, 1)
            laps(nc.tensor, [(2, turn), (1, one), (0, two)])

        @block.scalar
        def _(act):
            def copy_h(i, k, T, rows):
                g = i * GR + k
                act.wait_ge(turned.sem, turned.done(g))
                act.wait_ge(first.sem, first.free(g, 2))
                nc.scalar.copy(h_t[:, k % 2, 0:T * rows], h_t_ps[0:D, k % 2, 0:T * rows]).then_inc(copied.sem, 1)

            def rectify(i, k, T, rows):
                g = i * GR + k
                act.wait_ge(first.sem, first.done(g))
                act.wait_ge(second.sem, second.free(g, 2))
                nc.scalar.activation(r_t[0:D, k % 2, 0:T * rows], r_t_ps[0:D, k % 2, 0:T * rows], ACT.Relu,
                                     bias=column(c, "b1")).then_inc(rectified.sem, 1)
            laps(nc.scalar, [(1, copy_h), (0, rectify)])

        @block.vector
        def _(dve):
            nc.vector.memset(r_t[D:W, :, :], 1.0).then_inc(ready, 1)

            def count(i, k, T, rows):
                g = i * GR + k
                dve.wait_ge(second_t.sem, second_t.done(g))
                nc.vector.bn_stats(record(c.stat, g), h2_t_ps[0:D, 0:T * rows]).then_inc(counted.sem, 1)

            def keep(i, k, T, rows):
                g = i * GR + k
                dve.wait_ge(second.sem, second.done(g))
                dve.wait_ge(h_made.sem, h_made.done(g))
                nc.vector.tensor_copy(c.node_tab[0:rows, bass.ds(g * GT, T), 0:D],
                                      h2_ps[0:rows, k % 2, 0:T * D].rearrange("p (a b) -> p a b", a=T))\
                    .then_inc(kept.sem, 1)
            laps(nc.vector, [(0, count), (0, keep)])


def out_nodes(nc, c, x, out):
    with Phase(nc) as ctx:
        def sb(name, shape, dt=F32):
            return ctx.sbuf(name, shape, dt)

        x_in = sb("x_in", [P, RING, GT, D])
        scaled = sb("scaled", [P, 2, GT, D])
        z = sb("z", [P, 2, GT, D])
        res = sb("res", [P, RING, GT, D])
        terms = sb("terms", [D, 2])
        diag = sb("diag", [D, 2, D])
        scale = sb("scale", [P, GT, D])
        shift = sb("shift", [P, GT, D])
        rows_ps = ctx.psum("rows_ps", [P, 512], F32)
        ready = ctx.semaphore("ready")
        diag_made = ctx.semaphore("diag_made")
        spread_out = ctx.semaphore("spread_out")
        norm_h = Norm(ctx, nc, "h2")
        loaded = DmaRing(ctx, nc, "loaded")
        stored = DmaRing(ctx, nc, "stored")
        scaled_made = Count(ctx, nc, "scaled_made")
        shifted = Count(ctx, nc, "shifted")
        z_made = Count(ctx, nc, "z_made")
        res_made = Count(ctx, nc, "res_made")
        norm = RowNorm(ctx, nc, "norm", ready)
        block = ctx.enter_context(nc.Block())

        @block.sync
        def _(sp):
            def load(i, k, T, rows):
                g = i * GR + k
                wait_apart(nc.sync, ready, (z_made.sem, z_made.free(g, RING)))
                sp.dma_start(x_in[0:rows, k % RING, 0:T, :], group_rows(x, g, T, rows)).then_inc(loaded.sem(k), 16)

            def store(i, k, T, rows):
                g = i * GR + k
                wait_apart(nc.sync, ready, (res_made.sem, res_made.done(g)))
                sp.dma_start(group_rows(out, g, T, rows), res[0:rows, k % RING, 0:T, :]).then_inc(stored.sem(k), 16)
            sp.wait_ge(ready, 1)
            laps(nc.sync, [(3, load), (0, store)])
            wait_stores(sp, stored)

        @block.tensor
        def _(pe):
            pe.wait_ge(diag_made, 2)
            for n in range(2):
                last = nc.tensor.matmul(rows_ps[:, n * D:(n + 1) * D], c.ones[0:D, :], diag[:, n, :], start=True, stop=True)
            last.then_inc(spread_out, 1)

        @block.gpsimd
        def _(pool):
            def multiply(i, k, T, rows):
                g = i * GR + k
                wait_apart(nc.gpsimd, ready, (z_made.sem, z_made.free(g, 2)))
                nc.gpsimd.tensor_tensor(scaled[0:rows, k % 2, 0:T, :], c.node_tab[0:rows, bass.ds(g * GT, T), 0:D],
                                        scale[0:rows, 0:T, :], ALU.mult).then_inc(scaled_made.sem, 1)
            pool.wait_ge(ready, 1)
            laps(nc.gpsimd, [(0, multiply)])

        @block.scalar
        def _(act):
            norm_h.on_scalar(act)

            def root(i, k, T, rows):
                norm.take_root(act, i * GR + k, k % 2, T, rows)

            def normalise(i, k, T, rows):
                g = i * GR + k
                act.wait_ge(stored.sem(k), stored.free(i, k))
                norm.apply(act, g, k % 2, T, rows, lambda j: z[0:rows, k % 2, j, :],
                           lambda j: res[0:rows, k % RING, j, :]).then_inc(res_made.sem, 1)
            laps(nc.scalar, [(1, root), (0, normalise)])

        @block.vector
        def _(dve):
            norm_h.on_vector(dve, c.stat, column(c, "gamma"), column(c, "beta"), terms)
            for n in range(2):
                nc.vector.tensor_scalar(diag[:, n, :], c.ident[0:D, 0:D], terms[:, n:n + 1], None, ALU.mult)\
                    .then_inc(diag_made, 1)
            dve.wait_ge(spread_out, 1)
            for n, to in enumerate((scale, shift)):
                for j in range(GT):
                    last = nc.vector.tensor_copy(to[:, j, :], rows_ps[:, n * D:(n + 1) * D])
            last.then_inc(ready, 1)

            def join(i, k, T, rows):
                g = i * GR + k
                dve.wait_ge(scaled_made.sem, scaled_made.done(g))
                dve.wait_ge(res_made.sem, res_made.free(g, 2))
                u = flat(z[0:rows, k % 2, 0:T, :])
                nc.vector.tensor_tensor(u, flat(scaled[0:rows, k % 2, 0:T, :]), flat(shift[0:rows, 0:T, :]), ALU.add)\
                    .then_inc(shifted.sem, 1)
                dve.wait_ge(shifted.sem, shifted.done(g))
                dve.wait_ge(loaded.sem(k), loaded.done(i, k))
                nc.vector.scalar_tensor_tensor(u, u, 0.0, flat(x_in[0:rows, k % RING, 0:T, :]), ALU.max, ALU.add)\
                    .then_inc(z_made.sem, 1)
                dve.wait_ge(z_made.sem, z_made.done(g))
                norm.moments(dve, g, k % 2, T, rows, lambda j: z[0:rows, k % 2, j, :])

            def bias(i, k, T, rows):
                norm.make_bias(dve, i * GR + k, k % 2, T, rows)
            dve.wait_ge(ready, 1)
            laps(nc.vector, [(1, join), (0, bias)])


def wait_stores(sp, stored):
    for k in range(RING):
        last = max(g for g in range(GROUPS + 1) if g % RING == k)
        sp.wait_ge(stored.sem(k), stored.done(last // GR, last % GR))


def given_arrays(np, inputs):
    a = {k: np.asarray(v) for k, v in inputs.items()}
    out = {"x": a["x"], "src": a["src"], "dst": a["dst"],
           "src_cols": a["src"][:TILES * P].reshape(TILES, P).T,
           "dst_cols": a["dst"][:TILES * P].reshape(TILES, P).T,
           "edge4_t": a["edge_attr_4"].T, "edge32_t": a["edge_attr_32"].T}
    unit = np.zeros((1, W), np.float32)
    unit[0, D] = 1
    for l in range(2):
        w0, b0 = a["L0_gnn_W0"][l], a["L0_gnn_b0"][l]
        w1, b1 = a["L0_gnn_W1"][l], a["L0_gnn_b1"][l]
        w2, b2 = a["L0_gnn_W2"][l], a["L0_gnn_b2"][l]
        out[f"self_t{l}"] = np.concatenate([np.concatenate([w1, b1[None]]).T, unit])
        out[f"near_t{l}"] = np.concatenate([w0, b0[None]]).T
        out[f"w2_self{l}"] = np.concatenate([w2[:D], b2[None]])
        out[f"w2_near{l}"] = w2[D:]
    wm = a["L2_gnn_W_msg"]
    out["w_src"] = np.concatenate([wm[:D], a["L2_gnn_b_msg"][None]])
    out["w_dst"] = wm[D:2 * D]
    out["w_feat"] = wm[2 * D:]
    out["w_edge4"] = np.concatenate([a["L2_gnn_W_edge"], a["L2_gnn_b_edge"][None]])
    out["qkv"] = np.concatenate([a["L1_gnn_qW"], a["L1_gnn_kW"], a["L1_gnn_vW"]], axis=1)
    out["w_node"] = a["L2_gnn_W_node"]
    out["w_edge32"] = np.concatenate([a["L3_gnn_We"], a["L3_gnn_be"][None]])
    out["w1"] = a["L3_gnn_W1"]
    out["w2"] = np.concatenate([a["L3_gnn_W2"], a["L3_gnn_b2"][None]])
    out["cols"] = np.stack([a["L2_gnn_b_node"], a["L2_gnn_g_node"], a["L2_gnn_beta_node"], a["L2_gnn_g_edge"],
                            a["L2_gnn_beta_edge"], a["L2_gnn_g_msg"], a["L2_gnn_beta_msg"], a["L3_gnn_b1"],
                            a["L3_gnn_gamma"], a["L3_gnn_beta"]], axis=1)
    return {k: np.ascontiguousarray(v) for k, v in out.items()}


def kernel(**inputs):
    import numpy as np
    import concourse.bacc as bacc
    from concourse.bass_utils import run_bass_kernel_spmd as run

    nc = bacc.Bacc("TRN2", target_bir_lowering=False, num_devices=1)
    arrays = given_arrays(np, inputs)
    given = {k: nc.dram_tensor(f"in_{k}", a.shape, mybir.dt.from_np(a.dtype), kind="ExternalInput").ap()
             for k, a in arrays.items()}
    out = nc.dram_tensor("out", (N, D), F32, kind="ExternalOutput").ap()
    gnn(nc, given, out)
    r = run(nc, [{f"in_{k}": a for k, a in arrays.items()}], core_ids=[0])
    return r.results[0]["out"]
```

```python
import concourse.bass as bass
from concourse import mybir
from contextlib import ExitStack

F32 = mybir.dt.float32
I32 = mybir.dt.int32
ALU = mybir.AluOpType
ACT = mybir.ActivationFunctionType
AX = mybir.AxisListType

N = 50000
D = 96
W = D + 1
HEADS = 4
DH = D // HEADS
M = D + HEADS
P = 128
TILES = N // P
TAIL = N - TILES * P
GT = 3
GR = 10
LAPS = TILES // (GT * GR)
GROUPS = LAPS * GR
RING = 5
PAIRS = GROUPS // 2
STEP = 8
SLOTS = TILES + 2
DUMP = N
HALF_TABLE = SLOTS * 5 // 8
EPS = 1e-5
FULL = (GT, P)
LAST = (1, TAIL)


class Phase(ExitStack):

    count = 0

    def __init__(self, nc):
        super().__init__()
        self.nc = nc
        Phase.count += 1
        self.tag = f"p{Phase.count}_"
        self.sems = []

    def sbuf(self, name, shape, dt):
        return self.enter_context(self.nc.sbuf_tensor(self.tag + name, shape, dt))

    def psum(self, name, shape, dt):
        return self.enter_context(self.nc.psum_tensor(self.tag + name, shape, dt))

    def semaphore(self, name):
        self.sems.append(self.nc.alloc_semaphore(self.tag + name))
        return self.sems[-1]

    def __exit__(self, *error):
        super().__exit__(*error)
        if error[0] is None:
            self.nc.clear_and_free_semaphores(self.sems)
            self.nc.all_engine_barrier(sem_only=True)


START = 32


class Count:

    def __init__(self, ctx, nc, name, unit=1):
        self.sem = ctx.semaphore(name)
        self.unit = unit
        nc.sync.sem_inc(self.sem, START * unit)

    def done(self, g):
        return (g + (START + 1)) * self.unit

    def free(self, g, ring):
        return (g + (START + 1 - ring)) * self.unit


class DmaRing:

    def __init__(self, ctx, nc, name, dmas=1, pool=False, ring=RING):
        self.ring = ring
        self.sems = [ctx.semaphore(f"{name}{s}") for s in range(ring)]
        self.inc = 16 * dmas
        self.first = 1 if pool else 2
        if not pool:
            for s in self.sems:
                nc.sync.sem_inc(s, self.inc)

    def sem(self, k):
        return self.sems[k % self.ring]

    def done(self, i, k):
        return (i * (GR // self.ring) + (k // self.ring + self.first)) * self.inc

    def free(self, i, k):
        return (i * (GR // self.ring) + (k // self.ring + 1)) * self.inc


def wait_apart(eng, steady, *waits):
    held = [v if isinstance(v, int) else eng.snap(eng.to_reg(v)) for _, v in waits]
    eng.wait_ge(steady, 1)
    for (sem, _), value in zip(waits, held):
        eng.wait_ge(sem, value)


def laps(eng, stages):
    most = max(max(leads) if isinstance(leads, tuple) else leads for leads, _ in stages)

    def group(g):
        return (g // GR, g % GR, *(LAST if g == GROUPS else FULL)) if 0 <= g <= GROUPS else None

    def beside(g):
        for leads, step in stages:
            if isinstance(leads, tuple):
                groups = [group(g + lead) for lead in leads]
                if any(groups):
                    step(*groups)
            elif group(g + leads):
                step(*group(g + leads))

    for g in range(-most, 0):
        beside(g)
    with eng.Fori(0, LAPS - 1) as i:
        for k in range(GR):
            for leads, step in stages:
                if isinstance(leads, tuple):
                    step(*((i + (k + lead) // GR, (k + lead) % GR, *FULL) for lead in leads))
                else:
                    step(i + (k + leads) // GR, (k + leads) % GR, *FULL)
    for g in range(GROUPS - GR, GROUPS + 1):
        beside(g)


def group_rows(dram, g, T, rows):
    if rows == TAIL:
        return dram[TILES * P:N, :].rearrange("(t p) f -> p t f", t=1)
    return dram[bass.ds(g * (GT * P), GT * P), :].rearrange("(t p) f -> p t f", p=P)


def group_cols(dram, g, rows):
    if rows == TAIL:
        return dram[:, TILES * P:N]
    return dram[:, bass.ds(g * (GT * P), GT * P)]


class Chip:
    pass


def gnn(nc, given, out):
    with ExitStack() as ctx:
        def sb(name, shape, dt=F32):
            return ctx.enter_context(nc.sbuf_tensor(name, shape, dt))

        def dram(name, shape, dt=F32):
            return nc.dram_tensor(name, shape, dt, kind="Internal").ap()

        c = Chip()
        c.iota256 = sb("iota256", [P, 2 * P])
        c.tile_base = sb("tile_base", [P, SLOTS])
        c.ident = sb("ident", [P, P])
        c.ones = sb("ones", [P, P])
        c.eps = sb("eps", [P, 1])
        c.zeros = sb("zeros", [P, GT, M])
        c.dst_f = sb("dst_f", [P, TILES + 1])
        c.steps = sb("steps", [1, (GROUPS + 2) * STEP], I32)
        c.w_src = sb("w_src", [W, D])
        c.w_dst = sb("w_dst", [D, D])
        c.w_feat = sb("w_feat", [D, D])
        c.w_edge4 = sb("w_edge4", [5, D])
        c.w_node = sb("w_node", [D, D])
        c.w_edge32 = sb("w_edge32", [33, D])
        c.w1 = sb("w1", [D, D])
        c.w2 = sb("w2", [W, D])
        c.cols = sb("cols", [D, 10])
        c.stat = sb("stat", [D, GROUPS + 1, 6])
        c.stat_msg = sb("stat_msg", [D, GROUPS + 1, 6])
        c.hop_tab = dram("steps_dram", [(PAIRS + 1), 2 * STEP], I32)
        c.att = [dram(f"att{h}", [P * SLOTS, M]) for h in range(2)]
        x1, x2, x3, x4 = (dram(f"x{l}", [N, D]) for l in range(1, 5))
        x0 = given["x"]
        c.src, c.src_cols, c.dst, c.dst_cols = (given[k] for k in ("src", "src_cols", "dst", "dst_cols"))

        with ExitStack() as early:
            def sb_early(name, shape, dt=F32):
                return early.enter_context(nc.sbuf_tensor(name, shape, dt))

            c.lower = sb_early("lower", [P, P])
            c.src_f = sb_early("src_f", [P, TILES + 1])
            c.to_dump = sb_early("to_dump", [P, TILES + 1])
            c.mix_self = [sb_early(f"mix_self{l}", [W, D]) for l in range(2)]
            c.mix_near = [sb_early(f"mix_near{l}", [W, D]) for l in range(2)]
            c.qkv = sb_early("qkv", [D, 3 * D])
            with nc.sbuf_tensor("node_tab", [P, SLOTS, W], F32) as c.node_tab:
                load_and_index(nc, c, given)
                edge_norm(nc, c, given)
                gather_sum(nc, c, x0, clear=c.att)
                mix_nodes(nc, c, x0, x1, 0, None)
                gather_sum(nc, c, x1)
                mix_nodes(nc, c, x1, x2, 1, x0)
            attention_edges(nc, c, x2)
            attention_nodes(nc, c, x2, x3)
        with nc.sbuf_tensor("node_tab2", [P, SLOTS, W], F32) as c.node_tab:
            clear_table(nc, c)
            message_edges(nc, c, x3, given["edge4_t"])
            message_nodes(nc, c, x3, x4)
            gather_sum(nc, c, x4, given["edge32_t"])
            mlp_nodes(nc, c, x4)
            out_nodes(nc, c, x4, out)


COLS = ["b_node", "g_node", "beta_node", "g_edge", "beta_edge", "g_msg", "beta_msg", "b1", "gamma", "beta"]


def column(c, name):
    k = COLS.index(name)
    return c.cols[:, k:k + 1]


def load_and_index(nc, c, given):
    with Phase(nc) as ctx:
        def sb(name, shape, dt=F32):
            return ctx.sbuf(name, shape, dt)

        def sem(name):
            return ctx.semaphore(name)

        src_i = sb("src_i", [P, TILES + 1], I32)
        dst_i = sb("dst_i", [P, TILES + 1], I32)
        hops = sb("hops", [PAIRS + 1, 2 * GT * P], I32)
        hops_f = sb("hops_f", [PAIRS + 1, 2 * GT, P])
        low = sb("low", [PAIRS + 1, 2 * GT])
        more = sb("more", [PAIRS + 1, 2 * GT])
        anymore = sb("anymore", [PAIRS + 1, 2])
        step_rows = sb("step_rows", [PAIRS + 1, 2, STEP], I32)
        self_t = [sb(f"self_t{l}", [W, W]) for l in range(2)]
        near_t = [sb(f"near_t{l}", [D, W]) for l in range(2)]
        w2_self = [sb(f"w2_self{l}", [W, D]) for l in range(2)]
        w2_near = [sb(f"w2_near{l}", [D, D]) for l in range(2)]
        mix = ctx.psum("mix", [P, 4, 512], F32)
        filled = sem("filled")
        masks = sem("masks")
        idx_loaded = sem("idx_loaded")
        w_loaded = sem("w_loaded")
        step = sem("step")
        steps_out = sem("steps_out")
        steps_in = sem("steps_in")
        mixed = sem("mixed")
        block = ctx.enter_context(nc.Block())
        weights = ([(self_t[l][:], given[f"self_t{l}"]) for l in range(2)]
                   + [(near_t[l][:], given[f"near_t{l}"]) for l in range(2)]
                   + [(w2_self[l][:], given[f"w2_self{l}"]) for l in range(2)]
                   + [(w2_near[l][:], given[f"w2_near{l}"]) for l in range(2)]
                   + [(c.w_src[:], given["w_src"]), (c.w_dst[:], given["w_dst"]), (c.w_feat[:], given["w_feat"]),
                      (c.w_edge4[:], given["w_edge4"]), (c.qkv[:], given["qkv"]), (c.w_node[:], given["w_node"]),
                      (c.w_edge32[:], given["w_edge32"]), (c.w1[:], given["w1"]), (c.w2[:], given["w2"]),
                      (c.cols[:], given["cols"])])
        tail = slice(TILES * P, N)
        src, dst = given["src"], given["dst"]

        @block.sync
        def _(sp):
            sp.wait_ge(filled, 4)
            loads = [(hops[0:PAIRS, :], dst[0:TILES * P].rearrange("(i f) -> i f", i=PAIRS)),
                     (hops[PAIRS:PAIRS + 1, 0:P], dst[N - P:N].rearrange("(o f) -> o f", o=1)),
                     (dst_i[:, 0:TILES], given["dst_cols"]),
                     (dst_i[0:TAIL, TILES:TILES + 1], dst[tail].rearrange("(p o) -> p o", o=1)),
                     (src_i[:, 0:TILES], given["src_cols"]),
                     (src_i[0:TAIL, TILES:TILES + 1], src[tail].rearrange("(p o) -> p o", o=1))]
            for to, frm in loads:
                sp.dma_start(to, frm).then_inc(idx_loaded, 16)
            for to, frm in weights:
                sp.dma_start(to, frm).then_inc(w_loaded, 16)
            sp.wait_ge(step, 12)
            sp.dma_start(c.hop_tab, step_rows[:].rearrange("p a b -> p (a b)")).then_inc(steps_out, 16)
            sp.wait_ge(steps_out, 16)
            sp.dma_start(c.steps[:], c.hop_tab.rearrange("(o i) k -> o (i k)", o=1)).then_inc(steps_in, 16)
            sp.wait_ge(steps_in, 16)

        @block.gpsimd
        def _(pool):
            nc.gpsimd.iota(c.iota256[:], pattern=[[1, 2 * P]], base=0, channel_multiplier=0,
                           allow_small_or_imprecise_dtypes=True)
            nc.gpsimd.iota(c.tile_base[:], pattern=[[P, SLOTS]], base=0, channel_multiplier=0,
                           allow_small_or_imprecise_dtypes=True)
            nc.gpsimd.iota(c.to_dump[:], pattern=[[0, TILES + 1]], base=DUMP, channel_multiplier=1,
                           allow_small_or_imprecise_dtypes=True).then_inc(masks, 1)
            nc.gpsimd.memset(c.ident[:], 0.0).then_inc(masks, 1)
            nc.gpsimd.memset(c.lower[:], 1.0).then_inc(masks, 1)
            pool.wait_ge(masks, 3)
            nc.gpsimd.affine_select(out=c.ident[:], in_=c.ident[:], compare_op=ALU.not_equal, fill=1.0,
                                    base=0, pattern=[[-1, P]], channel_multiplier=1)
            nc.gpsimd.affine_select(out=c.lower[:], in_=c.lower[:], compare_op=ALU.is_gt, fill=0.0,
                                    base=0, pattern=[[-1, P]], channel_multiplier=1)
            nc.gpsimd.memset(flat(c.node_tab[:, HALF_TABLE:SLOTS, :]), 0.0)

        @block.tensor
        def _(pe):
            pe.wait_ge(w_loaded, 16 * len(weights))
            for l in range(2):
                nc.tensor.matmul(mix[0:W, 2 * l, 0:D], self_t[l][:], w2_self[l][:], start=True, stop=True)\
                    .then_inc(mixed, 1)
                nc.tensor.matmul(mix[0:W, 2 * l + 1, 0:D], near_t[l][:], w2_near[l][:], start=True, stop=True)\
                    .then_inc(mixed, 1)

        @block.scalar
        def _(act):
            for l in range(2):
                act.wait_ge(mixed, 2 * l + 2)
                nc.scalar.copy(c.mix_self[l][:], mix[0:W, 2 * l, 0:D])
                nc.scalar.copy(c.mix_near[l][:], mix[0:W, 2 * l + 1, 0:D])

        @block.vector
        def _(dve):
            nc.vector.memset(hops[:], 0).then_inc(filled, 1)
            nc.vector.memset(step_rows[:], 0).then_inc(filled, 1)
            nc.vector.memset(dst_i[:, TILES:TILES + 1], 0).then_inc(filled, 1)
            nc.vector.memset(src_i[:, TILES:TILES + 1], 0).then_inc(filled, 1)
            nc.vector.memset(c.zeros[:], 0.0)
            nc.vector.memset(c.ones[:], 1.0)
            nc.vector.memset(c.eps[:], EPS)
            dve.wait_ge(filled, 4)
            dve.wait_ge(idx_loaded, 16 * 6)
            count = 0

            def then(ins):
                nonlocal count
                count += 1
                ins.then_inc(step, 1)
                dve.wait_ge(step, count)

            then(nc.vector.tensor_copy(c.dst_f[:], dst_i[:]))
            then(nc.vector.tensor_copy(c.src_f[:], src_i[:]))
            dve.wait_ge(masks, 3)
            then(nc.vector.tensor_tensor(c.to_dump[:], c.to_dump[:], c.src_f[:], ALU.subtract))
            then(nc.vector.tensor_scalar(hops[:], hops[:], 7, None, ALU.arith_shift_right))
            then(nc.vector.tensor_copy(hops_f[:].rearrange("p a b -> p (a b)"), hops[:]))
            then(nc.vector.tensor_reduce(low[:], hops_f[:], AX.X, ALU.min))
            then(nc.vector.tensor_reduce(more[:], hops_f[:], AX.X, ALU.max))
            then(nc.vector.tensor_tensor(more[:], more[:], low[:], ALU.subtract))
            then(nc.vector.tensor_scalar(more[:], more[:], -1.0, 0.0, ALU.add, ALU.max))
            then(nc.vector.tensor_reduce(anymore[:], more[:].rearrange("p (a b) -> p a b", a=2), AX.X, ALU.max))
            nc.vector.tensor_copy(step_rows[:, :, 0:GT], low[:].rearrange("p (a b) -> p a b", a=2))
            nc.vector.tensor_copy(step_rows[:, :, 4:4 + GT], more[:].rearrange("p (a b) -> p a b", a=2))\
                .then_inc(step, 1)
            nc.vector.tensor_copy(step_rows[:, :, 3:4], anymore[:].rearrange("p (a b) -> p a b", b=1))\
                .then_inc(step, 1)
            nc.vector.memset(flat(c.node_tab[:, 0:HALF_TABLE, :]), 0.0)


class Norm:

    def __init__(self, ctx, nc, name):
        self.nc = nc
        self.mv = ctx.sbuf(f"{name}_mv", [D, 2], F32)
        self.inv = ctx.sbuf(f"{name}_inv", [D, 1], F32)
        self.root = ctx.sbuf(f"{name}_root", [D, 1], F32)
        self.stepped = ctx.semaphore(f"{name}_stepped")
        self.rooted = ctx.semaphore(f"{name}_rooted")

    def on_vector(self, dve, stat, gamma, beta, terms):
        nc, mv, inv = self.nc, self.mv, self.inv
        nc.vector.bn_aggr(mv[:], stat[:].rearrange("p a b -> p (a b)")).then_inc(self.stepped, 1)
        dve.wait_ge(self.stepped, 1)
        nc.vector.tensor_scalar(inv[:], mv[:, 1:2], EPS, None, ALU.add).then_inc(self.stepped, 1)
        dve.wait_ge(self.stepped, 2)
        nc.vector.reciprocal(inv[:], inv[:]).then_inc(self.stepped, 1)
        dve.wait_ge(self.rooted, 1)
        nc.vector.tensor_tensor(terms[:, 0:1], self.root[:], gamma, ALU.mult).then_inc(self.stepped, 1)
        dve.wait_ge(self.stepped, 4)
        nc.vector.tensor_tensor(terms[:, 1:2], mv[:, 0:1], terms[:, 0:1], ALU.mult).then_inc(self.stepped, 1)
        dve.wait_ge(self.stepped, 5)
        nc.vector.tensor_tensor(terms[:, 1:2], beta, terms[:, 1:2], ALU.subtract).then_inc(self.stepped, 1)
        dve.wait_ge(self.stepped, 6)

    def on_scalar(self, act):
        act.wait_ge(self.stepped, 3)
        self.nc.scalar.activation(self.root[:], self.inv[:], ACT.Sqrt).then_inc(self.rooted, 1)


def flat(ap):
    return ap.rearrange("p a b -> p (a b)")


def record(stat, g):
    return flat(stat[:, bass.ds(g, 1), :])


def edge_norm(nc, c, given):
    with Phase(nc) as ctx:
        def sb(name, shape, dt=F32):
            return ctx.sbuf(name, shape, dt)

        def sem(name):
            return ctx.semaphore(name)

        feats = sb("feats", [5, RING, GT * P])
        h = sb("h", [D, 2, GT * P])
        terms = sb("terms", [D, 2])
        shift_l = sb("shift_l", [D, W])
        h_ps = ctx.psum("h_ps", [P, 2, 512], F32)
        fold_ps = ctx.psum("fold_ps", [P, 512], F32)
        norm = Norm(ctx, nc, "edge")
        feats_in = DmaRing(ctx, nc, "feats_in")
        multiplied = Count(ctx, nc, "multiplied")
        rectified = Count(ctx, nc, "rectified")
        counted = Count(ctx, nc, "counted")
        ones_set = sem("ones_set")
        shift_set = sem("shift_set")
        folded = sem("folded")
        block = ctx.enter_context(nc.Block())

        @block.sync
        def _(sp):
            def load(i, k, T, rows):
                g = i * GR + k
                wait_apart(nc.sync, ones_set, (multiplied.sem, multiplied.free(g, RING)))
                sp.dma_start(feats[0:4, k % RING, 0:T * rows], group_cols(given["edge4_t"], g, rows))\
                    .then_inc(feats_in.sem(k), 16)
            sp.wait_ge(ones_set, 1)
            laps(nc.sync, [(0, load)])

        @block.tensor
        def _(pe):
            def multiply(i, k, T, rows):
                g = i * GR + k
                pe.wait_ge(feats_in.sem(k), feats_in.done(i, k))
                pe.wait_ge(rectified.sem, rectified.free(g, 2))
                nc.tensor.matmul(h_ps[0:D, k % 2, 0:T * rows], c.w_edge4[:], feats[:, k % RING, 0:T * rows],
                                 start=True, stop=True).then_inc(multiplied.sem, 1)
            laps(nc.tensor, [(0, multiply)])
            pe.wait_ge(shift_set, 2)
            nc.tensor.matmul(fold_ps[0:W, 0:D], c.ident[0:W, 0:W], c.w_src[:], start=True, stop=False)
            nc.tensor.matmul(fold_ps[0:W, 0:D], shift_l[:], c.w_feat[:], start=False, stop=True).then_inc(folded, 1)

        @block.scalar
        def _(act):
            def rectify(i, k, T, rows):
                g = i * GR + k
                act.wait_ge(multiplied.sem, multiplied.done(g))
                act.wait_ge(counted.sem, counted.free(g, 2))
                nc.scalar.activation(h[:, k % 2, 0:T * rows], h_ps[0:D, k % 2, 0:T * rows], ACT.Relu)\
                    .then_inc(rectified.sem, 1)
            laps(nc.scalar, [(0, rectify)])
            norm.on_scalar(act)

        @block.vector
        def _(dve):
            nc.vector.memset(feats[:], 1.0).then_inc(ones_set, 1)
            nc.vector.memset(shift_l[:], 0.0).then_inc(shift_set, 1)

            def count(i, k, T, rows):
                g = i * GR + k
                dve.wait_ge(rectified.sem, rectified.done(g))
                nc.vector.bn_stats(record(c.stat, g), h[:, k % 2, 0:T * rows]).then_inc(counted.sem, 1)
            laps(nc.vector, [(0, count)])
            dve.wait_ge(counted.sem, counted.done(GROUPS))
            norm.on_vector(dve, c.stat, column(c, "g_edge"), column(c, "beta_edge"), terms)
            dve.wait_ge(shift_set, 1)
            nc.vector.tensor_copy(shift_l[:, D:W], terms[:, 1:2]).then_inc(shift_set, 1)
            dve.wait_ge(folded, 1)
            nc.vector.tensor_copy(c.w_src[:], fold_ps[0:W, 0:D])
            nc.vector.tensor_scalar(c.w_feat[:], c.w_feat[:], terms[:, 0:1], None, ALU.mult)


def clear_table(nc, c):
    with Phase(nc) as ctx:
        block = ctx.enter_context(nc.Block())

        @block.vector
        def _(dve):
            nc.vector.memset(flat(c.node_tab[:, 0:HALF_TABLE, :]), 0.0)

        @block.gpsimd
        def _(pool):
            nc.gpsimd.memset(flat(c.node_tab[:, HALF_TABLE:SLOTS, :]), 0.0)


class NodeSum:

    def __init__(self, ctx, nc, c, banks):
        self.nc, self.c, self.tag = nc, c, ctx.tag
        self.hot = ctx.sbuf("hot", [P, GT, 2 * P], F32)
        self.far_hot = ctx.sbuf("far_hot", [P, P], F32)
        self.banks = banks
        self.acc = ctx.psum("acc", [P, banks, 512], F32)
        self.far_acc = ctx.psum("far_acc", [P, 512], F32)
        self.hot_made = Count(ctx, nc, "hot_made")
        self.summed = Count(ctx, nc, "summed")
        self.added = Count(ctx, nc, "added")
        self.far_matched = ctx.semaphore("far_matched")
        self.far_summed = ctx.semaphore("far_summed")
        self.far_added = ctx.semaphore("far_added")

    def acc_of(self, k, j):
        return self.acc[:, (GT * k + j) % self.banks, 0:2 * W]

    def on_tensor(self, pe, rows_of, wait_rows):
        nc, c = self.nc, self.c
        far = nc.tensor.alloc_register(self.tag + "far_steps_pe")
        any_far = nc.tensor.alloc_register(self.tag + "any_far_pe")
        more = [nc.tensor.alloc_register(self.tag + f"more_pe{j}") for j in range(4)]
        nc.tensor.reg_mov(far, 0)

        def load_flag(g):
            nc.tensor.reg_load(any_far, c.steps[0:1, bass.ds(g * STEP + 3, 1)])
        load_flag(0)

        def step(i, k, T, rows):
            g = i * GR + k
            some = nc.tensor.snap(any_far, min_val=0, max_val=TILES)
            wait_rows(i, k)
            with nc.tensor.If(some > 0):
                nc.tensor.reg_load(more, c.steps[0:1, bass.ds(g * STEP + 4, 4)])
                for j in range(T):
                    count = nc.tensor.snap(more[j], min_val=0, max_val=TILES)
                    with nc.tensor.If(count > 0):
                        with nc.tensor.Fori(0, count):
                            nc.tensor.reg_add(far, far, 1)
                            now = nc.tensor.snap(far)
                            pe.wait_ge(self.far_matched, now)
                            nc.tensor.matmul(self.far_acc[:, 0:W], self.far_hot[0:rows, :], rows_of(k, j, rows),
                                             start=True, stop=True).then_inc(self.far_summed, 1)
                            pe.wait_ge(self.far_added, now)
            for j in range(T):
                t = g * GT + j
                pe.wait_ge(self.hot_made.sem, self.hot_made.done(t))
                pe.wait_ge(self.added.sem, self.added.free(t, self.banks))
                for h in range(2):
                    last = nc.tensor.matmul(self.acc_of(k, j)[:, h * W:(h + 1) * W],
                                            self.hot[0:rows, j, h * P:(h + 1) * P], rows_of(k, j, rows),
                                            start=True, stop=True)
                last.then_inc(self.summed.sem, 1)
                if j == 1:
                    load_flag(g + 1)
        return step

    def on_vector(self, dve):
        nc, c = self.nc, self.c
        far = nc.vector.alloc_register(self.tag + "far_steps_dve")
        near = [[nc.vector.alloc_register(self.tag + f"near_dve{s}_{j}") for j in range(4)] for s in range(2)]
        more = [nc.vector.alloc_register(self.tag + f"more_dve{j}") for j in range(4)]
        nc.vector.reg_mov(far, 0)
        first = {}

        def match(g, j, rows, base):
            t = g * GT + j
            dve.wait_ge(self.summed.sem, self.summed.free(t, GT))
            nc.vector.tensor_scalar(self.hot[0:rows, j, :], c.iota256[0:rows, :], c.tile_base[0:rows, bass.ds(base, 1)],
                                    c.dst_f[0:rows, bass.ds(t, 1)], ALU.add, ALU.is_equal).then_inc(self.hot_made.sem, 1)

        def add(g, k, j):
            t = g * GT + j
            dve.wait_ge(self.added.sem, self.added.free(t, 1))
            dve.wait_ge(self.summed.sem, self.summed.done(t))
            at = c.node_tab[:, bass.ds(first[j], 2), :]
            nc.vector.tensor_tensor(at, at, self.acc_of(k, j).rearrange("p (a b) -> p a b", a=2),
                                    ALU.add).then_inc(self.added.sem, 1)

        def start(i, k, T, rows):
            g = i * GR + k
            nc.vector.reg_load(near[k % 2], c.steps[0:1, bass.ds(g * STEP, 4)])
            match(g, 0, rows, nc.vector.snap(near[k % 2][0], min_val=0, max_val=TILES))

        def middle(i, k, T, rows):
            g = i * GR + k
            regs = near[k % 2]
            for j in range(T):
                first[j] = nc.vector.snap(regs[j], min_val=0, max_val=TILES)
            with nc.vector.If(nc.vector.snap(regs[3], min_val=0, max_val=TILES) > 0):
                nc.vector.reg_load(more, c.steps[0:1, bass.ds(g * STEP + 4, 4)])
                for j in range(T):
                    count = nc.vector.snap(more[j], min_val=0, max_val=TILES)
                    with nc.vector.If(count > 0):
                        with nc.vector.Fori(0, count) as n:
                            nc.vector.reg_add(far, far, 1)
                            now = nc.vector.snap(far)
                            tile = nc.s_assert_within(first[j] + 2 + n, 2, TILES)
                            t = g * GT + j
                            dve.wait_ge(self.added.sem, self.added.free(g * GT, 1))
                            nc.vector.tensor_scalar(self.far_hot[0:rows, :], c.iota256[0:rows, 0:P],
                                                    c.tile_base[0:rows, bass.ds(tile, 1)],
                                                    c.dst_f[0:rows, bass.ds(t, 1)], ALU.add, ALU.is_equal)\
                                .then_inc(self.far_matched, 1)
                            dve.wait_ge(self.far_summed, now)
                            at = c.node_tab[:, bass.ds(tile, 1), :]
                            nc.vector.tensor_tensor(at, at, self.far_acc[:, 0:W].rearrange("p (a b) -> p a b", a=1),
                                                    ALU.add).then_inc(self.far_added, 1)
                            dve.wait_ge(self.far_added, now)
            for j in range(1, T):
                match(g, j, rows, first[j])
                add(g, k, j - 1)

        def end(i, k, T, rows):
            add(i * GR + k, k, T - 1)
        return start, middle, end


def gather_sum(nc, c, x, edge32_t=None, clear=()):
    with Phase(nc) as ctx:
        def sb(name, shape, dt=F32):
            return ctx.sbuf(name, shape, dt)

        def sem(name):
            return ctx.semaphore(name)

        rows_in = sb("rows_in", [P, RING, GT, W])
        idx = sb("idx", [P, GR, GT], I32)
        idx_in = DmaRing(ctx, nc, "idx_in", ring=GR)
        gathered = DmaRing(ctx, nc, "gathered", GT, pool=True)
        ones_set = sem("ones_set")
        node_sum = NodeSum(ctx, nc, c, GT)
        if edge32_t is not None:
            feats = sb("feats", [33, RING, GT * P])
            msg = sb("msg", [P, 2, GT, W])
            pre_ps = ctx.psum("pre_ps", [P, 2, 512], F32)
            feats_in = DmaRing(ctx, nc, "feats_in")
            pre_made = Count(ctx, nc, "pre_made")
            msg_made = Count(ctx, nc, "msg_made")
        if clear:
            cleared = DmaRing(ctx, nc, "cleared", len(clear))
            dump_cleared = sem("dump_cleared")
        block = ctx.enter_context(nc.Block())

        @block.sync
        def _(sp):
            def load(i, k, T, rows):
                g = i * GR + k
                if edge32_t is not None:
                    wait_apart(nc.sync, ones_set, (pre_made.sem, pre_made.free(g, GR)))
                else:
                    wait_apart(nc.sync, ones_set, (node_sum.summed.sem,
                                                   node_sum.summed.free(g * GT + GT - 1, GT * GR)))
                sp.dma_start(idx[0:rows, k % GR, 0:T], idx_cols(c.src_cols, c.src, g, rows))\
                    .then_inc(idx_in.sem(k), 16)

            def load_feats(i, k, T, rows):
                g = i * GR + k
                wait_apart(nc.sync, ones_set, (pre_made.sem, pre_made.free(g, RING)))
                sp.dma_start(feats[0:32, k % RING, 0:T * rows], group_cols(edge32_t, g, rows))\
                    .then_inc(feats_in.sem(k), 16)
            sp.wait_ge(ones_set, 1)
            laps(nc.sync, [(0, load)] if edge32_t is None else [(3, load), (0, load_feats)])

        @block.gpsimd
        def _(pool):
            used = pre_made if edge32_t is not None else node_sum.summed
            per_group = 1 if edge32_t is not None else GT
            take = PoolTakes(nc, ctx.tag)
            idx_at = take.ring(idx_in.done(0, 0), idx_in)
            used_at = take.counter(used.free(per_group - 1, per_group * RING), per_group)

            def gather(i, k, T, rows):
                take.next_group(k, [used_at])
                idx_value, used_value = take.value(idx_at), take.value(used_at)
                pool.wait_ge(ones_set, 1)
                pool.wait_ge(idx_in.sem(k), idx_value)
                pool.wait_ge(used.sem, used_value)
                for j in range(T):
                    gather_tile(nc, rows_in[0:rows, k % RING, j, 0:D], x, idx[0:rows, k % GR, j:j + 1])\
                        .then_inc(gathered.sem(k), 16 * GT if T == 1 else 16)
            laps(nc.gpsimd, [(0, gather)])

        @block.tensor
        def _(pe):
            pe.wait_ge(ones_set, 1)

            def pre(i, k, T, rows):
                g = i * GR + k
                pe.wait_ge(feats_in.sem(k), feats_in.done(i, k))
                pe.wait_ge(gathered.sem(k), gathered.done(i, k))
                pe.wait_ge(msg_made.sem, msg_made.free(g, 2))
                for j in range(T):
                    to = pre_ps[0:rows, k % 2, j * D:(j + 1) * D]
                    nc.tensor.matmul(to, feats[:, k % RING, j * P:j * P + rows], c.w_edge32[:], start=True, stop=False)
                    last = nc.tensor.matmul(to, c.ident[0:rows, 0:rows], rows_in[0:rows, k % RING, j, 0:D],
                                            start=False, stop=True)
                last.then_inc(pre_made.sem, 1)

            if edge32_t is not None:
                add_up = node_sum.on_tensor(pe, lambda k, j, rows: msg[0:rows, k % 2, j, :],
                                            lambda i, k: pe.wait_ge(msg_made.sem, msg_made.done(i * GR + k)))
            else:
                add_up = node_sum.on_tensor(pe, lambda k, j, rows: rows_in[0:rows, k % RING, j, :],
                                            lambda i, k: pe.wait_ge(gathered.sem(k), gathered.done(i, k)))

            laps(nc.tensor, [(1, pre), (0, add_up)] if edge32_t is not None else [(0, add_up)])

        if clear:
            @block.scalar
            def _(act):
                def zero(i, k, T, rows):
                    g = i * GR + k
                    wait_apart(nc.scalar, ones_set, (node_sum.summed.sem, node_sum.summed.done(g * GT)))
                    for table in clear:
                        nc.scalar.dma_start(group_rows(table, g, T, rows), c.zeros[0:rows, 0:T, :])\
                            .then_inc(cleared.sem(k), 16)
                laps(nc.scalar, [(0, zero)])
                for table in clear:
                    nc.scalar.dma_start(table[N:N + P, :], c.zeros[:, 0, :]).then_inc(dump_cleared, 16)
                wait_stores(act, cleared)
                act.wait_ge(dump_cleared, 16 * len(clear))

        if edge32_t is not None:
            @block.scalar
            def _(act):
                def rectify(i, k, T, rows):
                    g = i * GR + k
                    act.wait_ge(pre_made.sem, pre_made.done(g))
                    act.wait_ge(node_sum.summed.sem, node_sum.summed.free(g * GT + GT - 1, 2 * GT))
                    nc.scalar.activation(msg[0:rows, k % 2, 0:T, 0:D],
                                         pre_ps[0:rows, k % 2, 0:T * D].rearrange("p (a b) -> p a b", a=T),
                                         ACT.Relu).then_inc(msg_made.sem, 1)
                laps(nc.scalar, [(0, rectify)])

        @block.vector
        def _(dve):
            if edge32_t is not None:
                nc.vector.memset(feats[:], 1.0)
                nc.vector.memset(msg[:, :, :, D:W], 1.0)
            nc.vector.memset(rows_in[:, :, :, D:W], 1.0).then_inc(ones_set, 1)
            start, middle, end = node_sum.on_vector(dve)
            laps(nc.vector, [(0, middle), (1, start), (0, end)])


def idx_cols(cols, whole, g, rows):
    if rows == TAIL:
        return whole[TILES * P:N].rearrange("(p o) -> p o", o=1)
    return cols[:, bass.ds(g * GT, GT)]


def gather_tile(nc, to, table, idx):
    return nc.gpsimd.indirect_dma_start(out=to, out_offset=None, in_=table,
                                        in_offset=bass.IndirectOffsetOnAxis(ap=idx, axis=0))


class PoolTakes:

    def __init__(self, nc, tag):
        self.nc, self.tag = nc, tag
        self.rings = []
        self.made = 0

    def counter(self, first, by):
        self.made += 1
        reg = self.nc.gpsimd.alloc_register(f"{self.tag}take{self.made}")
        self.nc.gpsimd.reg_mov(reg, first - by)
        return reg, by

    def ring(self, first, ring):
        self.rings.append((*self.counter(first, ring.inc), ring.ring))
        return self.rings[-1][0:2]

    def next_group(self, k, counters):
        for reg, by in counters + [(reg, by) for reg, by, ring in self.rings if k % ring == 0]:
            self.nc.gpsimd.reg_add(reg, reg, by)

    def value(self, at):
        return self.nc.gpsimd.snap(at[0])


class RowNorm:

    def __init__(self, ctx, nc, c, name, steady, factor=None):
        def sb(what, shape):
            return ctx.sbuf(f"{name}_{what}", shape, F32)
        self.nc, self.c, self.factor, self.steady = nc, c, factor, steady
        self.stat = sb("stat", [P, 2, GT, 6])
        self.mv = sb("mv", [P, 2, GT, 2])
        self.dev = sb("dev", [P, 2, GT])
        self.root = sb("root", [P, 2, GT])
        self.bias = sb("bias", [P, 2, GT])
        self.stat_made = Count(ctx, nc, f"{name}_stat_made")
        self.mv_made = Count(ctx, nc, f"{name}_mv_made")
        self.dev_made = Count(ctx, nc, f"{name}_dev_made")
        self.root_made = Count(ctx, nc, f"{name}_root_made")
        self.bias_made = Count(ctx, nc, f"{name}_bias_made")

    def records(self, g, b, T, rows, tile):
        for j in range(T):
            last = self.nc.vector.bn_stats(self.stat[0:rows, b, j, :], tile(j))
        last.then_inc(self.stat_made.sem, 1)

    def moments(self, g, b, T, rows):
        wait_apart(self.nc.vector, self.steady, (self.stat_made.sem, self.stat_made.done(g)))
        for j in range(T):
            last = self.nc.vector.bn_aggr(self.mv[0:rows, b, j, :], self.stat[0:rows, b, j, :])
        last.then_inc(self.mv_made.sem, 1)

    def deviate(self, act, g, b, T, rows):
        act.wait_ge(self.mv_made.sem, self.mv_made.done(g))
        act.wait_ge(self.root_made.sem, self.root_made.free(g, 2))
        bias, factor = (self.c.eps[0:rows, :], 1.0) if self.factor is None else (0.0, self.factor)
        self.nc.scalar.activation(self.dev[0:rows, b, 0:T], self.mv[0:rows, b, 0:T, 1], ACT.Sqrt, bias=bias,
                                  scale=factor).then_inc(self.dev_made.sem, 1)

    def invert(self, dve, g, b, T, rows):
        dve.wait_ge(self.dev_made.sem, self.dev_made.done(g))
        self.nc.vector.reciprocal(self.root[0:rows, b, 0:T], self.dev[0:rows, b, 0:T]).then_inc(self.root_made.sem, 1)

    def make_bias(self, dve, g, b, T, rows):
        if self.factor is None:
            dve.wait_ge(self.root_made.sem, self.root_made.done(g))
            self.nc.vector.scalar_tensor_tensor(self.bias[0:rows, b, 0:T], self.mv[0:rows, b, 0:T, 0], -1.0,
                                                self.root[0:rows, b, 0:T], ALU.mult, ALU.mult)\
                .then_inc(self.bias_made.sem, 1)

    def apply(self, act, g, b, T, rows, tile, to):
        biased = self.factor is None
        if biased:
            act.wait_ge(self.bias_made.sem, self.bias_made.done(g))
        else:
            act.wait_ge(self.root_made.sem, self.root_made.done(g))
        for j in range(T):
            bias = self.bias[0:rows, b, j:j + 1] if biased else 0.0
            last = self.nc.scalar.activation(to(j), tile(j), ACT.Identity if biased else ACT.Copy, bias=bias,
                                             scale=self.root[0:rows, b, j:j + 1])
        return last


def measure_rows(*parts):
    for norm, g, b, T, rows, tile in parts:
        norm.records(g, b, T, rows, tile)
    for norm, g, b, T, rows, _ in parts:
        norm.moments(g, b, T, rows)


def finish_rows(dve, *parts):
    for norm, g, b, T, rows in parts:
        norm.invert(dve, g, b, T, rows)
    for norm, g, b, T, rows in parts:
        norm.make_bias(dve, g, b, T, rows)


def take_sums(nc, c, steady, taken, used, sums, g, k, T):
    wait_apart(nc.gpsimd, steady, (used.sem, used.free(g, 2)))
    tiles = GT if T == GT else 2
    at = c.node_tab[:, bass.ds(g * GT, tiles), :]
    nc.gpsimd.tensor_copy(sums[:, k % 2, 0:tiles, :], at).then_inc(taken.sem, 1)
    wait_apart(nc.gpsimd, steady, (taken.sem, taken.done(g)))
    nc.gpsimd.tensor_copy(at, c.zeros[:, 0:tiles, 0:W])


def transposed(nc, to, T, rows, cols, tile, ident):
    for j in range(T):
        last = nc.tensor.transpose(to[0:cols, j * P:j * P + rows], tile(j), ident[0:rows, 0:rows])
    return last


def mix_nodes(nc, c, x, x_out, layer, first):
    with Phase(nc) as ctx:
        def sb(name, shape, dt=F32):
            return ctx.sbuf(name, shape, dt)

        x_in = sb("x_in", [P, RING, GT, W])
        sums = sb("sums", [P, 2, GT, W])
        x_t = sb("x_t", [W, 2, GT * P])
        s_t = sb("s_t", [W, 2, GT * P])
        res = sb("res", [P, RING, GT, D])
        x_t_ps = ctx.psum("x_t_ps", [P, 2, 512], F32)
        s_t_ps = ctx.psum("s_t_ps", [P, 2, 512], F32)
        y_ps = ctx.psum("y_ps", [P, 2, 512], F32)
        ones_set = ctx.semaphore("ones_set")
        loaded = DmaRing(ctx, nc, "loaded")
        stored = DmaRing(ctx, nc, "stored")
        taken = Count(ctx, nc, "taken")
        x_turned = Count(ctx, nc, "x_turned")
        s_turned = Count(ctx, nc, "s_turned")
        x_copied = Count(ctx, nc, "x_copied")
        s_copied = Count(ctx, nc, "s_copied")
        mixed = Count(ctx, nc, "mixed")
        res_made = Count(ctx, nc, "res_made")
        spread = RowNorm(ctx, nc, c, "spread", ones_set, factor=D / (D - 1))
        if first is not None:
            first_in = sb("first_in", [P, RING, GT, D])
            z = sb("z", [P, 2, GT, D])
            first_loaded = DmaRing(ctx, nc, "first_loaded")
            z_made = Count(ctx, nc, "z_made")
            norm = RowNorm(ctx, nc, c, "norm", ones_set)
        block = ctx.enter_context(nc.Block())

        @block.sync
        def _(sp):
            def load(i, k, T, rows):
                g = i * GR + k
                wait_apart(nc.sync, ones_set, (x_turned.sem, x_turned.free(g, RING)))
                sp.dma_start(x_in[0:rows, k % RING, 0:T, 0:D], group_rows(x, g, T, rows)).then_inc(loaded.sem(k), 16)
                if first is not None:
                    wait_apart(nc.sync, ones_set, (z_made.sem, z_made.free(g, RING)))
                    sp.dma_start(first_in[0:rows, k % RING, 0:T, :], group_rows(first, g, T, rows))\
                        .then_inc(first_loaded.sem(k), 16)
            sp.wait_ge(ones_set, 1)
            laps(nc.sync, [(0, load)])
            wait_stores(sp, stored)

        @block.gpsimd
        def _(pool):
            def take(i, k, T, rows):
                take_sums(nc, c, ones_set, taken, s_turned, sums, i * GR + k, k, T)
            laps(nc.gpsimd, [(0, take)])

        @block.tensor
        def _(pe):
            def turn(i, k, T, rows):
                g = i * GR + k
                pe.wait_ge(loaded.sem(k), loaded.done(i, k))
                pe.wait_ge(x_copied.sem, x_copied.free(g, 2))
                transposed(nc, x_t_ps[:, k % 2, :], T, rows, W, lambda j: x_in[0:rows, k % RING, j, :], c.ident)\
                    .then_inc(x_turned.sem, 1)
                pe.wait_ge(taken.sem, taken.done(g))
                pe.wait_ge(s_copied.sem, s_copied.free(g, 2))
                transposed(nc, s_t_ps[:, k % 2, :], T, rows, W, lambda j: sums[0:rows, k % 2, j, :], c.ident)\
                    .then_inc(s_turned.sem, 1)

            def mix(i, k, T, rows):
                g = i * GR + k
                pe.wait_ge(x_copied.sem, x_copied.done(g))
                pe.wait_ge(s_copied.sem, s_copied.done(g))
                used = res_made if first is None else z_made
                pe.wait_ge(used.sem, used.free(g, 2))
                for j in range(T):
                    to = y_ps[0:rows, k % 2, j * D:(j + 1) * D]
                    nc.tensor.matmul(to, x_t[:, k % 2, j * P:j * P + rows], c.mix_self[layer][:], start=True, stop=False)
                    last = nc.tensor.matmul(to, s_t[:, k % 2, j * P:j * P + rows], c.mix_near[layer][:],
                                            start=False, stop=True)
                last.then_inc(mixed.sem, 1)
            pe.wait_ge(ones_set, 1)
            laps(nc.tensor, [(1, turn), (0, mix)])

        @block.scalar
        def _(act):
            def copy_x(i, k, T, rows):
                g = i * GR + k
                act.wait_ge(x_turned.sem, x_turned.done(g))
                act.wait_ge(mixed.sem, mixed.free(g, 2))
                nc.scalar.copy(x_t[:, k % 2, 0:(T - 1) * P + rows], x_t_ps[0:W, k % 2, 0:(T - 1) * P + rows])\
                    .then_inc(x_copied.sem, 1)

            def scale(i, k, T, rows):
                g = i * GR + k
                act.wait_ge(stored.sem(k), stored.free(i, k))
                spread.apply(act, g, k % 2, T, rows, lambda j: y_ps[0:rows, k % 2, j * D:(j + 1) * D],
                             lambda j: res[0:rows, k % RING, j, :]).then_inc(res_made.sem, 1)

            def normalise(i, k, T, rows):
                g = i * GR + k
                act.wait_ge(stored.sem(k), stored.free(i, k))
                norm.apply(act, g, k % 2, T, rows, lambda j: z[0:rows, k % 2, j, :],
                           lambda j: res[0:rows, k % RING, j, :]).then_inc(res_made.sem, 1)

            def store(i, k, T, rows):
                g = i * GR + k
                act.wait_ge(res_made.sem, res_made.done(g))
                nc.scalar.dma_start(group_rows(x_out, g, T, rows), res[0:rows, k % RING, 0:T, :])\
                    .then_inc(stored.sem(k), 16)

            def deviate_y(i, k, T, rows):
                spread.deviate(act, i * GR + k, k % 2, T, rows)

            def deviate_z(i, k, T, rows):
                norm.deviate(act, i * GR + k, k % 2, T, rows)

            if first is None:
                laps(nc.scalar, [(0, scale), (1, deviate_y), (3, copy_x), (0, store)])
            else:
                laps(nc.scalar, [(0, normalise), (2, deviate_y), (1, deviate_z), (4, copy_x), (0, store)])

        @block.vector
        def _(dve):
            def copy_s(i, k, T, rows):
                g = i * GR + k
                dve.wait_ge(s_turned.sem, s_turned.done(g))
                dve.wait_ge(mixed.sem, mixed.free(g, 2))
                nc.vector.tensor_copy(s_t[:, k % 2, 0:(T - 1) * P + rows], s_t_ps[0:W, k % 2, 0:(T - 1) * P + rows])\
                    .then_inc(s_copied.sem, 1)

            def y_part(i, k, T, rows):
                g = i * GR + k
                dve.wait_ge(mixed.sem, mixed.done(g))
                return spread, g, k % 2, T, rows, lambda j: y_ps[0:rows, k % 2, j * D:(j + 1) * D]

            def z_part(i, k, T, rows):
                g = i * GR + k
                dve.wait_ge(z_made.sem, z_made.done(g))
                return norm, g, k % 2, T, rows, lambda j: z[0:rows, k % 2, j, :]

            def measure(i, k, T, rows):
                measure_rows(y_part(i, k, T, rows))

            def join(i, k, T, rows):
                g = i * GR + k
                dve.wait_ge(spread.root_made.sem, spread.root_made.done(g))
                dve.wait_ge(first_loaded.sem(k), first_loaded.done(i, k))
                dve.wait_ge(res_made.sem, res_made.free(g, 2))
                for j in range(T):
                    last = nc.vector.scalar_tensor_tensor(z[0:rows, k % 2, j, :], y_ps[0:rows, k % 2, j * D:(j + 1) * D],
                                                          spread.root[0:rows, k % 2, j:j + 1],
                                                          first_in[0:rows, k % RING, j, :], ALU.mult, ALU.add)
                last.then_inc(z_made.sem, 1)

            def measure_both(of_y, of_z):
                measure_rows(*([y_part(*of_y)] if of_y else []), *([z_part(*of_z)] if of_z else []))

            def finish_y(i, k, T, rows):
                g = i * GR + k
                dve.wait_ge(res_made.sem, res_made.free(g, 2))
                finish_rows(dve, (spread, g, k % 2, T, rows))

            def finish_both(of_y, of_z):
                parts = [(norm_of, of[0] * GR + of[1], of[1] % 2, *of[2:])
                         for norm_of, of in ((spread, of_y), (norm, of_z)) if of]
                finish_rows(dve, *parts)
            nc.vector.memset(x_in[:, :, :, D:W], 1.0).then_inc(ones_set, 1)
            if first is None:
                laps(nc.vector, [(0, finish_y), (1, measure), (3, copy_s)])
            else:
                laps(nc.vector, [((1, 0), finish_both), (1, join), ((2, 1), measure_both), (4, copy_s)])


def attention_edges(nc, c, x):
    with Phase(nc) as ctx:
        def sb(name, shape, dt=F32):
            return ctx.sbuf(name, shape, dt)

        def ps(name):
            return ctx.psum(name, [P, 512], F32)

        idx = sb("idx", [P, GR, 2, GT], I32)
        sources = sb("sources", [P, RING, GT * P], I32)
        rows_s = sb("rows_s", [P, RING, GT, D])
        rows_d = sb("rows_d", [P, RING, GT, D])
        s_t = sb("s_t", [D, 2, GT * P])
        d_t = sb("d_t", [D, 2, GT * P])
        q = sb("q", [P, GT, D])
        qk = sb("qk", [P, GT, D])
        score = sb("score", [P, GT * HEADS])
        weight = sb("weight", [P, 2, GT * HEADS])
        pay = sb("pay", [P, 2, GT, M])
        same = sb("same", [P, RING, GT, P])
        before = sb("before", [P, GT, P])
        repeats = sb("repeats", [P, RING, GT])
        target_f = sb("target_f", [P, RING, GT])
        target = sb("target", [P, RING, GT], I32)
        total = sb("total", [P, RING, GT, M])
        dump_rows = sb("dump_rows", [P, 1], I32)
        s_t_ps, d_t_ps, q_ps, k_ps, v_ps, total_ps = (ps(n) for n in ("s_t_ps", "d_t_ps", "q_ps", "k_ps", "v_ps", "total_ps"))
        ready = ctx.semaphore("ready")
        idx_in = DmaRing(ctx, nc, "idx_in", 2, ring=GR)
        sources_in = DmaRing(ctx, nc, "sources_in")
        gathered = DmaRing(ctx, nc, "gathered", 2 * GT, pool=True)
        scattered = [ctx.semaphore(f"scattered{h}") for h in range(2)]
        dump_set = ctx.semaphore("dump_set")
        landed = Count(ctx, nc, "landed")
        turned = Count(ctx, nc, "turned")
        s_copied = Count(ctx, nc, "s_copied")
        d_copied = Count(ctx, nc, "d_copied")
        projected = Count(ctx, nc, "projected")
        q_copied = Count(ctx, nc, "q_copied")
        qk_made = Count(ctx, nc, "qk_made")
        scored = Count(ctx, nc, "scored")
        clipped = Count(ctx, nc, "clipped")
        weighed = Count(ctx, nc, "weighed")
        paid = Count(ctx, nc, "paid")
        matched = Count(ctx, nc, "matched")
        counted = Count(ctx, nc, "counted")
        aimed_f = Count(ctx, nc, "aimed_f")
        aimed = Count(ctx, nc, "aimed")
        totalled = Count(ctx, nc, "totalled")
        total_copied = Count(ctx, nc, "total_copied")
        block = ctx.enter_context(nc.Block())

        @block.sync
        def _(sp):
            def load(i, k, T, rows):
                g = i * GR + k
                wait_apart(nc.sync, ready, (turned.sem, turned.free(g, GR)))
                sp.dma_start(idx[0:rows, k % GR, 0, 0:T], idx_cols(c.src_cols, c.src, g, rows))\
                    .then_inc(idx_in.sem(k), 16)
                sp.dma_start(idx[0:rows, k % GR, 1, 0:T], idx_cols(c.dst_cols, c.dst, g, rows))\
                    .then_inc(idx_in.sem(k), 16)

            def load_sources(i, k, T, rows):
                g = i * GR + k
                wait_apart(nc.sync, ready, (matched.sem, matched.free(g, RING)))
                n = T * rows
                row = (c.src[TILES * P:N] if rows == TAIL else c.src[bass.ds(g * (GT * P), GT * P)])
                sp.dma_start(sources[0:rows, k % RING, 0:n], row.rearrange("(o f) -> o f", o=1).to_broadcast([rows, n]))\
                    .then_inc(sources_in.sem(k), 16)
            sp.wait_ge(ready, 1)
            laps(nc.sync, [(3, load), (0, load_sources)])

        @block.gpsimd
        def _(pool):
            take = PoolTakes(nc, ctx.tag)
            idx_at = take.ring(idx_in.done(0, 0), idx_in)
            turned_at = take.counter(turned.free(0, RING), 1)
            total_at = take.counter(total_copied.done(0), 1)
            added = [nc.gpsimd.alloc_register(f"added{h}") for h in range(2)]
            nc.gpsimd.iota(dump_rows[:], pattern=[[0, 1]], base=DUMP, channel_multiplier=1).then_inc(dump_set, 1)
            pool.wait_ge(dump_set, 1)
            for h in range(2):
                nc.gpsimd.indirect_dma_start(
                    out=c.att[h], out_offset=bass.IndirectOffsetOnAxis(ap=dump_rows[:], axis=0),
                    in_=flat(c.zeros[:])[:, 0:M], in_offset=None, compute_op=ALU.add).then_inc(scattered[h], 16)
                nc.gpsimd.reg_mov(added[h], 16)

            def gather(side, j, k, T, rows):
                to = (rows_s, rows_d)[side]
                gather_tile(nc, to[0:rows, k % RING, j, :], x, idx[0:rows, k % GR, side, j:j + 1])\
                    .then_inc(gathered.sem(k), 16 * GT if T == 1 else 16)

            def scatter(j, k, T, rows, total_value):
                h = (GT * k + j) % 2
                added_value = nc.gpsimd.snap(added[h])
                pool.wait_ge(ready, 1)
                pool.wait_ge(scattered[h], added_value)
                if j == 0:
                    pool.wait_ge(total_copied.sem, total_value)
                nc.gpsimd.sem_inc(landed.sem, 1)
                nc.gpsimd.indirect_dma_start(
                    out=c.att[h], out_offset=bass.IndirectOffsetOnAxis(ap=target[0:rows, k % RING, j:j + 1], axis=0),
                    in_=total[0:rows, k % RING, j, :], in_offset=None, compute_op=ALU.add).then_inc(scattered[h], 16)
                nc.gpsimd.reg_add(added[h], added[h], 16)

            def move(of_gather, of_scatter):
                if of_gather:
                    _, k, T, rows = of_gather
                    take.next_group(k, [turned_at])
                    idx_value, turned_value = take.value(idx_at), take.value(turned_at)
                    pool.wait_ge(ready, 1)
                    pool.wait_ge(idx_in.sem(k), idx_value)
                    pool.wait_ge(turned.sem, turned_value)
                    for side in range(2):
                        gather(side, 0, k, T, rows)
                if of_scatter:
                    take.next_group(1, [total_at])
                    total_value = take.value(total_at)
                for j in range(GT):
                    if of_scatter and j < of_scatter[2]:
                        scatter(j, *of_scatter[1:], total_value)
                    if of_gather and 0 < j + 1 < of_gather[2]:
                        for side in range(2):
                            gather(side, j + 1, *of_gather[1:])
            laps(nc.gpsimd, [((4, 0), move)])
            for h in range(2):
                pool.wait_ge(scattered[h], 16 * (1 + (TILES + 2 - h) // 2))

        @block.tensor
        def _(pe):
            def turn(i, k, T, rows):
                g = i * GR + k
                pe.wait_ge(gathered.sem(k), gathered.done(i, k))
                pe.wait_ge(s_copied.sem, s_copied.free(g, 1))
                transposed(nc, s_t_ps, T, rows, D, lambda j: rows_s[0:rows, k % RING, j, :], c.ident)
                pe.wait_ge(d_copied.sem, d_copied.free(g, 1))
                transposed(nc, d_t_ps, T, rows, D, lambda j: rows_d[0:rows, k % RING, j, :], c.ident)\
                    .then_inc(turned.sem, 1)

            def project(i, k, T, rows):
                g = i * GR + k
                pe.wait_ge(s_copied.sem, s_copied.done(g))
                pe.wait_ge(d_copied.sem, d_copied.done(g))
                pe.wait_ge(paid.sem, paid.free(g, 1))
                for j in range(T):
                    for n, (to, side) in enumerate(((q_ps, s_t), (k_ps, d_t), (v_ps, d_t))):
                        last = nc.tensor.matmul(to[0:rows, j * D:(j + 1) * D], side[:, k % 2, j * P:j * P + rows],
                                                c.qkv[:, n * D:(n + 1) * D], start=True, stop=True)
                last.then_inc(projected.sem, 1)

            def sum_up(i, k, T, rows):
                g = i * GR + k
                pe.wait_ge(paid.sem, paid.done(g))
                pe.wait_ge(total_copied.sem, total_copied.free(g, 1))
                for j in range(T):
                    last = nc.tensor.matmul(total_ps[0:rows, j * M:(j + 1) * M], same[0:rows, k % RING, j, 0:rows],
                                            pay[0:rows, k % 2, j, :], start=True, stop=True)
                last.then_inc(totalled.sem, 1)
            pe.wait_ge(ready, 1)
            laps(nc.tensor, [(2, turn), (1, project), (0, sum_up)])

        @block.scalar
        def _(act):
            def copy_s(i, k, T, rows):
                g = i * GR + k
                act.wait_ge(turned.sem, turned.done(g))
                act.wait_ge(projected.sem, projected.free(g, 2))
                n = (T - 1) * P + rows
                nc.scalar.copy(s_t[:, k % 2, 0:n], s_t_ps[0:D, 0:n]).then_inc(s_copied.sem, 1)

            def copy_q(i, k, T, rows):
                g = i * GR + k
                act.wait_ge(projected.sem, projected.done(g))
                act.wait_ge(qk_made.sem, qk_made.free(g, 1))
                nc.scalar.copy(flat(q[0:rows, 0:T, :]), q_ps[0:rows, 0:T * D]).then_inc(q_copied.sem, 1)

            def weigh(i, k, T, rows):
                g = i * GR + k
                act.wait_ge(clipped.sem, clipped.done(g))
                act.wait_ge(paid.sem, paid.free(g, 2))
                nc.scalar.activation(weight[0:rows, k % 2, 0:T * HEADS], score[0:rows, 0:T * HEADS], ACT.Exp)\
                    .then_inc(weighed.sem, 1)

            def copy_total(i, k, T, rows):
                g = i * GR + k
                act.wait_ge(totalled.sem, totalled.done(g))
                act.wait_ge(aimed.sem, aimed.done(g))
                act.wait_ge(landed.sem, landed.free(g * GT, GT * (RING - 1) - 1))
                nc.scalar.copy(flat(total[0:rows, k % RING, 0:T, :]), total_ps[0:rows, 0:T * M]).then_inc(total_copied.sem, 1)

            laps(nc.scalar, [(2, copy_s), (1, copy_q), (1, weigh), (0, copy_total)])

        @block.vector
        def _(dve):
            def match(i, k, T, rows):
                g = i * GR + k
                dve.wait_ge(sources_in.sem(k), sources_in.done(i, k))
                dve.wait_ge(totalled.sem, totalled.free(g, RING))
                for j in range(T):
                    last = nc.vector.tensor_scalar(same[0:rows, k % RING, j, 0:rows],
                                                   sources[0:rows, k % RING, j * P:j * P + rows],
                                                   c.src_f[0:rows, bass.ds(g * GT + j, 1)], None, ALU.is_equal)
                last.then_inc(matched.sem, 1)
                dve.wait_ge(matched.sem, matched.done(g))
                dve.wait_ge(total_copied.sem, total_copied.free(g, RING))
                for j in range(T):
                    last = nc.vector.scalar_tensor_tensor(before[0:rows, j, 0:rows], same[0:rows, k % RING, j, 0:rows], 1.0,
                                                          c.lower[0:rows, 0:rows], ALU.mult, ALU.mult,
                                                          accum_out=repeats[0:rows, k % RING, j:j + 1])
                last.then_inc(counted.sem, 1)
                dve.wait_ge(counted.sem, counted.done(g))
                nc.vector.scalar_tensor_tensor(target_f[0:rows, k % RING, 0:T], repeats[0:rows, k % RING, 0:T], 0.0,
                                               c.to_dump[0:rows, bass.ds(g * GT, T)], ALU.is_gt, ALU.mult)\
                    .then_inc(aimed_f.sem, 1)
                dve.wait_ge(aimed_f.sem, aimed_f.done(g))
                dve.wait_ge(landed.sem, landed.free(g * GT, GT * (RING - 1) - 1))
                nc.vector.tensor_tensor(target[0:rows, k % RING, 0:T], target_f[0:rows, k % RING, 0:T],
                                        c.src_f[0:rows, bass.ds(g * GT, T)], ALU.add).then_inc(aimed.sem, 1)

            def copy_d(i, k, T, rows):
                g = i * GR + k
                dve.wait_ge(turned.sem, turned.done(g))
                dve.wait_ge(projected.sem, projected.free(g, 2))
                n = (T - 1) * P + rows
                nc.vector.tensor_copy(d_t[:, k % 2, 0:n], d_t_ps[0:D, 0:n]).then_inc(d_copied.sem, 1)

            def score_edges(i, k, T, rows):
                g = i * GR + k
                dve.wait_ge(q_copied.sem, q_copied.done(g))
                dve.wait_ge(scored.sem, scored.free(g, 1))
                nc.vector.tensor_tensor(flat(qk[0:rows, 0:T, :]), flat(q[0:rows, 0:T, :]), k_ps[0:rows, 0:T * D],
                                        ALU.mult).then_inc(qk_made.sem, 1)
                dve.wait_ge(qk_made.sem, qk_made.done(g))
                dve.wait_ge(weighed.sem, weighed.free(g, 1))
                nc.vector.tensor_reduce(score[0:rows, 0:T * HEADS],
                                        flat(qk[0:rows, 0:T, :]).rearrange("p (h f) -> p h f", f=DH), AX.X, ALU.add)\
                    .then_inc(scored.sem, 1)
                dve.wait_ge(scored.sem, scored.done(g))
                nc.vector.tensor_scalar(score[0:rows, 0:T * HEADS], score[0:rows, 0:T * HEADS], -10.0, 10.0,
                                        ALU.max, ALU.min).then_inc(clipped.sem, 1)

            def pay_edges(i, k, T, rows):
                g = i * GR + k
                dve.wait_ge(weighed.sem, weighed.done(g))
                dve.wait_ge(totalled.sem, totalled.free(g, 2))
                w = weight[0:rows, k % 2, 0:T * HEADS]
                nc.vector.tensor_copy(pay[0:rows, k % 2, 0:T, D:M], w.rearrange("p (t h) -> p t h", h=HEADS))
                for j in range(T):
                    last = nc.vector.tensor_tensor(
                        pay[0:rows, k % 2, j, 0:D].rearrange("p (h f) -> p h f", f=DH),
                        v_ps[0:rows, j * D:(j + 1) * D].rearrange("p (h f) -> p h f", f=DH),
                        w[:, j * HEADS:(j + 1) * HEADS].rearrange("p (h o) -> p h o", o=1).to_broadcast([rows, HEADS, DH]),
                        ALU.mult)
                last.then_inc(paid.sem, 1)
            nc.vector.memset(before[:], 0.0).then_inc(ready, 1)
            laps(nc.vector, [(2, match), (2, copy_d), (1, score_edges), (1, pay_edges)])


def attention_nodes(nc, c, x, x_out):
    with Phase(nc) as ctx:
        def sb(name, shape, dt=F32):
            return ctx.sbuf(name, shape, dt)

        att_in = sb("att_in", [P, RING, GT, M])
        att_in2 = sb("att_in2", [P, RING, GT, M])
        x_in = sb("x_in", [P, RING, GT, D])
        share = sb("share", [P, 2, GT, HEADS])
        seen = sb("seen", [P, 2, GT, D])
        z = sb("z", [P, 2, GT, D])
        res = sb("res", [P, RING, GT, D])
        x_t = sb("x_t", [D, 2, GT * P])
        f = sb("f", [D, 2, GT * P])
        x_t_ps = ctx.psum("x_t_ps", [P, 2, 512], F32)
        f_ps = ctx.psum("f_ps", [P, 2, 512], F32)
        ready = ctx.semaphore("ready")
        loaded = DmaRing(ctx, nc, "loaded", 3)
        att_whole = Count(ctx, nc, "att_whole")
        stored = DmaRing(ctx, nc, "stored")
        floored = Count(ctx, nc, "floored")
        shared = Count(ctx, nc, "shared")
        seen_made = Count(ctx, nc, "seen_made")
        z_made = Count(ctx, nc, "z_made")
        res_made = Count(ctx, nc, "res_made")
        turned = Count(ctx, nc, "turned")
        copied = Count(ctx, nc, "copied")
        projected = Count(ctx, nc, "projected")
        rectified = Count(ctx, nc, "rectified")
        counted = Count(ctx, nc, "counted")
        norm = RowNorm(ctx, nc, c, "norm", ready)
        block = ctx.enter_context(nc.Block())

        @block.sync
        def _(sp):
            def load(i, k, T, rows):
                g = i * GR + k
                wait_apart(nc.sync, ready, (z_made.sem, z_made.free(g, RING)))
                for h, to in enumerate((att_in, att_in2)):
                    sp.dma_start(to[0:rows, k % RING, 0:T, :], group_rows(c.att[h], g, T, rows)).then_inc(loaded.sem(k), 16)
                sp.dma_start(x_in[0:rows, k % RING, 0:T, :], group_rows(x, g, T, rows)).then_inc(loaded.sem(k), 16)
            sp.wait_ge(ready, 1)
            laps(nc.sync, [(0, load)])
            wait_stores(sp, stored)

        @block.tensor
        def _(pe):
            def turn(i, k, T, rows):
                g = i * GR + k
                pe.wait_ge(res_made.sem, res_made.done(g))
                pe.wait_ge(copied.sem, copied.free(g, 2))
                transposed(nc, x_t_ps[:, k % 2, :], T, rows, D, lambda j: res[0:rows, k % RING, j, :], c.ident)\
                    .then_inc(turned.sem, 1)

            def project(i, k, T, rows):
                g = i * GR + k
                pe.wait_ge(copied.sem, copied.done(g))
                pe.wait_ge(rectified.sem, rectified.free(g, 2))
                nc.tensor.matmul(f_ps[0:D, k % 2, 0:T * rows], c.w_node[:], x_t[:, k % 2, 0:T * rows],
                                 start=True, stop=True).then_inc(projected.sem, 1)
            laps(nc.tensor, [(2, turn), (0, project)])

        @block.scalar
        def _(act):
            def normalise(i, k, T, rows):
                g = i * GR + k
                act.wait_ge(stored.sem(k), stored.free(i, k))
                act.wait_ge(turned.sem, turned.free(g, RING))
                norm.apply(act, g, k % 2, T, rows, lambda j: z[0:rows, k % 2, j, :],
                           lambda j: res[0:rows, k % RING, j, :]).then_inc(res_made.sem, 1)

            def copy_x(i, k, T, rows):
                g = i * GR + k
                act.wait_ge(turned.sem, turned.done(g))
                act.wait_ge(projected.sem, projected.free(g, 2))
                nc.scalar.copy(x_t[:, k % 2, 0:T * rows], x_t_ps[0:D, k % 2, 0:T * rows]).then_inc(copied.sem, 1)

            def rectify(i, k, T, rows):
                g = i * GR + k
                act.wait_ge(projected.sem, projected.done(g))
                act.wait_ge(counted.sem, counted.free(g, 2))
                nc.scalar.activation(f[:, k % 2, 0:T * rows], f_ps[0:D, k % 2, 0:T * rows], ACT.Relu,
                                     bias=column(c, "b_node")).then_inc(rectified.sem, 1)
            def store(i, k, T, rows):
                g = i * GR + k
                act.wait_ge(res_made.sem, res_made.done(g))
                nc.scalar.dma_start(group_rows(x_out, g, T, rows), res[0:rows, k % RING, 0:T, :])\
                    .then_inc(stored.sem(k), 16)

            def deviate(i, k, T, rows):
                norm.deviate(act, i * GR + k, k % 2, T, rows)

            laps(nc.scalar, [(4, normalise), (5, deviate), (2, copy_x), (0, rectify), (4, store)])

        @block.gpsimd
        def _(pool):
            def see(i, k, T, rows):
                g = i * GR + k
                pool.wait_ge(shared.sem, shared.done(g))
                pool.wait_ge(z_made.sem, z_made.free(g, 2))
                for j in range(T):
                    last = nc.gpsimd.tensor_tensor(
                        seen[0:rows, k % 2, j, :].rearrange("p (h f) -> p h f", f=DH),
                        att_in[0:rows, k % RING, j, 0:D].rearrange("p (h f) -> p h f", f=DH),
                        share[0:rows, k % 2, j, :].rearrange("p (h o) -> p h o", o=1).to_broadcast([rows, HEADS, DH]),
                        ALU.mult)
                last.then_inc(seen_made.sem, 1)
            laps(nc.gpsimd, [(0, see)])

        @block.vector
        def _(dve):
            nc.vector.memset(share[:], 0.0).then_inc(ready, 1)

            def add_up(i, k, T, rows):
                g = i * GR + k
                dve.wait_ge(loaded.sem(k), loaded.done(i, k))
                whole = flat(att_in[0:rows, k % RING, 0:T, :])
                nc.vector.tensor_tensor(whole, whole, flat(att_in2[0:rows, k % RING, 0:T, :]), ALU.add)\
                    .then_inc(att_whole.sem, 1)

            def divide(i, k, T, rows):
                g = i * GR + k
                dve.wait_ge(att_whole.sem, att_whole.done(g))
                dve.wait_ge(seen_made.sem, seen_made.free(g, 2))
                at = share[0:rows, k % 2, 0:T, :]
                nc.vector.tensor_scalar(at, att_in[0:rows, k % RING, 0:T, D:M], 1e-8, None, ALU.add)\
                    .then_inc(floored.sem, 1)
                dve.wait_ge(floored.sem, floored.done(g))
                nc.vector.reciprocal(at, at).then_inc(shared.sem, 1)

            def join(i, k, T, rows):
                g = i * GR + k
                dve.wait_ge(seen_made.sem, seen_made.done(g))
                dve.wait_ge(res_made.sem, res_made.free(g, 2))
                nc.vector.scalar_tensor_tensor(flat(z[0:rows, k % 2, 0:T, :]), flat(x_in[0:rows, k % RING, 0:T, :]), 2.0,
                                               flat(seen[0:rows, k % 2, 0:T, :]), ALU.mult, ALU.add)\
                    .then_inc(z_made.sem, 1)
                dve.wait_ge(z_made.sem, z_made.done(g))
                measure_rows((norm, g, k % 2, T, rows, lambda j: z[0:rows, k % 2, j, :]))

            def finish(i, k, T, rows):
                finish_rows(dve, (norm, i * GR + k, k % 2, T, rows))

            def count(i, k, T, rows):
                g = i * GR + k
                dve.wait_ge(rectified.sem, rectified.done(g))
                nc.vector.bn_stats(record(c.stat, g), f[:, k % 2, 0:T * rows]).then_inc(counted.sem, 1)
            laps(nc.vector, [(5, finish), (6, join), (8, divide), (9, add_up), (0, count)])


def message_edges(nc, c, x, edge4_t):
    with Phase(nc) as ctx:
        def sb(name, shape, dt=F32):
            return ctx.sbuf(name, shape, dt)

        idx = sb("idx", [P, GR, 2, GT], I32)
        rows_s = sb("rows_s", [P, RING, GT, D])
        rows_d = sb("rows_d", [P, RING, GT, D])
        feats = sb("feats", [5, RING, GT * P])
        s_t = sb("s_t", [W, 2, GT * P])
        d_t = sb("d_t", [D, 2, GT * P])
        f_t = sb("f_t", [D, 2, GT * P])
        m_t = sb("m_t", [D, 2, GT * P])
        msg = sb("msg", [P, 2, GT, W])
        s_t_ps, d_t_ps, f_t_ps, m_t_ps, msg_ps = (ctx.psum(n, [P, 512], F32)
                                                  for n in ("s_t_ps", "d_t_ps", "f_t_ps", "m_t_ps", "msg_ps"))
        ready = ctx.semaphore("ready")
        idx_in = DmaRing(ctx, nc, "idx_in", 2, ring=GR)
        feats_in = DmaRing(ctx, nc, "feats_in")
        gathered = DmaRing(ctx, nc, "gathered", 2 * GT, pool=True)
        turned = Count(ctx, nc, "turned")
        s_copied = Count(ctx, nc, "s_copied")
        d_copied = Count(ctx, nc, "d_copied")
        f_made = Count(ctx, nc, "f_made")
        multiplied = Count(ctx, nc, "multiplied")
        m_made = Count(ctx, nc, "m_made")
        counted = Count(ctx, nc, "counted")
        turned_back = Count(ctx, nc, "turned_back")
        msg_made = Count(ctx, nc, "msg_made")
        node_sum = NodeSum(ctx, nc, c, 2)
        block = ctx.enter_context(nc.Block())

        @block.sync
        def _(sp):
            def load(i, k, T, rows):
                g = i * GR + k
                wait_apart(nc.sync, ready, (turned.sem, turned.free(g, GR)))
                sp.dma_start(idx[0:rows, k % GR, 0, 0:T], idx_cols(c.src_cols, c.src, g, rows))\
                    .then_inc(idx_in.sem(k), 16)
                sp.dma_start(idx[0:rows, k % GR, 1, 0:T], idx_cols(c.dst_cols, c.dst, g, rows))\
                    .then_inc(idx_in.sem(k), 16)

            def load_feats(i, k, T, rows):
                g = i * GR + k
                wait_apart(nc.sync, ready, (turned.sem, turned.free(g, RING)))
                sp.dma_start(feats[0:4, k % RING, 0:T * rows], group_cols(edge4_t, g, rows)).then_inc(feats_in.sem(k), 16)
            sp.wait_ge(ready, 1)
            laps(nc.sync, [(3, load), (0, load_feats)])

        @block.gpsimd
        def _(pool):
            take = PoolTakes(nc, ctx.tag)
            idx_at = take.ring(idx_in.done(0, 0), idx_in)
            turned_at = take.counter(turned.free(0, RING), 1)

            def gather(i, k, T, rows):
                take.next_group(k, [turned_at])
                idx_value, turned_value = take.value(idx_at), take.value(turned_at)
                pool.wait_ge(ready, 1)
                pool.wait_ge(idx_in.sem(k), idx_value)
                pool.wait_ge(turned.sem, turned_value)
                for side, to in enumerate((rows_s, rows_d)):
                    for j in range(T):
                        gather_tile(nc, to[0:rows, k % RING, j, :], x, idx[0:rows, k % GR, side, j:j + 1])\
                            .then_inc(gathered.sem(k), 16 * GT if T == 1 else 16)
            laps(nc.gpsimd, [(0, gather)])

        @block.tensor
        def _(pe):
            def turn(i, k, T, rows):
                g = i * GR + k
                pe.wait_ge(feats_in.sem(k), feats_in.done(i, k))
                pe.wait_ge(f_made.sem, f_made.free(g, 1))
                nc.tensor.matmul(f_t_ps[0:D, 0:T * rows], c.w_edge4[:], feats[:, k % RING, 0:T * rows],
                                 start=True, stop=True)
                pe.wait_ge(gathered.sem(k), gathered.done(i, k))
                pe.wait_ge(s_copied.sem, s_copied.free(g, 1))
                transposed(nc, s_t_ps, T, rows, D, lambda j: rows_s[0:rows, k % RING, j, :], c.ident)
                pe.wait_ge(d_copied.sem, d_copied.free(g, 1))
                transposed(nc, d_t_ps, T, rows, D, lambda j: rows_d[0:rows, k % RING, j, :], c.ident)\
                    .then_inc(turned.sem, 1)

            def multiply(i, k, T, rows):
                g = i * GR + k
                pe.wait_ge(s_copied.sem, s_copied.done(g))
                pe.wait_ge(d_copied.sem, d_copied.done(g))
                pe.wait_ge(f_made.sem, f_made.done(g))
                pe.wait_ge(m_made.sem, m_made.free(g, 1))
                n = T * rows
                to = m_t_ps[0:D, 0:n]
                nc.tensor.matmul(to, c.w_src[:], s_t[:, k % 2, 0:n], start=True, stop=False)
                nc.tensor.matmul(to, c.w_dst[:], d_t[:, k % 2, 0:n], start=False, stop=False)
                nc.tensor.matmul(to, c.w_feat[:], f_t[:, k % 2, 0:n], start=False, stop=True).then_inc(multiplied.sem, 1)

            def turn_back(i, k, T, rows):
                g = i * GR + k
                pe.wait_ge(m_made.sem, m_made.done(g))
                pe.wait_ge(msg_made.sem, msg_made.free(g, 1))
                for j in range(T):
                    last = nc.tensor.transpose(msg_ps[0:rows, j * D:(j + 1) * D], m_t[:, k % 2, j * P:j * P + rows],
                                               c.ident[0:D, 0:D])
                last.then_inc(turned_back.sem, 1)
            add_up = node_sum.on_tensor(pe, lambda k, j, rows: msg[0:rows, k % 2, j, :],
                                        lambda i, k: pe.wait_ge(msg_made.sem, msg_made.done(i * GR + k)))
            pe.wait_ge(ready, 1)
            laps(nc.tensor, [(3, turn), (2, multiply), (1, turn_back), (0, add_up)])

        @block.scalar
        def _(act):
            def copy_s(i, k, T, rows):
                g = i * GR + k
                act.wait_ge(turned.sem, turned.done(g))
                act.wait_ge(multiplied.sem, multiplied.free(g, 2))
                nc.scalar.copy(s_t[0:D, k % 2, 0:T * rows], s_t_ps[0:D, 0:T * rows]).then_inc(s_copied.sem, 1)
                nc.scalar.activation(f_t[:, k % 2, 0:T * rows], f_t_ps[0:D, 0:T * rows], ACT.Relu).then_inc(f_made.sem, 1)

            def rectify(i, k, T, rows):
                g = i * GR + k
                act.wait_ge(multiplied.sem, multiplied.done(g))
                act.wait_ge(counted.sem, counted.free(g, 2))
                act.wait_ge(turned_back.sem, turned_back.free(g, 2))
                nc.scalar.activation(m_t[:, k % 2, 0:T * rows], m_t_ps[0:D, 0:T * rows], ACT.Relu).then_inc(m_made.sem, 1)

            def copy_back(i, k, T, rows):
                g = i * GR + k
                act.wait_ge(turned_back.sem, turned_back.done(g))
                act.wait_ge(node_sum.summed.sem, node_sum.summed.free(g * GT + GT - 1, 2 * GT))
                nc.scalar.copy(msg[0:rows, k % 2, 0:T, 0:D],
                               msg_ps[0:rows, 0:T * D].rearrange("p (a b) -> p a b", a=T)).then_inc(msg_made.sem, 1)
            laps(nc.scalar, [(3, copy_s), (2, rectify), (1, copy_back)])

        @block.vector
        def _(dve):
            nc.vector.memset(feats[:], 1.0)
            nc.vector.memset(s_t[D:W, :, :], 1.0)
            nc.vector.memset(msg[:, :, :, D:W], 1.0).then_inc(ready, 1)

            def copy_d(i, k, T, rows):
                g = i * GR + k
                dve.wait_ge(turned.sem, turned.done(g))
                dve.wait_ge(multiplied.sem, multiplied.free(g, 2))
                nc.vector.tensor_copy(d_t[:, k % 2, 0:T * rows], d_t_ps[0:D, 0:T * rows]).then_inc(d_copied.sem, 1)

            def count(i, k, T, rows):
                g = i * GR + k
                dve.wait_ge(m_made.sem, m_made.done(g))
                nc.vector.bn_stats(record(c.stat_msg, g), m_t[:, k % 2, 0:T * rows]).then_inc(counted.sem, 1)
            start, middle, end = node_sum.on_vector(dve)
            laps(nc.vector, [(3, copy_d), (2, count), (0, middle), (1, start), (0, end)])


def message_nodes(nc, c, x, x_out):
    with Phase(nc) as ctx:
        def sb(name, shape, dt=F32):
            return ctx.sbuf(name, shape, dt)

        x_in = sb("x_in", [P, RING, GT, W])
        sums = sb("sums", [P, 2, GT, W])
        x_t = sb("x_t", [W, 2, GT * P])
        s_t = sb("s_t", [W, 2, GT * P])
        f_t = sb("f_t", [D, 2, GT * P])
        res = sb("res", [P, RING, GT, D])
        terms_n = sb("terms_n", [D, 2])
        terms_m = sb("terms_m", [D, 2])
        left_x = sb("left_x", [D, W])
        left_m = sb("left_m", [D, W])
        keep_x = sb("keep_x", [W, D])
        scale_m = sb("scale_m", [W, D])
        scale_n = sb("scale_n", [D, D])
        x_t_ps = ctx.psum("x_t_ps", [P, 2, 512], F32)
        s_t_ps = ctx.psum("s_t_ps", [P, 2, 512], F32)
        f_t_ps = ctx.psum("f_t_ps", [P, 512], F32)
        z_ps = ctx.psum("z_ps", [P, 2, 512], F32)
        small_ps = ctx.psum("small_ps", [P, 512], F32)
        ready = ctx.semaphore("ready")
        folding = ctx.semaphore("folding")
        folded = ctx.semaphore("folded")
        constants = ctx.semaphore("constants")
        norm_n = Norm(ctx, nc, "nodes")
        norm_m = Norm(ctx, nc, "messages")
        loaded = DmaRing(ctx, nc, "loaded")
        stored = DmaRing(ctx, nc, "stored")
        taken = Count(ctx, nc, "taken")
        x_turned = Count(ctx, nc, "x_turned")
        s_turned = Count(ctx, nc, "s_turned")
        x_copied = Count(ctx, nc, "x_copied")
        s_copied = Count(ctx, nc, "s_copied")
        projected = Count(ctx, nc, "projected")
        f_made = Count(ctx, nc, "f_made")
        joined = Count(ctx, nc, "joined")
        res_made = Count(ctx, nc, "res_made")
        norm = RowNorm(ctx, nc, c, "norm", ready)
        block = ctx.enter_context(nc.Block())

        @block.sync
        def _(sp):
            def load(i, k, T, rows):
                g = i * GR + k
                wait_apart(nc.sync, ready, (x_turned.sem, x_turned.free(g, RING)))
                sp.dma_start(x_in[0:rows, k % RING, 0:T, 0:D], group_rows(x, g, T, rows)).then_inc(loaded.sem(k), 16)
            sp.wait_ge(ready, 1)
            laps(nc.sync, [(0, load)])
            wait_stores(sp, stored)

        @block.gpsimd
        def _(pool):
            def take(i, k, T, rows):
                take_sums(nc, c, ready, taken, s_turned, sums, i * GR + k, k, T)
            laps(nc.gpsimd, [(0, take)])

        @block.tensor
        def _(pe):
            pe.wait_ge(folding, 2)
            nc.tensor.matmul(small_ps[0:W, 0:D], left_x[:], c.ident[0:D, 0:D], start=True, stop=True)
            nc.tensor.matmul(small_ps[0:W, D:2 * D], left_m[:], c.ident[0:D, 0:D], start=True, stop=True)\
                .then_inc(folded, 1)
            pe.wait_ge(constants, 3)
            pe.wait_ge(ready, 1)

            def turn(i, k, T, rows):
                g = i * GR + k
                pe.wait_ge(loaded.sem(k), loaded.done(i, k))
                pe.wait_ge(x_copied.sem, x_copied.free(g, 2))
                transposed(nc, x_t_ps[:, k % 2, :], T, rows, W, lambda j: x_in[0:rows, k % RING, j, :], c.ident)\
                    .then_inc(x_turned.sem, 1)
                pe.wait_ge(taken.sem, taken.done(g))
                pe.wait_ge(s_copied.sem, s_copied.free(g, 2))
                transposed(nc, s_t_ps[:, k % 2, :], T, rows, W, lambda j: sums[0:rows, k % 2, j, :], c.ident)\
                    .then_inc(s_turned.sem, 1)

            def project(i, k, T, rows):
                g = i * GR + k
                pe.wait_ge(x_copied.sem, x_copied.done(g))
                pe.wait_ge(f_made.sem, f_made.free(g, 1))
                nc.tensor.matmul(f_t_ps[0:D, 0:T * rows], c.w_node[:], x_t[0:D, k % 2, 0:T * rows],
                                 start=True, stop=True).then_inc(projected.sem, 1)

            def join(i, k, T, rows):
                g = i * GR + k
                pe.wait_ge(s_copied.sem, s_copied.done(g))
                pe.wait_ge(f_made.sem, f_made.done(g))
                pe.wait_ge(res_made.sem, res_made.free(g, 2))
                for j in range(T):
                    to = z_ps[0:rows, k % 2, j * D:(j + 1) * D]
                    at = slice(j * P, j * P + rows)
                    nc.tensor.matmul(to, x_t[:, k % 2, at], keep_x[:], start=True, stop=False)
                    nc.tensor.matmul(to, s_t[:, k % 2, at], scale_m[:], start=False, stop=False)
                    last = nc.tensor.matmul(to, f_t[:, k % 2, at], scale_n[:], start=False, stop=True)
                last.then_inc(joined.sem, 1)
            laps(nc.tensor, [(3, turn), (2, project), (1, join)])

        @block.scalar
        def _(act):
            norm_n.on_scalar(act)
            norm_m.on_scalar(act)

            def copy_x(i, k, T, rows):
                g = i * GR + k
                act.wait_ge(x_turned.sem, x_turned.done(g))
                act.wait_ge(joined.sem, joined.free(g, 2))
                nc.scalar.copy(x_t[:, k % 2, 0:T * rows], x_t_ps[0:W, k % 2, 0:T * rows]).then_inc(x_copied.sem, 1)

            def rectify(i, k, T, rows):
                g = i * GR + k
                act.wait_ge(projected.sem, projected.done(g))
                act.wait_ge(joined.sem, joined.free(g, 2))
                nc.scalar.activation(f_t[:, k % 2, 0:T * rows], f_t_ps[0:D, 0:T * rows], ACT.Relu,
                                     bias=column(c, "b_node")).then_inc(f_made.sem, 1)

            def normalise(i, k, T, rows):
                g = i * GR + k
                act.wait_ge(stored.sem(k), stored.free(i, k))
                norm.apply(act, g, k % 2, T, rows, lambda j: z_ps[0:rows, k % 2, j * D:(j + 1) * D],
                           lambda j: res[0:rows, k % RING, j, :]).then_inc(res_made.sem, 1)
            def store(i, k, T, rows):
                g = i * GR + k
                act.wait_ge(res_made.sem, res_made.done(g))
                nc.scalar.dma_start(group_rows(x_out, g, T, rows), res[0:rows, k % RING, 0:T, :])\
                    .then_inc(stored.sem(k), 16)

            def deviate(i, k, T, rows):
                norm.deviate(act, i * GR + k, k % 2, T, rows)

            laps(nc.scalar, [(2, rectify), (0, normalise), (3, copy_x), (1, deviate), (0, store)])

        @block.vector
        def _(dve):
            nc.vector.memset(x_in[:, :, :, D:W], 1.0).then_inc(ready, 1)
            norm_n.on_vector(dve, c.stat, column(c, "g_node"), column(c, "beta_node"), terms_n)
            norm_m.on_vector(dve, c.stat_msg, column(c, "g_msg"), column(c, "beta_msg"), terms_m)
            eye = c.ident[0:D, 0:D]
            nc.vector.tensor_copy(left_x[:, 0:D], eye)
            nc.vector.tensor_copy(left_x[:, D:W], terms_n[:, 1:2]).then_inc(folding, 1)
            nc.vector.tensor_scalar(left_m[:, 0:D], eye, terms_m[:, 0:1], None, ALU.mult)
            nc.vector.tensor_copy(left_m[:, D:W], terms_m[:, 1:2]).then_inc(folding, 1)
            nc.vector.tensor_scalar(scale_n[:], eye, terms_n[:, 0:1], None, ALU.mult).then_inc(constants, 1)
            dve.wait_ge(folded, 1)
            nc.vector.tensor_copy(keep_x[:], small_ps[0:W, 0:D]).then_inc(constants, 1)
            nc.vector.tensor_copy(scale_m[:], small_ps[0:W, D:2 * D]).then_inc(constants, 1)

            def copy_s(i, k, T, rows):
                g = i * GR + k
                dve.wait_ge(s_turned.sem, s_turned.done(g))
                dve.wait_ge(joined.sem, joined.free(g, 2))
                nc.vector.tensor_copy(s_t[:, k % 2, 0:T * rows], s_t_ps[0:W, k % 2, 0:T * rows]).then_inc(s_copied.sem, 1)

            def measure(i, k, T, rows):
                g = i * GR + k
                dve.wait_ge(joined.sem, joined.done(g))
                measure_rows((norm, g, k % 2, T, rows, lambda j: z_ps[0:rows, k % 2, j * D:(j + 1) * D]))

            def finish(i, k, T, rows):
                dve.wait_ge(res_made.sem, res_made.free(i * GR + k, 2))
                finish_rows(dve, (norm, i * GR + k, k % 2, T, rows))
            laps(nc.vector, [(0, finish), (1, measure), (3, copy_s)])


def mlp_nodes(nc, c, x):
    with Phase(nc) as ctx:
        def sb(name, shape, dt=F32):
            return ctx.sbuf(name, shape, dt)

        x_in = sb("x_in", [P, RING, GT, D])
        h = sb("h", [P, 2, GT, D])
        h_t = sb("h_t", [D, 2, GT * P])
        r_t = sb("r_t", [W, 2, GT * P])
        h_t_ps = ctx.psum("h_t_ps", [P, 2, 512], F32)
        r_t_ps = ctx.psum("r_t_ps", [P, 2, 512], F32)
        h2_t_ps = ctx.psum("h2_t_ps", [P, 512], F32)
        h2_ps = ctx.psum("h2_ps", [P, 2, 512], F32)
        ready = ctx.semaphore("ready")
        loaded = DmaRing(ctx, nc, "loaded")
        h_made = Count(ctx, nc, "h_made")
        turned = Count(ctx, nc, "turned")
        copied = Count(ctx, nc, "copied")
        first = Count(ctx, nc, "first")
        rectified = Count(ctx, nc, "rectified")
        second_t = Count(ctx, nc, "second_t")
        second = Count(ctx, nc, "second")
        counted = Count(ctx, nc, "counted")
        kept = Count(ctx, nc, "kept")
        block = ctx.enter_context(nc.Block())

        @block.sync
        def _(sp):
            def load(i, k, T, rows):
                g = i * GR + k
                wait_apart(nc.sync, ready, (h_made.sem, h_made.free(g, RING)))
                sp.dma_start(x_in[0:rows, k % RING, 0:T, :], group_rows(x, g, T, rows)).then_inc(loaded.sem(k), 16)
            sp.wait_ge(ready, 1)
            laps(nc.sync, [(0, load)])

        @block.gpsimd
        def _(pool):
            def join(i, k, T, rows):
                g = i * GR + k
                wait_apart(nc.gpsimd, ready, (loaded.sem(k), loaded.done(i, k)), (turned.sem, turned.free(g, 2)))
                nc.gpsimd.tensor_tensor(h[0:rows, k % 2, 0:T, :], x_in[0:rows, k % RING, 0:T, :],
                                        c.node_tab[0:rows, bass.ds(g * GT, T), 0:D], ALU.add).then_inc(h_made.sem, 1)
            laps(nc.gpsimd, [(0, join)])

        @block.tensor
        def _(pe):
            def turn(i, k, T, rows):
                g = i * GR + k
                pe.wait_ge(h_made.sem, h_made.done(g))
                pe.wait_ge(copied.sem, copied.free(g, 2))
                transposed(nc, h_t_ps[:, k % 2, :], T, rows, D, lambda j: h[0:rows, k % 2, j, :], c.ident)\
                    .then_inc(turned.sem, 1)

            def one(i, k, T, rows):
                g = i * GR + k
                pe.wait_ge(copied.sem, copied.done(g))
                pe.wait_ge(rectified.sem, rectified.free(g, 2))
                nc.tensor.matmul(r_t_ps[0:D, k % 2, 0:T * rows], c.w1[:], h_t[:, k % 2, 0:T * rows],
                                 start=True, stop=True).then_inc(first.sem, 1)

            def two(i, k, T, rows):
                g = i * GR + k
                pe.wait_ge(rectified.sem, rectified.done(g))
                pe.wait_ge(counted.sem, counted.free(g, 1))
                nc.tensor.matmul(h2_t_ps[0:D, 0:T * rows], c.w2[:], r_t[:, k % 2, 0:T * rows],
                                 start=True, stop=True).then_inc(second_t.sem, 1)
                pe.wait_ge(kept.sem, kept.free(g, 2))
                for j in range(T):
                    last = nc.tensor.matmul(h2_ps[0:rows, k % 2, j * D:(j + 1) * D], r_t[:, k % 2, j * P:j * P + rows],
                                            c.w2[:], start=True, stop=True)
                last.then_inc(second.sem, 1)
            pe.wait_ge(ready, 1)
            laps(nc.tensor, [(2, turn), (1, one), (0, two)])

        @block.scalar
        def _(act):
            def copy_h(i, k, T, rows):
                g = i * GR + k
                act.wait_ge(turned.sem, turned.done(g))
                act.wait_ge(first.sem, first.free(g, 2))
                nc.scalar.copy(h_t[:, k % 2, 0:T * rows], h_t_ps[0:D, k % 2, 0:T * rows]).then_inc(copied.sem, 1)

            def rectify(i, k, T, rows):
                g = i * GR + k
                act.wait_ge(first.sem, first.done(g))
                act.wait_ge(second.sem, second.free(g, 2))
                nc.scalar.activation(r_t[0:D, k % 2, 0:T * rows], r_t_ps[0:D, k % 2, 0:T * rows], ACT.Relu,
                                     bias=column(c, "b1")).then_inc(rectified.sem, 1)
            laps(nc.scalar, [(1, copy_h), (0, rectify)])

        @block.vector
        def _(dve):
            nc.vector.memset(r_t[D:W, :, :], 1.0).then_inc(ready, 1)

            def count(i, k, T, rows):
                g = i * GR + k
                dve.wait_ge(second_t.sem, second_t.done(g))
                nc.vector.bn_stats(record(c.stat, g), h2_t_ps[0:D, 0:T * rows]).then_inc(counted.sem, 1)

            def keep(i, k, T, rows):
                g = i * GR + k
                dve.wait_ge(second.sem, second.done(g))
                dve.wait_ge(h_made.sem, h_made.done(g))
                nc.vector.tensor_copy(c.node_tab[0:rows, bass.ds(g * GT, T), 0:D],
                                      h2_ps[0:rows, k % 2, 0:T * D].rearrange("p (a b) -> p a b", a=T))\
                    .then_inc(kept.sem, 1)
            laps(nc.vector, [(0, count), (0, keep)])


def out_nodes(nc, c, x, out):
    with Phase(nc) as ctx:
        def sb(name, shape, dt=F32):
            return ctx.sbuf(name, shape, dt)

        x_in = sb("x_in", [P, RING, GT, D])
        scaled = sb("scaled", [P, 2, GT, D])
        z = sb("z", [P, 2, GT, D])
        res = sb("res", [P, RING, GT, D])
        terms = sb("terms", [D, 2])
        diag = sb("diag", [D, 2, D])
        scale = sb("scale", [P, GT, D])
        shift = sb("shift", [P, GT, D])
        rows_ps = ctx.psum("rows_ps", [P, 512], F32)
        ready = ctx.semaphore("ready")
        diag_made = ctx.semaphore("diag_made")
        spread_out = ctx.semaphore("spread_out")
        norm_h = Norm(ctx, nc, "h2")
        loaded = DmaRing(ctx, nc, "loaded")
        stored = DmaRing(ctx, nc, "stored")
        scaled_made = Count(ctx, nc, "scaled_made")
        shifted = Count(ctx, nc, "shifted")
        z_made = Count(ctx, nc, "z_made")
        res_made = Count(ctx, nc, "res_made")
        norm = RowNorm(ctx, nc, c, "norm", ready)
        block = ctx.enter_context(nc.Block())

        @block.sync
        def _(sp):
            def load(i, k, T, rows):
                g = i * GR + k
                wait_apart(nc.sync, ready, (z_made.sem, z_made.free(g, RING)))
                sp.dma_start(x_in[0:rows, k % RING, 0:T, :], group_rows(x, g, T, rows)).then_inc(loaded.sem(k), 16)
            sp.wait_ge(ready, 1)
            laps(nc.sync, [(0, load)])
            wait_stores(sp, stored)

        @block.tensor
        def _(pe):
            pe.wait_ge(diag_made, 2)
            for n in range(2):
                last = nc.tensor.matmul(rows_ps[:, n * D:(n + 1) * D], c.ones[0:D, :], diag[:, n, :], start=True, stop=True)
            last.then_inc(spread_out, 1)

        @block.gpsimd
        def _(pool):
            def multiply(i, k, T, rows):
                g = i * GR + k
                wait_apart(nc.gpsimd, ready, (z_made.sem, z_made.free(g, 2)))
                nc.gpsimd.tensor_tensor(scaled[0:rows, k % 2, 0:T, :], c.node_tab[0:rows, bass.ds(g * GT, T), 0:D],
                                        scale[0:rows, 0:T, :], ALU.mult).then_inc(scaled_made.sem, 1)
            pool.wait_ge(ready, 1)
            laps(nc.gpsimd, [(0, multiply)])

        @block.scalar
        def _(act):
            norm_h.on_scalar(act)

            def normalise(i, k, T, rows):
                g = i * GR + k
                act.wait_ge(stored.sem(k), stored.free(i, k))
                norm.apply(act, g, k % 2, T, rows, lambda j: z[0:rows, k % 2, j, :],
                           lambda j: res[0:rows, k % RING, j, :]).then_inc(res_made.sem, 1)
            def store(i, k, T, rows):
                g = i * GR + k
                act.wait_ge(res_made.sem, res_made.done(g))
                nc.scalar.dma_start(group_rows(out, g, T, rows), res[0:rows, k % RING, 0:T, :])\
                    .then_inc(stored.sem(k), 16)

            def deviate(i, k, T, rows):
                norm.deviate(act, i * GR + k, k % 2, T, rows)

            laps(nc.scalar, [(0, normalise), (1, deviate), (0, store)])

        @block.vector
        def _(dve):
            norm_h.on_vector(dve, c.stat, column(c, "gamma"), column(c, "beta"), terms)
            for n in range(2):
                nc.vector.tensor_scalar(diag[:, n, :], c.ident[0:D, 0:D], terms[:, n:n + 1], None, ALU.mult)\
                    .then_inc(diag_made, 1)
            dve.wait_ge(spread_out, 1)
            for n, to in enumerate((scale, shift)):
                for j in range(GT):
                    last = nc.vector.tensor_copy(to[:, j, :], rows_ps[:, n * D:(n + 1) * D])
            last.then_inc(ready, 1)

            def add_shift(i, k, T, rows):
                g = i * GR + k
                dve.wait_ge(scaled_made.sem, scaled_made.done(g))
                u = flat(scaled[0:rows, k % 2, 0:T, :])
                nc.vector.tensor_tensor(u, u, flat(shift[0:rows, 0:T, :]), ALU.add).then_inc(shifted.sem, 1)

            def join(i, k, T, rows):
                g = i * GR + k
                dve.wait_ge(shifted.sem, shifted.done(g))
                dve.wait_ge(loaded.sem(k), loaded.done(i, k))
                dve.wait_ge(res_made.sem, res_made.free(g, 2))
                nc.vector.scalar_tensor_tensor(flat(z[0:rows, k % 2, 0:T, :]), flat(scaled[0:rows, k % 2, 0:T, :]), 0.0,
                                               flat(x_in[0:rows, k % RING, 0:T, :]), ALU.max, ALU.add)\
                    .then_inc(z_made.sem, 1)
                dve.wait_ge(z_made.sem, z_made.done(g))
                measure_rows((norm, g, k % 2, T, rows, lambda j: z[0:rows, k % 2, j, :]))

            def finish(i, k, T, rows):
                finish_rows(dve, (norm, i * GR + k, k % 2, T, rows))
            dve.wait_ge(ready, 1)
            laps(nc.vector, [(0, finish), (1, join), (2, add_shift)])


def wait_stores(sp, stored):
    for k in range(RING):
        last = max(g for g in range(GROUPS + 1) if g % RING == k)
        sp.wait_ge(stored.sem(k), stored.done(last // GR, last % GR))


def given_arrays(np, inputs):
    a = {k: np.asarray(v) for k, v in inputs.items()}
    out = {"x": a["x"], "src": a["src"], "dst": a["dst"],
           "src_cols": a["src"][:TILES * P].reshape(TILES, P).T,
           "dst_cols": a["dst"][:TILES * P].reshape(TILES, P).T,
           "edge4_t": a["edge_attr_4"].T, "edge32_t": a["edge_attr_32"].T}
    unit = np.zeros((1, W), np.float32)
    unit[0, D] = 1
    for l in range(2):
        w0, b0 = a["L0_gnn_W0"][l], a["L0_gnn_b0"][l]
        w1, b1 = a["L0_gnn_W1"][l], a["L0_gnn_b1"][l]
        w2, b2 = a["L0_gnn_W2"][l], a["L0_gnn_b2"][l]
        out[f"self_t{l}"] = np.concatenate([np.concatenate([w1, b1[None]]).T, unit])
        out[f"near_t{l}"] = np.concatenate([w0, b0[None]]).T
        out[f"w2_self{l}"] = np.concatenate([w2[:D], b2[None]])
        out[f"w2_near{l}"] = w2[D:]
    wm = a["L2_gnn_W_msg"]
    out["w_src"] = np.concatenate([wm[:D], a["L2_gnn_b_msg"][None]])
    out["w_dst"] = wm[D:2 * D]
    out["w_feat"] = wm[2 * D:]
    out["w_edge4"] = np.concatenate([a["L2_gnn_W_edge"], a["L2_gnn_b_edge"][None]])
    out["qkv"] = np.concatenate([a["L1_gnn_qW"], a["L1_gnn_kW"], a["L1_gnn_vW"]], axis=1)
    out["w_node"] = a["L2_gnn_W_node"]
    out["w_edge32"] = np.concatenate([a["L3_gnn_We"], a["L3_gnn_be"][None]])
    out["w1"] = a["L3_gnn_W1"]
    out["w2"] = np.concatenate([a["L3_gnn_W2"], a["L3_gnn_b2"][None]])
    out["cols"] = np.stack([a["L2_gnn_b_node"], a["L2_gnn_g_node"], a["L2_gnn_beta_node"], a["L2_gnn_g_edge"],
                            a["L2_gnn_beta_edge"], a["L2_gnn_g_msg"], a["L2_gnn_beta_msg"], a["L3_gnn_b1"],
                            a["L3_gnn_gamma"], a["L3_gnn_beta"]], axis=1)
    return {k: np.ascontiguousarray(v) for k, v in out.items()}


def kernel(**inputs):
    import numpy as np
    import concourse.bacc as bacc
    from concourse.bass_utils import run_bass_kernel_spmd as run

    nc = bacc.Bacc("TRN2", target_bir_lowering=False, num_devices=1)
    arrays = given_arrays(np, inputs)
    given = {k: nc.dram_tensor(f"in_{k}", a.shape, mybir.dt.from_np(a.dtype), kind="ExternalInput").ap()
             for k, a in arrays.items()}
    out = nc.dram_tensor("out", (N, D), F32, kind="ExternalOutput").ap()
    gnn(nc, given, out)
    r = run(nc, [{f"in_{k}": a for k, a in arrays.items()}], core_ids=[0])
    return r.results[0]["out"]
```

```python
import concourse.bass as bass
from concourse import mybir
from contextlib import ExitStack

F32 = mybir.dt.float32
I32 = mybir.dt.int32
ALU = mybir.AluOpType
ACT = mybir.ActivationFunctionType
AX = mybir.AxisListType

N = 50000
D = 96
W = D + 1
HEADS = 4
DH = D // HEADS
M = D + HEADS
P = 128
TILES = N // P
TAIL = N - TILES * P
GT = 3
GR = 10
LAPS = TILES // (GT * GR)
GROUPS = LAPS * GR
RING = 5
PAIRS = GROUPS // 2
STEP = 8
SLOTS = TILES + 2
DUMP = N
HALF_TABLE = SLOTS * 5 // 8
EPS = 1e-5
FULL = (GT, P)
LAST = (1, TAIL)


class Phase(ExitStack):

    count = 0

    def __init__(self, nc):
        super().__init__()
        self.nc = nc
        Phase.count += 1
        self.tag = f"p{Phase.count}_"
        self.sems = []

    def sbuf(self, name, shape, dt):
        return self.enter_context(self.nc.sbuf_tensor(self.tag + name, shape, dt))

    def psum(self, name, shape, dt):
        return self.enter_context(self.nc.psum_tensor(self.tag + name, shape, dt))

    def semaphore(self, name):
        self.sems.append(self.nc.alloc_semaphore(self.tag + name))
        return self.sems[-1]

    def __exit__(self, *error):
        super().__exit__(*error)
        if error[0] is None:
            self.nc.clear_and_free_semaphores(self.sems)
            self.nc.all_engine_barrier(sem_only=True)


START = 32


class Count:

    def __init__(self, ctx, nc, name, unit=1):
        self.sem = ctx.semaphore(name)
        self.unit = unit
        nc.sync.sem_inc(self.sem, START * unit)

    def done(self, g):
        return (g + (START + 1)) * self.unit

    def free(self, g, ring):
        return (g + (START + 1 - ring)) * self.unit


class DmaRing:

    def __init__(self, ctx, nc, name, dmas=1, pool=False, ring=RING):
        self.ring = ring
        self.sems = [ctx.semaphore(f"{name}{s}") for s in range(ring)]
        self.inc = 16 * dmas
        self.first = 1 if pool else 2
        if not pool:
            for s in self.sems:
                nc.sync.sem_inc(s, self.inc)

    def sem(self, k):
        return self.sems[k % self.ring]

    def done(self, i, k):
        return (i * (GR // self.ring) + (k // self.ring + self.first)) * self.inc

    def free(self, i, k):
        return (i * (GR // self.ring) + (k // self.ring + 1)) * self.inc


def wait_apart(eng, steady, *waits):
    held = [v if isinstance(v, int) else eng.snap(eng.to_reg(v)) for _, v in waits]
    eng.wait_ge(steady, 1)
    for (sem, _), value in zip(waits, held):
        eng.wait_ge(sem, value)


def laps(eng, stages):
    most = max(max(leads) if isinstance(leads, tuple) else leads for leads, _ in stages)

    def group(g):
        return (g // GR, g % GR, *(LAST if g == GROUPS else FULL)) if 0 <= g <= GROUPS else None

    def beside(g):
        for leads, step in stages:
            if isinstance(leads, tuple):
                groups = [group(g + lead) for lead in leads]
                if any(groups):
                    step(*groups)
            elif group(g + leads):
                step(*group(g + leads))

    for g in range(-most, 0):
        beside(g)
    with eng.Fori(0, LAPS - 1) as i:
        for k in range(GR):
            for leads, step in stages:
                if isinstance(leads, tuple):
                    step(*((i + (k + lead) // GR, (k + lead) % GR, *FULL) for lead in leads))
                else:
                    step(i + (k + leads) // GR, (k + leads) % GR, *FULL)
    for g in range(GROUPS - GR, GROUPS + 1):
        beside(g)


def group_rows(dram, g, T, rows):
    if rows == TAIL:
        return dram[TILES * P:N, :].rearrange("(t p) f -> p t f", t=1)
    return dram[bass.ds(g * (GT * P), GT * P), :].rearrange("(t p) f -> p t f", p=P)


def packed_rows(dram, g, T, rows):
    if rows == TAIL:
        return group_rows(dram, g, T, rows)
    return dram[bass.ds(g * (GT * P), GT * P), :].rearrange("(p t) f -> p t f", p=P)


def group_cols(dram, g, rows):
    if rows == TAIL:
        return dram[:, TILES * P:N]
    return dram[:, bass.ds(g * (GT * P), GT * P)]


class Chip:
    pass


def gnn(nc, given, out):
    with ExitStack() as ctx:
        def sb(name, shape, dt=F32):
            return ctx.enter_context(nc.sbuf_tensor(name, shape, dt))

        def dram(name, shape, dt=F32):
            return nc.dram_tensor(name, shape, dt, kind="Internal").ap()

        c = Chip()
        c.iota256 = sb("iota256", [P, 2 * P])
        c.tile_base = sb("tile_base", [P, SLOTS])
        c.ident = sb("ident", [P, P])
        c.ones = sb("ones", [P, P])
        c.eps = sb("eps", [P, 1])
        c.zeros = sb("zeros", [P, GT, M])
        c.dst_f = sb("dst_f", [P, TILES + 1])
        c.steps = sb("steps", [1, (GROUPS + 2) * STEP], I32)
        c.w_src = sb("w_src", [W, D])
        c.w_dst = sb("w_dst", [D, D])
        c.w_feat = sb("w_feat", [D, D])
        c.w_edge4 = sb("w_edge4", [5, D])
        c.w_node = sb("w_node", [D, D])
        c.w_edge32 = sb("w_edge32", [33, D])
        c.w1 = sb("w1", [D, D])
        c.w2 = sb("w2", [W, D])
        c.cols = sb("cols", [D, 10])
        c.stat = sb("stat", [D, GROUPS + 1, 6])
        c.stat_msg = sb("stat_msg", [D, GROUPS + 1, 6])
        c.hop_tab = dram("steps_dram", [(PAIRS + 1), 2 * STEP], I32)
        c.att = [dram(f"att{h}", [P * SLOTS, M]) for h in range(2)]
        x1, x2, x3, x4 = (dram(f"x{l}", [N, D]) for l in range(1, 5))
        x0 = given["x"]
        c.src, c.src_cols, c.dst, c.dst_cols = (given[k] for k in ("src", "src_cols", "dst", "dst_cols"))

        with ExitStack() as early:
            def sb_early(name, shape, dt=F32):
                return early.enter_context(nc.sbuf_tensor(name, shape, dt))

            c.lower = sb_early("lower", [P, P])
            c.src_f = sb_early("src_f", [P, TILES + 1])
            c.to_dump = sb_early("to_dump", [P, TILES + 1])
            c.mix_self = [sb_early(f"mix_self{l}", [W, D]) for l in range(2)]
            c.mix_near = [sb_early(f"mix_near{l}", [W, D]) for l in range(2)]
            c.qkv = sb_early("qkv", [D, 3 * D])
            with nc.sbuf_tensor("node_tab", [P, SLOTS, W], F32) as c.node_tab:
                load_and_index(nc, c, given)
                gather_sum(nc, c, x0, clear=c.att)
                mix_nodes(nc, c, given["x_t"], x1, 0, None)
                gather_sum(nc, c, x1)
                mix_nodes(nc, c, x1, x2, 1, x0)
            attention_edges(nc, c, x2, given["edge4_t"])
            attention_nodes(nc, c, x2, x3)
        with nc.sbuf_tensor("node_tab2", [P, SLOTS, W], F32) as c.node_tab:
            clear_table(nc, c)
            message_edges(nc, c, x3, given["edge4_t"])
            message_nodes(nc, c, x3, x4)
            gather_sum(nc, c, x4, given["edge32_t"])
            mlp_nodes(nc, c, x4)
            out_nodes(nc, c, x4, out)


COLS = ["b_node", "g_node", "beta_node", "g_edge", "beta_edge", "g_msg", "beta_msg", "b1", "gamma", "beta"]


def column(c, name):
    k = COLS.index(name)
    return c.cols[:, k:k + 1]


def load_and_index(nc, c, given):
    with Phase(nc) as ctx:
        def sb(name, shape, dt=F32):
            return ctx.sbuf(name, shape, dt)

        def sem(name):
            return ctx.semaphore(name)

        src_i = sb("src_i", [P, TILES + 1], I32)
        dst_i = sb("dst_i", [P, TILES + 1], I32)
        hops = sb("hops", [PAIRS + 1, 2 * GT * P], I32)
        hops_f = sb("hops_f", [PAIRS + 1, 2 * GT, P])
        low = sb("low", [PAIRS + 1, 2 * GT])
        more = sb("more", [PAIRS + 1, 2 * GT])
        anymore = sb("anymore", [PAIRS + 1, 2])
        step_rows = sb("step_rows", [PAIRS + 1, 2, STEP], I32)
        self_t = [sb(f"self_t{l}", [W, W]) for l in range(2)]
        near_t = [sb(f"near_t{l}", [D, W]) for l in range(2)]
        w2_self = [sb(f"w2_self{l}", [W, D]) for l in range(2)]
        w2_near = [sb(f"w2_near{l}", [D, D]) for l in range(2)]
        mix = ctx.psum("mix", [P, 4, 512], F32)
        filled = sem("filled")
        masks = sem("masks")
        idx_loaded = sem("idx_loaded")
        w_loaded = sem("w_loaded")
        step = sem("step")
        steps_out = sem("steps_out")
        steps_in = sem("steps_in")
        mixed = sem("mixed")
        block = ctx.enter_context(nc.Block())
        weights = ([(self_t[l][:], given[f"self_t{l}"]) for l in range(2)]
                   + [(near_t[l][:], given[f"near_t{l}"]) for l in range(2)]
                   + [(w2_self[l][:], given[f"w2_self{l}"]) for l in range(2)]
                   + [(w2_near[l][:], given[f"w2_near{l}"]) for l in range(2)]
                   + [(c.w_src[:], given["w_src"]), (c.w_dst[:], given["w_dst"]), (c.w_feat[:], given["w_feat"]),
                      (c.w_edge4[:], given["w_edge4"]), (c.qkv[:], given["qkv"]), (c.w_node[:], given["w_node"]),
                      (c.w_edge32[:], given["w_edge32"]), (c.w1[:], given["w1"]), (c.w2[:], given["w2"]),
                      (c.cols[:], given["cols"])])
        tail = slice(TILES * P, N)
        src, dst = given["src"], given["dst"]

        @block.sync
        def _(sp):
            sp.wait_ge(filled, 4)
            loads = [(hops[0:PAIRS, :], dst[0:TILES * P].rearrange("(i f) -> i f", i=PAIRS)),
                     (hops[PAIRS:PAIRS + 1, 0:P], dst[N - P:N].rearrange("(o f) -> o f", o=1)),
                     (dst_i[:, 0:TILES], given["dst_cols"]),
                     (dst_i[0:TAIL, TILES:TILES + 1], dst[tail].rearrange("(p o) -> p o", o=1)),
                     (src_i[:, 0:TILES], given["src_cols"]),
                     (src_i[0:TAIL, TILES:TILES + 1], src[tail].rearrange("(p o) -> p o", o=1))]
            for to, frm in loads:
                sp.dma_start(to, frm).then_inc(idx_loaded, 16)
            for to, frm in weights:
                sp.dma_start(to, frm).then_inc(w_loaded, 16)
            sp.wait_ge(step, 12)
            sp.dma_start(c.hop_tab, step_rows[:].rearrange("p a b -> p (a b)")).then_inc(steps_out, 16)
            sp.wait_ge(steps_out, 16)
            sp.dma_start(c.steps[:], c.hop_tab.rearrange("(o i) k -> o (i k)", o=1)).then_inc(steps_in, 16)
            sp.wait_ge(steps_in, 16)

        @block.gpsimd
        def _(pool):
            nc.gpsimd.iota(c.iota256[:], pattern=[[1, 2 * P]], base=0, channel_multiplier=0,
                           allow_small_or_imprecise_dtypes=True)
            nc.gpsimd.iota(c.tile_base[:], pattern=[[P, SLOTS]], base=0, channel_multiplier=0,
                           allow_small_or_imprecise_dtypes=True)
            nc.gpsimd.iota(c.to_dump[:], pattern=[[0, TILES + 1]], base=DUMP, channel_multiplier=1,
                           allow_small_or_imprecise_dtypes=True).then_inc(masks, 1)
            nc.gpsimd.memset(c.ident[:], 0.0).then_inc(masks, 1)
            nc.gpsimd.memset(c.lower[:], 1.0).then_inc(masks, 1)
            pool.wait_ge(masks, 3)
            nc.gpsimd.affine_select(out=c.ident[:], in_=c.ident[:], compare_op=ALU.not_equal, fill=1.0,
                                    base=0, pattern=[[-1, P]], channel_multiplier=1)
            nc.gpsimd.affine_select(out=c.lower[:], in_=c.lower[:], compare_op=ALU.is_gt, fill=0.0,
                                    base=0, pattern=[[-1, P]], channel_multiplier=1)
            nc.gpsimd.memset(flat(c.node_tab[:, HALF_TABLE:SLOTS, :]), 0.0)

        @block.tensor
        def _(pe):
            pe.wait_ge(w_loaded, 16 * len(weights))
            for l in range(2):
                nc.tensor.matmul(mix[0:W, 2 * l, 0:D], self_t[l][:], w2_self[l][:], start=True, stop=True)\
                    .then_inc(mixed, 1)
                nc.tensor.matmul(mix[0:W, 2 * l + 1, 0:D], near_t[l][:], w2_near[l][:], start=True, stop=True)\
                    .then_inc(mixed, 1)

        @block.scalar
        def _(act):
            for l in range(2):
                act.wait_ge(mixed, 2 * l + 2)
                nc.scalar.copy(c.mix_self[l][:], mix[0:W, 2 * l, 0:D])
                nc.scalar.copy(c.mix_near[l][:], mix[0:W, 2 * l + 1, 0:D])

        @block.vector
        def _(dve):
            nc.vector.memset(hops[:], 0).then_inc(filled, 1)
            nc.vector.memset(step_rows[:], 0).then_inc(filled, 1)
            nc.vector.memset(dst_i[:, TILES:TILES + 1], 0).then_inc(filled, 1)
            nc.vector.memset(src_i[:, TILES:TILES + 1], 0).then_inc(filled, 1)
            nc.vector.memset(c.zeros[:], 0.0)
            nc.vector.memset(c.ones[:], 1.0)
            nc.vector.memset(c.eps[:], EPS)
            dve.wait_ge(filled, 4)
            dve.wait_ge(idx_loaded, 16 * 6)
            count = 0

            def then(ins):
                nonlocal count
                count += 1
                ins.then_inc(step, 1)
                dve.wait_ge(step, count)

            then(nc.vector.tensor_copy(c.dst_f[:], dst_i[:]))
            then(nc.vector.tensor_copy(c.src_f[:], src_i[:]))
            dve.wait_ge(masks, 3)
            then(nc.vector.tensor_tensor(c.to_dump[:], c.to_dump[:], c.src_f[:], ALU.subtract))
            then(nc.vector.tensor_scalar(hops[:], hops[:], 7, None, ALU.arith_shift_right))
            then(nc.vector.tensor_copy(hops_f[:].rearrange("p a b -> p (a b)"), hops[:]))
            then(nc.vector.tensor_reduce(low[:], hops_f[:], AX.X, ALU.min))
            then(nc.vector.tensor_reduce(more[:], hops_f[:], AX.X, ALU.max))
            then(nc.vector.tensor_tensor(more[:], more[:], low[:], ALU.subtract))
            then(nc.vector.tensor_scalar(more[:], more[:], -1.0, 0.0, ALU.add, ALU.max))
            then(nc.vector.tensor_reduce(anymore[:], more[:].rearrange("p (a b) -> p a b", a=2), AX.X, ALU.max))
            nc.vector.tensor_copy(step_rows[:, :, 0:GT], low[:].rearrange("p (a b) -> p a b", a=2))
            nc.vector.tensor_copy(step_rows[:, :, 4:4 + GT], more[:].rearrange("p (a b) -> p a b", a=2))\
                .then_inc(step, 1)
            nc.vector.tensor_copy(step_rows[:, :, 3:4], anymore[:].rearrange("p (a b) -> p a b", b=1))\
                .then_inc(step, 1)
            nc.vector.memset(flat(c.node_tab[:, 0:HALF_TABLE, :]), 0.0)


class Norm:

    def __init__(self, ctx, nc, name):
        self.nc = nc
        self.mv = ctx.sbuf(f"{name}_mv", [D, 2], F32)
        self.inv = ctx.sbuf(f"{name}_inv", [D, 1], F32)
        self.root = ctx.sbuf(f"{name}_root", [D, 1], F32)
        self.stepped = ctx.semaphore(f"{name}_stepped")
        self.rooted = ctx.semaphore(f"{name}_rooted")

    def on_vector(self, dve, stat, gamma, beta, terms):
        nc, mv, inv = self.nc, self.mv, self.inv
        nc.vector.bn_aggr(mv[:], stat[:].rearrange("p a b -> p (a b)")).then_inc(self.stepped, 1)
        dve.wait_ge(self.stepped, 1)
        nc.vector.tensor_scalar(inv[:], mv[:, 1:2], EPS, None, ALU.add).then_inc(self.stepped, 1)
        dve.wait_ge(self.stepped, 2)
        nc.vector.reciprocal(inv[:], inv[:]).then_inc(self.stepped, 1)
        dve.wait_ge(self.rooted, 1)
        nc.vector.tensor_tensor(terms[:, 0:1], self.root[:], gamma, ALU.mult).then_inc(self.stepped, 1)
        dve.wait_ge(self.stepped, 4)
        nc.vector.tensor_tensor(terms[:, 1:2], mv[:, 0:1], terms[:, 0:1], ALU.mult).then_inc(self.stepped, 1)
        dve.wait_ge(self.stepped, 5)
        nc.vector.tensor_tensor(terms[:, 1:2], beta, terms[:, 1:2], ALU.subtract).then_inc(self.stepped, 1)
        dve.wait_ge(self.stepped, 6)

    def on_scalar(self, act):
        act.wait_ge(self.stepped, 3)
        self.nc.scalar.activation(self.root[:], self.inv[:], ACT.Sqrt).then_inc(self.rooted, 1)


def flat(ap):
    return ap.rearrange("p a b -> p (a b)")


def record(stat, g):
    return flat(stat[:, bass.ds(g, 1), :])


class EdgeNorm:

    def __init__(self, ctx, nc, c, edge4_t, steady):
        self.nc, self.c, self.edge4_t, self.steady = nc, c, edge4_t, steady
        self.feats = ctx.sbuf("feats", [5, RING, GT * P], F32)
        self.h = ctx.sbuf("h", [D, 2, GT * P], F32)
        self.terms = ctx.sbuf("terms", [D, 2], F32)
        self.shift_l = ctx.sbuf("shift_l", [D, W], F32)
        self.h_ps = ctx.psum("h_ps", [P, 2, 512], F32)
        self.norm = Norm(ctx, nc, "edge")
        self.feats_in = DmaRing(ctx, nc, "feats_in")
        self.multiplied = Count(ctx, nc, "multiplied")
        self.rectified = Count(ctx, nc, "rectified")
        self.counted = Count(ctx, nc, "counted_feats")
        self.shift_set = ctx.semaphore("shift_set")
        self.folded = ctx.semaphore("folded")

    def load(self, i, k, T, rows):
        g = i * GR + k
        wait_apart(self.nc.sync, self.steady, (self.multiplied.sem, self.multiplied.free(g, RING)))
        self.nc.sync.dma_start(self.feats[0:4, k % RING, 0:T * rows], group_cols(self.edge4_t, g, rows))\
            .then_inc(self.feats_in.sem(k), 16)

    def multiply(self, pe, i, k, T, rows):
        g = i * GR + k
        pe.wait_ge(self.feats_in.sem(k), self.feats_in.done(i, k))
        pe.wait_ge(self.rectified.sem, self.rectified.free(g, 2))
        self.nc.tensor.matmul(self.h_ps[0:D, k % 2, 0:T * rows], self.c.w_edge4[:], self.feats[:, k % RING, 0:T * rows],
                              start=True, stop=True).then_inc(self.multiplied.sem, 1)

    def rectify(self, act, i, k, T, rows):
        g = i * GR + k
        act.wait_ge(self.multiplied.sem, self.multiplied.done(g))
        act.wait_ge(self.counted.sem, self.counted.free(g, 2))
        self.nc.scalar.activation(self.h[:, k % 2, 0:T * rows], self.h_ps[0:D, k % 2, 0:T * rows], ACT.Relu)\
            .then_inc(self.rectified.sem, 1)

    def count(self, dve, i, k, T, rows):
        g = i * GR + k
        dve.wait_ge(self.rectified.sem, self.rectified.done(g))
        self.nc.vector.bn_stats(record(self.c.stat, g), self.h[:, k % 2, 0:T * rows]).then_inc(self.counted.sem, 1)

    def set_up(self, last):
        self.nc.vector.memset(self.shift_l[:], 0.0).then_inc(self.shift_set, 1)
        self.nc.vector.memset(self.feats[:], 1.0).then_inc(last, 1)

    def fold_on_vector(self, dve):
        nc, c = self.nc, self.c
        dve.wait_ge(self.counted.sem, self.counted.done(GROUPS))
        self.norm.on_vector(dve, c.stat, column(c, "g_edge"), column(c, "beta_edge"), self.terms)
        dve.wait_ge(self.shift_set, 1)
        nc.vector.tensor_copy(self.shift_l[:, D:W], self.terms[:, 1:2]).then_inc(self.shift_set, 1)
        dve.wait_ge(self.folded, 1)
        nc.vector.tensor_copy(c.w_src[:], self.h_ps[0:W, 0, 0:D])
        nc.vector.tensor_scalar(c.w_feat[:], c.w_feat[:], self.terms[:, 0:1], None, ALU.mult)

    def fold_on_tensor(self, pe):
        nc, c, to = self.nc, self.c, self.h_ps[0:W, 0, 0:D]
        pe.wait_ge(self.shift_set, 2)
        nc.tensor.matmul(to, c.ident[0:W, 0:W], c.w_src[:], start=True, stop=False)
        nc.tensor.matmul(to, self.shift_l[:], c.w_feat[:], start=False, stop=True).then_inc(self.folded, 1)


def clear_table(nc, c):
    with Phase(nc) as ctx:
        block = ctx.enter_context(nc.Block())

        @block.vector
        def _(dve):
            nc.vector.memset(flat(c.node_tab[:, 0:HALF_TABLE, :]), 0.0)

        @block.gpsimd
        def _(pool):
            nc.gpsimd.memset(flat(c.node_tab[:, HALF_TABLE:SLOTS, :]), 0.0)


class NodeSum:

    def __init__(self, ctx, nc, c, banks):
        self.nc, self.c, self.tag = nc, c, ctx.tag
        self.hot = ctx.sbuf("hot", [P, GT, 2 * P], F32)
        self.far_hot = ctx.sbuf("far_hot", [P, P], F32)
        self.banks = banks
        self.acc = ctx.psum("acc", [P, banks, 512], F32)
        self.far_acc = ctx.psum("far_acc", [P, 512], F32)
        self.hot_made = Count(ctx, nc, "hot_made")
        self.summed = Count(ctx, nc, "summed")
        self.added = Count(ctx, nc, "added")
        self.far_matched = ctx.semaphore("far_matched")
        self.far_summed = ctx.semaphore("far_summed")
        self.far_added = ctx.semaphore("far_added")

    def acc_of(self, k, j):
        return self.acc[:, (GT * k + j) % self.banks, 0:2 * W]

    def on_tensor(self, pe, rows_of, wait_rows):
        nc, c = self.nc, self.c
        far = nc.tensor.alloc_register(self.tag + "far_steps_pe")
        any_far = nc.tensor.alloc_register(self.tag + "any_far_pe")
        more = [nc.tensor.alloc_register(self.tag + f"more_pe{j}") for j in range(4)]
        nc.tensor.reg_mov(far, 0)

        def load_flag(g):
            nc.tensor.reg_load(any_far, c.steps[0:1, bass.ds(g * STEP + 3, 1)])
        load_flag(0)

        def step(i, k, T, rows):
            g = i * GR + k
            some = nc.tensor.snap(any_far, min_val=0, max_val=TILES)
            wait_rows(i, k)
            with nc.tensor.If(some > 0):
                nc.tensor.reg_load(more, c.steps[0:1, bass.ds(g * STEP + 4, 4)])
                for j in range(T):
                    count = nc.tensor.snap(more[j], min_val=0, max_val=TILES)
                    with nc.tensor.If(count > 0):
                        with nc.tensor.Fori(0, count):
                            nc.tensor.reg_add(far, far, 1)
                            now = nc.tensor.snap(far)
                            pe.wait_ge(self.far_matched, now)
                            nc.tensor.matmul(self.far_acc[:, 0:W], self.far_hot[0:rows, :], rows_of(k, j, rows),
                                             start=True, stop=True).then_inc(self.far_summed, 1)
                            pe.wait_ge(self.far_added, now)
            for j in range(T):
                t = g * GT + j
                pe.wait_ge(self.hot_made.sem, self.hot_made.done(t))
                pe.wait_ge(self.added.sem, self.added.free(t, self.banks))
                for h in range(2):
                    last = nc.tensor.matmul(self.acc_of(k, j)[:, h * W:(h + 1) * W],
                                            self.hot[0:rows, j, h * P:(h + 1) * P], rows_of(k, j, rows),
                                            start=True, stop=True)
                last.then_inc(self.summed.sem, 1)
                if j == 1:
                    load_flag(g + 1)
        return step

    def on_vector(self, dve):
        nc, c = self.nc, self.c
        far = nc.vector.alloc_register(self.tag + "far_steps_dve")
        near = [[nc.vector.alloc_register(self.tag + f"near_dve{s}_{j}") for j in range(4)] for s in range(2)]
        more = [nc.vector.alloc_register(self.tag + f"more_dve{j}") for j in range(4)]
        nc.vector.reg_mov(far, 0)
        first = {}

        def match(g, j, rows, base):
            t = g * GT + j
            dve.wait_ge(self.summed.sem, self.summed.free(t, GT))
            nc.vector.tensor_scalar(self.hot[0:rows, j, :], c.iota256[0:rows, :], c.tile_base[0:rows, bass.ds(base, 1)],
                                    c.dst_f[0:rows, bass.ds(t, 1)], ALU.add, ALU.is_equal).then_inc(self.hot_made.sem, 1)

        def add(g, k, j):
            t = g * GT + j
            dve.wait_ge(self.added.sem, self.added.free(t, 1))
            dve.wait_ge(self.summed.sem, self.summed.done(t))
            at = c.node_tab[:, bass.ds(first[j], 2), :]
            nc.vector.tensor_tensor(at, at, self.acc_of(k, j).rearrange("p (a b) -> p a b", a=2),
                                    ALU.add).then_inc(self.added.sem, 1)

        def middle(i, k, T, rows):
            g = i * GR + k
            regs = near[k % 2]
            for j in range(T):
                first[j] = nc.vector.snap(regs[j], min_val=0, max_val=TILES)
            with nc.vector.If(nc.vector.snap(regs[3], min_val=0, max_val=TILES) > 0):
                nc.vector.reg_load(more, c.steps[0:1, bass.ds(g * STEP + 4, 4)])
                for j in range(T):
                    count = nc.vector.snap(more[j], min_val=0, max_val=TILES)
                    with nc.vector.If(count > 0):
                        with nc.vector.Fori(0, count) as n:
                            nc.vector.reg_add(far, far, 1)
                            now = nc.vector.snap(far)
                            tile = nc.s_assert_within(first[j] + 2 + n, 2, TILES)
                            t = g * GT + j
                            dve.wait_ge(self.added.sem, self.added.free(g * GT, 1))
                            nc.vector.tensor_scalar(self.far_hot[0:rows, :], c.iota256[0:rows, 0:P],
                                                    c.tile_base[0:rows, bass.ds(tile, 1)],
                                                    c.dst_f[0:rows, bass.ds(t, 1)], ALU.add, ALU.is_equal)\
                                .then_inc(self.far_matched, 1)
                            dve.wait_ge(self.far_summed, now)
                            at = c.node_tab[:, bass.ds(tile, 1), :]
                            nc.vector.tensor_tensor(at, at, self.far_acc[:, 0:W].rearrange("p (a b) -> p a b", a=1),
                                                    ALU.add).then_inc(self.far_added, 1)
                            dve.wait_ge(self.far_added, now)
            if T == GT:
                match(g, GT - 1, rows, first[GT - 1])
            add(g, k, 0)

        def turn_over(new, old):
            if new:
                i, k, T, rows = new
                nc.vector.reg_load(near[k % 2], c.steps[0:1, bass.ds((i * GR + k) * STEP, 4)])
            for j in range(GT - 1):
                if new and j < T:
                    match(i * GR + k, j, rows, nc.vector.snap(near[k % 2][j], min_val=0, max_val=TILES))
                if old and j + 1 < old[2]:
                    add(old[0] * GR + old[1], old[1], j + 1)
        return [(0, middle), ((1, 0), turn_over)]


def gather_sum(nc, c, x, edge32_t=None, clear=()):
    with Phase(nc) as ctx:
        def sb(name, shape, dt=F32):
            return ctx.sbuf(name, shape, dt)

        def sem(name):
            return ctx.semaphore(name)

        rows_in = sb("rows_in", [P, RING, GT, W])
        idx = sb("idx", [P, GR, GT], I32)
        idx_in = DmaRing(ctx, nc, "idx_in", ring=GR)
        gathered = DmaRing(ctx, nc, "gathered", GT, pool=True)
        ones_set = sem("ones_set")
        node_sum = NodeSum(ctx, nc, c, GT)
        if edge32_t is not None:
            feats = sb("feats", [33, RING, GT * P])
            msg = sb("msg", [P, 2, GT, W])
            pre_ps = ctx.psum("pre_ps", [P, 2, 512], F32)
            feats_in = DmaRing(ctx, nc, "feats_in")
            joined_rows = sb("joined_rows", [P, 2, GT, D])
            pre_made = Count(ctx, nc, "pre_made")
            joined = Count(ctx, nc, "joined")
            msg_made = Count(ctx, nc, "msg_made")
        if clear:
            cleared = DmaRing(ctx, nc, "cleared", len(clear))
            dump_cleared = sem("dump_cleared")
        block = ctx.enter_context(nc.Block())

        @block.sync
        def _(sp):
            def load(i, k, T, rows):
                g = i * GR + k
                if edge32_t is not None:
                    wait_apart(nc.sync, ones_set, (joined.sem, joined.free(g, GR)))
                else:
                    wait_apart(nc.sync, ones_set, (node_sum.summed.sem,
                                                   node_sum.summed.free(g * GT + GT - 1, GT * GR)))
                sp.dma_start(idx[0:rows, k % GR, 0:T], idx_cols(c.src_cols, c.src, g, rows))\
                    .then_inc(idx_in.sem(k), 16)

            def load_feats(i, k, T, rows):
                g = i * GR + k
                wait_apart(nc.sync, ones_set, (pre_made.sem, pre_made.free(g, RING)))
                sp.dma_start(feats[0:32, k % RING, 0:T * rows], group_cols(edge32_t, g, rows))\
                    .then_inc(feats_in.sem(k), 16)
            sp.wait_ge(ones_set, 1)
            laps(nc.sync, [(0, load)] if edge32_t is None else [(3, load), (0, load_feats)])

        @block.gpsimd
        def _(pool):
            used = joined if edge32_t is not None else node_sum.summed
            per_group = 1 if edge32_t is not None else GT
            take = PoolTakes(nc, ctx.tag)
            idx_at = take.ring(idx_in.done(0, 0), idx_in)
            used_at = take.counter(used.free(per_group - 1, per_group * RING), per_group)

            def gather(i, k, T, rows):
                take.next_group(k, [used_at])
                idx_value, used_value = take.value(idx_at), take.value(used_at)
                pool.wait_ge(ones_set, 1)
                pool.wait_ge(idx_in.sem(k), idx_value)
                pool.wait_ge(used.sem, used_value)
                for j in range(T):
                    gather_tile(nc, rows_in[0:rows, k % RING, j, 0:D], x, idx[0:rows, k % GR, j:j + 1])\
                        .then_inc(gathered.sem(k), 16 * GT if T == 1 else 16)
            laps(nc.gpsimd, [(0, gather)])

        @block.tensor
        def _(pe):
            pe.wait_ge(ones_set, 1)

            def pre(i, k, T, rows):
                g = i * GR + k
                pe.wait_ge(feats_in.sem(k), feats_in.done(i, k))
                pe.wait_ge(joined.sem, joined.free(g, 2))
                for j in range(T):
                    last = nc.tensor.matmul(pre_ps[0:rows, k % 2, j * D:(j + 1) * D],
                                            feats[:, k % RING, j * P:j * P + rows], c.w_edge32[:], start=True, stop=True)
                last.then_inc(pre_made.sem, 1)

            if edge32_t is not None:
                add_up = node_sum.on_tensor(pe, lambda k, j, rows: msg[0:rows, k % 2, j, :],
                                            lambda i, k: pe.wait_ge(msg_made.sem, msg_made.done(i * GR + k)))
            else:
                add_up = node_sum.on_tensor(pe, lambda k, j, rows: rows_in[0:rows, k % RING, j, :],
                                            lambda i, k: pe.wait_ge(gathered.sem(k), gathered.done(i, k)))

            laps(nc.tensor, [(3, pre), (0, add_up)] if edge32_t is not None else [(0, add_up)])

        if clear:
            @block.scalar
            def _(act):
                def zero(i, k, T, rows):
                    g = i * GR + k
                    wait_apart(nc.scalar, ones_set, (node_sum.summed.sem, node_sum.summed.done(g * GT)))
                    for table in clear:
                        nc.scalar.dma_start(group_rows(table, g, T, rows), c.zeros[0:rows, 0:T, :])\
                            .then_inc(cleared.sem(k), 16)
                laps(nc.scalar, [(0, zero)])
                for table in clear:
                    nc.scalar.dma_start(table[N:N + P, :], c.zeros[:, 0, :]).then_inc(dump_cleared, 16)
                wait_stores(act, cleared)
                act.wait_ge(dump_cleared, 16 * len(clear))

        if edge32_t is not None:
            @block.scalar
            def _(act):
                def rectify(i, k, T, rows):
                    g = i * GR + k
                    act.wait_ge(joined.sem, joined.done(g))
                    act.wait_ge(node_sum.summed.sem, node_sum.summed.free(g * GT + GT - 1, 2 * GT))
                    nc.scalar.activation(msg[0:rows, k % 2, 0:T, 0:D], joined_rows[0:rows, k % 2, 0:T, :], ACT.Relu)\
                        .then_inc(msg_made.sem, 1)
                laps(nc.scalar, [(0, rectify)])

        @block.vector
        def _(dve):
            if edge32_t is not None:
                nc.vector.memset(feats[:], 1.0)
                nc.vector.memset(msg[:, :, :, D:W], 1.0)
            nc.vector.memset(rows_in[:, :, :, D:W], 1.0).then_inc(ones_set, 1)
            def join(i, k, T, rows):
                g = i * GR + k
                dve.wait_ge(pre_made.sem, pre_made.done(g))
                dve.wait_ge(gathered.sem(k), gathered.done(i, k))
                dve.wait_ge(msg_made.sem, msg_made.free(g, 2))
                nc.vector.tensor_tensor(joined_rows[0:rows, k % 2, 0:T, :], rows_in[0:rows, k % RING, 0:T, 0:D],
                                        pre_ps[0:rows, k % 2, 0:T * D].rearrange("p (a b) -> p a b", a=T), ALU.add)\
                    .then_inc(joined.sem, 1)
            stages = node_sum.on_vector(dve)
            laps(nc.vector, stages if edge32_t is None else [(2, join), *stages])


def idx_cols(cols, whole, g, rows):
    if rows == TAIL:
        return whole[TILES * P:N].rearrange("(p o) -> p o", o=1)
    return cols[:, bass.ds(g * GT, GT)]


def gather_tile(nc, to, table, idx):
    return nc.gpsimd.indirect_dma_start(out=to, out_offset=None, in_=table,
                                        in_offset=bass.IndirectOffsetOnAxis(ap=idx, axis=0))


class PoolTakes:

    def __init__(self, nc, tag):
        self.nc, self.tag = nc, tag
        self.rings = []
        self.made = 0

    def counter(self, first, by):
        self.made += 1
        reg = self.nc.gpsimd.alloc_register(f"{self.tag}take{self.made}")
        self.nc.gpsimd.reg_mov(reg, first - by)
        return reg, by

    def ring(self, first, ring):
        self.rings.append((*self.counter(first, ring.inc), ring.ring))
        return self.rings[-1][0:2]

    def next_group(self, k, counters):
        for reg, by in counters + [(reg, by) for reg, by, ring in self.rings if k % ring == 0]:
            self.nc.gpsimd.reg_add(reg, reg, by)

    def value(self, at):
        return self.nc.gpsimd.snap(at[0])


class RowNorm:

    def __init__(self, ctx, nc, c, name, steady, factor=None):
        def sb(what, shape):
            return ctx.sbuf(f"{name}_{what}", shape, F32)
        self.nc, self.c, self.factor, self.steady = nc, c, factor, steady
        self.stat = sb("stat", [P, 2, GT, 6])
        self.mv = sb("mv", [P, 2, GT, 2])
        self.dev = sb("dev", [P, 2, GT])
        self.root = sb("root", [P, 2, GT])
        self.bias = sb("bias", [P, 2, GT])
        self.stat_made = Count(ctx, nc, f"{name}_stat_made")
        self.mv_made = Count(ctx, nc, f"{name}_mv_made")
        self.dev_made = Count(ctx, nc, f"{name}_dev_made")
        self.root_made = Count(ctx, nc, f"{name}_root_made")
        self.bias_made = Count(ctx, nc, f"{name}_bias_made")

    def records(self, g, b, T, rows, tile):
        for j in range(T):
            last = self.nc.vector.bn_stats(self.stat[0:rows, b, j, :], tile(j))
        last.then_inc(self.stat_made.sem, 1)

    def moments(self, g, b, T, rows):
        wait_apart(self.nc.vector, self.steady, (self.stat_made.sem, self.stat_made.done(g)))
        for j in range(T):
            last = self.nc.vector.bn_aggr(self.mv[0:rows, b, j, :], self.stat[0:rows, b, j, :])
        last.then_inc(self.mv_made.sem, 1)

    def deviate(self, act, g, b, T, rows):
        act.wait_ge(self.mv_made.sem, self.mv_made.done(g))
        act.wait_ge(self.root_made.sem, self.root_made.free(g, 2))
        bias, factor = (self.c.eps[0:rows, :], 1.0) if self.factor is None else (0.0, self.factor)
        self.nc.scalar.activation(self.dev[0:rows, b, 0:T], self.mv[0:rows, b, 0:T, 1], ACT.Sqrt, bias=bias,
                                  scale=factor).then_inc(self.dev_made.sem, 1)

    def invert(self, dve, g, b, T, rows):
        dve.wait_ge(self.dev_made.sem, self.dev_made.done(g))
        self.nc.vector.reciprocal(self.root[0:rows, b, 0:T], self.dev[0:rows, b, 0:T]).then_inc(self.root_made.sem, 1)

    def make_bias(self, dve, g, b, T, rows):
        if self.factor is None:
            dve.wait_ge(self.root_made.sem, self.root_made.done(g))
            self.nc.vector.scalar_tensor_tensor(self.bias[0:rows, b, 0:T], self.mv[0:rows, b, 0:T, 0], -1.0,
                                                self.root[0:rows, b, 0:T], ALU.mult, ALU.mult)\
                .then_inc(self.bias_made.sem, 1)

    def apply(self, act, g, b, T, rows, tile, to):
        biased = self.factor is None
        if biased:
            act.wait_ge(self.bias_made.sem, self.bias_made.done(g))
        else:
            act.wait_ge(self.root_made.sem, self.root_made.done(g))
        for j in range(T):
            bias = self.bias[0:rows, b, j:j + 1] if biased else 0.0
            last = self.nc.scalar.activation(to(j), tile(j), ACT.Identity if biased else ACT.Copy, bias=bias,
                                             scale=self.root[0:rows, b, j:j + 1])
        return last


def measure_rows(*parts):
    for norm, g, b, T, rows, tile in parts:
        norm.records(g, b, T, rows, tile)
    for norm, g, b, T, rows, _ in parts:
        norm.moments(g, b, T, rows)


def finish_rows(dve, *parts):
    for norm, g, b, T, rows in parts:
        norm.invert(dve, g, b, T, rows)
    for norm, g, b, T, rows in parts:
        norm.make_bias(dve, g, b, T, rows)


def take_sums(nc, c, steady, taken, used, sums, g, k, T):
    wait_apart(nc.gpsimd, steady, (used.sem, used.free(g, 2)))
    tiles = GT if T == GT else 2
    at = c.node_tab[:, bass.ds(g * GT, tiles), :]
    nc.gpsimd.tensor_copy(sums[:, k % 2, 0:tiles, :], at).then_inc(taken.sem, 1)
    wait_apart(nc.gpsimd, steady, (taken.sem, taken.done(g)))
    nc.gpsimd.tensor_copy(at, c.zeros[:, 0:tiles, 0:W])


def transposed(nc, to, T, rows, cols, tile, ident):
    for j in range(T):
        last = nc.tensor.transpose(to[0:cols, j * P:j * P + rows], tile(j), ident[0:rows, 0:rows])
    return last


def mix_nodes(nc, c, x, x_out, layer, first):
    with Phase(nc) as ctx:
        def sb(name, shape, dt=F32):
            return ctx.sbuf(name, shape, dt)

        turned_in = first is None
        x_in = sb("x_in", [W, RING, GT * P] if turned_in else [P, RING, GT, W])
        sums = sb("sums", [P, 2, GT, W])
        x_t = None if turned_in else sb("x_t", [W, 2, GT * P])
        s_t = sb("s_t", [W, 2, GT * P])
        res = sb("res", [P, RING, GT, D])
        x_t_ps = ctx.psum("x_t_ps", [P, 2, 512], F32)
        s_t_ps = ctx.psum("s_t_ps", [P, 2, 512], F32)
        y_ps = ctx.psum("y_ps", [P, 2, 512], F32)
        ones_set = ctx.semaphore("ones_set")
        loaded = DmaRing(ctx, nc, "loaded")
        stored = DmaRing(ctx, nc, "stored")
        taken = Count(ctx, nc, "taken")
        x_turned = Count(ctx, nc, "x_turned")
        s_turned = Count(ctx, nc, "s_turned")
        x_copied = Count(ctx, nc, "x_copied")
        s_copied = Count(ctx, nc, "s_copied")
        mixed = Count(ctx, nc, "mixed")
        res_made = Count(ctx, nc, "res_made")
        spread = RowNorm(ctx, nc, c, "spread", ones_set, factor=D / (D - 1))
        if first is not None:
            first_in = sb("first_in", [P, RING, GT, D])
            z = sb("z", [P, 2, GT, D])
            first_loaded = DmaRing(ctx, nc, "first_loaded")
            z_made = Count(ctx, nc, "z_made")
            norm = RowNorm(ctx, nc, c, "norm", ones_set)
        block = ctx.enter_context(nc.Block())

        @block.sync
        def _(sp):
            def load(i, k, T, rows):
                g = i * GR + k
                if turned_in:
                    wait_apart(nc.sync, ones_set, (mixed.sem, mixed.free(g, RING)))
                    sp.dma_start(x_in[0:D, k % RING, 0:T * rows], group_cols(x, g, rows)).then_inc(loaded.sem(k), 16)
                else:
                    wait_apart(nc.sync, ones_set, (x_turned.sem, x_turned.free(g, RING)))
                    sp.dma_start(x_in[0:rows, k % RING, 0:T, 0:D], group_rows(x, g, T, rows))\
                        .then_inc(loaded.sem(k), 16)
                if first is not None:
                    wait_apart(nc.sync, ones_set, (z_made.sem, z_made.free(g, RING)))
                    sp.dma_start(first_in[0:rows, k % RING, 0:T, :], group_rows(first, g, T, rows))\
                        .then_inc(first_loaded.sem(k), 16)
            sp.wait_ge(ones_set, 1)
            laps(nc.sync, [(0, load)])
            wait_stores(sp, stored)

        @block.gpsimd
        def _(pool):
            def take(i, k, T, rows):
                take_sums(nc, c, ones_set, taken, s_turned, sums, i * GR + k, k, T)
            laps(nc.gpsimd, [(0, take)])

        @block.tensor
        def _(pe):
            def turn(i, k, T, rows):
                g = i * GR + k
                if not turned_in:
                    pe.wait_ge(loaded.sem(k), loaded.done(i, k))
                    pe.wait_ge(x_copied.sem, x_copied.free(g, 2))
                    transposed(nc, x_t_ps[:, k % 2, :], T, rows, W, lambda j: x_in[0:rows, k % RING, j, :], c.ident)\
                        .then_inc(x_turned.sem, 1)
                pe.wait_ge(taken.sem, taken.done(g))
                pe.wait_ge(s_copied.sem, s_copied.free(g, 2))
                transposed(nc, s_t_ps[:, k % 2, :], T, rows, W, lambda j: sums[0:rows, k % 2, j, :], c.ident)\
                    .then_inc(s_turned.sem, 1)

            def mix(i, k, T, rows):
                g = i * GR + k
                if turned_in:
                    pe.wait_ge(loaded.sem(k), loaded.done(i, k))
                    x_of = x_in[:, k % RING, :]
                else:
                    pe.wait_ge(x_copied.sem, x_copied.done(g))
                    x_of = x_t[:, k % 2, :]
                pe.wait_ge(s_copied.sem, s_copied.done(g))
                used = res_made if first is None else z_made
                pe.wait_ge(used.sem, used.free(g, 2))
                for j in range(T):
                    to = y_ps[0:rows, k % 2, j * D:(j + 1) * D]
                    nc.tensor.matmul(to, x_of[:, j * P:j * P + rows], c.mix_self[layer][:], start=True, stop=False)
                    last = nc.tensor.matmul(to, s_t[:, k % 2, j * P:j * P + rows], c.mix_near[layer][:],
                                            start=False, stop=True)
                last.then_inc(mixed.sem, 1)
            pe.wait_ge(ones_set, 1)
            laps(nc.tensor, [(1, turn), (0, mix)])

        @block.scalar
        def _(act):
            def copy_x(i, k, T, rows):
                g = i * GR + k
                act.wait_ge(x_turned.sem, x_turned.done(g))
                act.wait_ge(mixed.sem, mixed.free(g, 2))
                nc.scalar.copy(x_t[:, k % 2, 0:(T - 1) * P + rows], x_t_ps[0:W, k % 2, 0:(T - 1) * P + rows])\
                    .then_inc(x_copied.sem, 1)

            def scale(i, k, T, rows):
                g = i * GR + k
                act.wait_ge(stored.sem(k), stored.free(i, k))
                spread.apply(act, g, k % 2, T, rows, lambda j: y_ps[0:rows, k % 2, j * D:(j + 1) * D],
                             lambda j: res[0:rows, k % RING, j, :]).then_inc(res_made.sem, 1)

            def normalise(i, k, T, rows):
                g = i * GR + k
                act.wait_ge(stored.sem(k), stored.free(i, k))
                norm.apply(act, g, k % 2, T, rows, lambda j: z[0:rows, k % 2, j, :],
                           lambda j: res[0:rows, k % RING, j, :]).then_inc(res_made.sem, 1)

            def store(i, k, T, rows):
                g = i * GR + k
                act.wait_ge(res_made.sem, res_made.done(g))
                nc.scalar.dma_start(group_rows(x_out, g, T, rows), res[0:rows, k % RING, 0:T, :])\
                    .then_inc(stored.sem(k), 16)

            def deviate_y(i, k, T, rows):
                spread.deviate(act, i * GR + k, k % 2, T, rows)

            def deviate_z(i, k, T, rows):
                norm.deviate(act, i * GR + k, k % 2, T, rows)

            if first is None:
                laps(nc.scalar, [(0, scale), (1, deviate_y), (0, store)])
            else:
                laps(nc.scalar, [(0, normalise), (2, deviate_y), (1, deviate_z), (4, copy_x), (0, store)])

        @block.vector
        def _(dve):
            def copy_s(i, k, T, rows):
                g = i * GR + k
                dve.wait_ge(s_turned.sem, s_turned.done(g))
                dve.wait_ge(mixed.sem, mixed.free(g, 2))
                nc.vector.tensor_copy(s_t[:, k % 2, 0:(T - 1) * P + rows], s_t_ps[0:W, k % 2, 0:(T - 1) * P + rows])\
                    .then_inc(s_copied.sem, 1)

            def y_part(i, k, T, rows):
                g = i * GR + k
                dve.wait_ge(mixed.sem, mixed.done(g))
                return spread, g, k % 2, T, rows, lambda j: y_ps[0:rows, k % 2, j * D:(j + 1) * D]

            def z_part(i, k, T, rows):
                g = i * GR + k
                dve.wait_ge(z_made.sem, z_made.done(g))
                return norm, g, k % 2, T, rows, lambda j: z[0:rows, k % 2, j, :]

            def measure(i, k, T, rows):
                measure_rows(y_part(i, k, T, rows))

            def join(i, k, T, rows):
                g = i * GR + k
                dve.wait_ge(spread.root_made.sem, spread.root_made.done(g))
                dve.wait_ge(first_loaded.sem(k), first_loaded.done(i, k))
                dve.wait_ge(res_made.sem, res_made.free(g, 2))
                for j in range(T):
                    last = nc.vector.scalar_tensor_tensor(z[0:rows, k % 2, j, :], y_ps[0:rows, k % 2, j * D:(j + 1) * D],
                                                          spread.root[0:rows, k % 2, j:j + 1],
                                                          first_in[0:rows, k % RING, j, :], ALU.mult, ALU.add)
                last.then_inc(z_made.sem, 1)

            def measure_both(of_y, of_z):
                measure_rows(*([y_part(*of_y)] if of_y else []), *([z_part(*of_z)] if of_z else []))

            def finish_y(i, k, T, rows):
                g = i * GR + k
                dve.wait_ge(res_made.sem, res_made.free(g, 2))
                finish_rows(dve, (spread, g, k % 2, T, rows))

            def finish_both(of_y, of_z):
                parts = [(norm_of, of[0] * GR + of[1], of[1] % 2, *of[2:])
                         for norm_of, of in ((spread, of_y), (norm, of_z)) if of]
                finish_rows(dve, *parts)
            nc.vector.memset(x_in[D:W, :, :] if turned_in else x_in[:, :, :, D:W], 1.0).then_inc(ones_set, 1)
            if first is None:
                laps(nc.vector, [(0, finish_y), (1, measure), (3, copy_s)])
            else:
                laps(nc.vector, [((1, 0), finish_both), (1, join), ((2, 1), measure_both), (4, copy_s)])


def attention_edges(nc, c, x, edge4_t):
    with Phase(nc) as ctx:
        def sb(name, shape, dt=F32):
            return ctx.sbuf(name, shape, dt)

        def ps(name):
            return ctx.psum(name, [P, 512], F32)

        idx = sb("idx", [P, GR, 2, GT], I32)
        sources = sb("sources", [P, RING, GT * P], I32)
        rows_s = sb("rows_s", [P, RING, GT, D])
        rows_d = sb("rows_d", [P, RING, GT, D])
        s_t = sb("s_t", [D, 2, GT * P])
        d_t = sb("d_t", [D, 2, GT * P])
        q = sb("q", [P, GT, D])
        qk = sb("qk", [P, GT, D])
        score = sb("score", [P, GT * HEADS])
        weight = sb("weight", [P, 2, GT * HEADS])
        pay = sb("pay", [P, 2, GT, M])
        same = sb("same", [P, RING, GT, P])
        before = sb("before", [P, GT, P])
        repeats = sb("repeats", [P, RING, GT])
        target_f = sb("target_f", [P, RING, GT])
        target = sb("target", [P, RING, GT], I32)
        total = sb("total", [P, RING, GT, M])
        dump_rows = sb("dump_rows", [P, 1], I32)
        s_t_ps, d_t_ps, q_ps, k_ps, v_ps, total_ps = (ps(n) for n in ("s_t_ps", "d_t_ps", "q_ps", "k_ps", "v_ps", "total_ps"))
        ready = ctx.semaphore("ready")
        idx_in = DmaRing(ctx, nc, "idx_in", 2, ring=GR)
        sources_in = DmaRing(ctx, nc, "sources_in")
        gathered = DmaRing(ctx, nc, "gathered", 2 * GT, pool=True)
        scattered = [ctx.semaphore(f"scattered{h}") for h in range(2)]
        dump_set = ctx.semaphore("dump_set")
        landed = Count(ctx, nc, "landed")
        turned = Count(ctx, nc, "turned")
        s_copied = Count(ctx, nc, "s_copied")
        d_copied = Count(ctx, nc, "d_copied")
        projected = Count(ctx, nc, "projected")
        q_copied = Count(ctx, nc, "q_copied")
        qk_made = Count(ctx, nc, "qk_made")
        scored = Count(ctx, nc, "scored")
        clipped = Count(ctx, nc, "clipped")
        weighed = Count(ctx, nc, "weighed")
        paid = Count(ctx, nc, "paid")
        matched = Count(ctx, nc, "matched")
        counted = Count(ctx, nc, "counted")
        aimed_f = Count(ctx, nc, "aimed_f")
        aimed = Count(ctx, nc, "aimed")
        totalled = Count(ctx, nc, "totalled")
        total_copied = Count(ctx, nc, "total_copied")
        edge_norm = EdgeNorm(ctx, nc, c, edge4_t, ready)
        block = ctx.enter_context(nc.Block())

        @block.sync
        def _(sp):
            def load(i, k, T, rows):
                g = i * GR + k
                wait_apart(nc.sync, ready, (turned.sem, turned.free(g, GR)))
                sp.dma_start(idx[0:rows, k % GR, 0, 0:T], idx_cols(c.src_cols, c.src, g, rows))\
                    .then_inc(idx_in.sem(k), 16)
                sp.dma_start(idx[0:rows, k % GR, 1, 0:T], idx_cols(c.dst_cols, c.dst, g, rows))\
                    .then_inc(idx_in.sem(k), 16)

            def load_sources(i, k, T, rows):
                g = i * GR + k
                wait_apart(nc.sync, ready, (matched.sem, matched.free(g, RING)))
                n = T * rows
                row = (c.src[TILES * P:N] if rows == TAIL else c.src[bass.ds(g * (GT * P), GT * P)])
                sp.dma_start(sources[0:rows, k % RING, 0:n], row.rearrange("(o f) -> o f", o=1).to_broadcast([rows, n]))\
                    .then_inc(sources_in.sem(k), 16)
            sp.wait_ge(ready, 1)
            laps(nc.sync, [(3, load), (0, load_sources), (0, edge_norm.load)])

        @block.gpsimd
        def _(pool):
            take = PoolTakes(nc, ctx.tag)
            idx_at = take.ring(idx_in.done(0, 0), idx_in)
            turned_at = take.counter(turned.free(0, RING), 1)
            total_at = take.counter(total_copied.done(0), 1)
            added = [nc.gpsimd.alloc_register(f"added{h}") for h in range(2)]
            nc.gpsimd.iota(dump_rows[:], pattern=[[0, 1]], base=DUMP, channel_multiplier=1).then_inc(dump_set, 1)
            pool.wait_ge(dump_set, 1)
            for h in range(2):
                nc.gpsimd.indirect_dma_start(
                    out=c.att[h], out_offset=bass.IndirectOffsetOnAxis(ap=dump_rows[:], axis=0),
                    in_=flat(c.zeros[:])[:, 0:M], in_offset=None, compute_op=ALU.add).then_inc(scattered[h], 16)
                nc.gpsimd.reg_mov(added[h], 16)

            def gather(side, j, k, T, rows):
                to = (rows_s, rows_d)[side]
                gather_tile(nc, to[0:rows, k % RING, j, :], x, idx[0:rows, k % GR, side, j:j + 1])\
                    .then_inc(gathered.sem(k), 16 * GT if T == 1 else 16)

            def scatter(j, k, T, rows, total_value):
                h = (GT * k + j) % 2
                added_value = nc.gpsimd.snap(added[h])
                pool.wait_ge(ready, 1)
                pool.wait_ge(scattered[h], added_value)
                if j == 0:
                    pool.wait_ge(total_copied.sem, total_value)
                nc.gpsimd.sem_inc(landed.sem, 1)
                nc.gpsimd.indirect_dma_start(
                    out=c.att[h], out_offset=bass.IndirectOffsetOnAxis(ap=target[0:rows, k % RING, j:j + 1], axis=0),
                    in_=total[0:rows, k % RING, j, :], in_offset=None, compute_op=ALU.add).then_inc(scattered[h], 16)
                nc.gpsimd.reg_add(added[h], added[h], 16)

            def move(of_gather, of_scatter):
                if of_gather:
                    _, k, T, rows = of_gather
                    take.next_group(k, [turned_at])
                    idx_value, turned_value = take.value(idx_at), take.value(turned_at)
                    pool.wait_ge(ready, 1)
                    pool.wait_ge(idx_in.sem(k), idx_value)
                    pool.wait_ge(turned.sem, turned_value)
                    for side in range(2):
                        gather(side, 0, k, T, rows)
                if of_scatter:
                    take.next_group(1, [total_at])
                    total_value = take.value(total_at)
                for j in range(GT):
                    if of_scatter and j < of_scatter[2]:
                        scatter(j, *of_scatter[1:], total_value)
                    if of_gather and 0 < j + 1 < of_gather[2]:
                        for side in range(2):
                            gather(side, j + 1, *of_gather[1:])
            laps(nc.gpsimd, [((4, 0), move)])
            for h in range(2):
                pool.wait_ge(scattered[h], 16 * (1 + (TILES + 2 - h) // 2))

        @block.tensor
        def _(pe):
            def turn(i, k, T, rows):
                g = i * GR + k
                pe.wait_ge(gathered.sem(k), gathered.done(i, k))
                pe.wait_ge(s_copied.sem, s_copied.free(g, 1))
                transposed(nc, s_t_ps, T, rows, D, lambda j: rows_s[0:rows, k % RING, j, :], c.ident)
                pe.wait_ge(d_copied.sem, d_copied.free(g, 1))
                transposed(nc, d_t_ps, T, rows, D, lambda j: rows_d[0:rows, k % RING, j, :], c.ident)\
                    .then_inc(turned.sem, 1)

            def project(i, k, T, rows):
                g = i * GR + k
                pe.wait_ge(s_copied.sem, s_copied.done(g))
                pe.wait_ge(d_copied.sem, d_copied.done(g))
                pe.wait_ge(paid.sem, paid.free(g, 1))
                for j in range(T):
                    for n, (to, side) in enumerate(((q_ps, s_t), (k_ps, d_t), (v_ps, d_t))):
                        last = nc.tensor.matmul(to[0:rows, j * D:(j + 1) * D], side[:, k % 2, j * P:j * P + rows],
                                                c.qkv[:, n * D:(n + 1) * D], start=True, stop=True)
                last.then_inc(projected.sem, 1)

            def sum_up(i, k, T, rows):
                g = i * GR + k
                pe.wait_ge(paid.sem, paid.done(g))
                pe.wait_ge(total_copied.sem, total_copied.free(g, 1))
                for j in range(T):
                    last = nc.tensor.matmul(total_ps[0:rows, j * M:(j + 1) * M], same[0:rows, k % RING, j, 0:rows],
                                            pay[0:rows, k % 2, j, :], start=True, stop=True)
                last.then_inc(totalled.sem, 1)
            pe.wait_ge(ready, 1)

            def multiply(i, k, T, rows):
                edge_norm.multiply(pe, i, k, T, rows)
            laps(nc.tensor, [(2, turn), (1, project), (0, sum_up), (0, multiply)])
            edge_norm.fold_on_tensor(pe)

        @block.scalar
        def _(act):
            def copy_s(i, k, T, rows):
                g = i * GR + k
                act.wait_ge(turned.sem, turned.done(g))
                act.wait_ge(projected.sem, projected.free(g, 2))
                n = (T - 1) * P + rows
                nc.scalar.copy(s_t[:, k % 2, 0:n], s_t_ps[0:D, 0:n]).then_inc(s_copied.sem, 1)

            def copy_q(i, k, T, rows):
                g = i * GR + k
                act.wait_ge(projected.sem, projected.done(g))
                act.wait_ge(qk_made.sem, qk_made.free(g, 1))
                nc.scalar.copy(flat(q[0:rows, 0:T, :]), q_ps[0:rows, 0:T * D]).then_inc(q_copied.sem, 1)

            def weigh(i, k, T, rows):
                g = i * GR + k
                act.wait_ge(clipped.sem, clipped.done(g))
                act.wait_ge(paid.sem, paid.free(g, 2))
                nc.scalar.activation(weight[0:rows, k % 2, 0:T * HEADS], score[0:rows, 0:T * HEADS], ACT.Exp)\
                    .then_inc(weighed.sem, 1)

            def copy_total(i, k, T, rows):
                g = i * GR + k
                act.wait_ge(totalled.sem, totalled.done(g))
                act.wait_ge(aimed.sem, aimed.done(g))
                act.wait_ge(landed.sem, landed.free(g * GT, GT * (RING - 1) - 1))
                nc.scalar.copy(flat(total[0:rows, k % RING, 0:T, :]), total_ps[0:rows, 0:T * M]).then_inc(total_copied.sem, 1)

            def rectify(i, k, T, rows):
                edge_norm.rectify(act, i, k, T, rows)
            laps(nc.scalar, [(2, copy_s), (1, copy_q), (1, weigh), (0, copy_total), (0, rectify)])
            edge_norm.norm.on_scalar(act)

        @block.vector
        def _(dve):
            def match(i, k, T, rows):
                g = i * GR + k
                dve.wait_ge(sources_in.sem(k), sources_in.done(i, k))
                dve.wait_ge(totalled.sem, totalled.free(g, RING))
                for j in range(T):
                    last = nc.vector.tensor_scalar(same[0:rows, k % RING, j, 0:rows],
                                                   sources[0:rows, k % RING, j * P:j * P + rows],
                                                   c.src_f[0:rows, bass.ds(g * GT + j, 1)], None, ALU.is_equal)
                last.then_inc(matched.sem, 1)
                dve.wait_ge(matched.sem, matched.done(g))
                dve.wait_ge(total_copied.sem, total_copied.free(g, RING))
                for j in range(T):
                    last = nc.vector.scalar_tensor_tensor(before[0:rows, j, 0:rows], same[0:rows, k % RING, j, 0:rows], 1.0,
                                                          c.lower[0:rows, 0:rows], ALU.mult, ALU.mult,
                                                          accum_out=repeats[0:rows, k % RING, j:j + 1])
                last.then_inc(counted.sem, 1)
                dve.wait_ge(counted.sem, counted.done(g))
                nc.vector.scalar_tensor_tensor(target_f[0:rows, k % RING, 0:T], repeats[0:rows, k % RING, 0:T], 0.0,
                                               c.to_dump[0:rows, bass.ds(g * GT, T)], ALU.is_gt, ALU.mult)\
                    .then_inc(aimed_f.sem, 1)
                dve.wait_ge(aimed_f.sem, aimed_f.done(g))
                dve.wait_ge(landed.sem, landed.free(g * GT, GT * (RING - 1) - 1))
                nc.vector.tensor_tensor(target[0:rows, k % RING, 0:T], target_f[0:rows, k % RING, 0:T],
                                        c.src_f[0:rows, bass.ds(g * GT, T)], ALU.add).then_inc(aimed.sem, 1)

            def copy_d(i, k, T, rows):
                g = i * GR + k
                dve.wait_ge(turned.sem, turned.done(g))
                dve.wait_ge(projected.sem, projected.free(g, 2))
                n = (T - 1) * P + rows
                nc.vector.tensor_copy(d_t[:, k % 2, 0:n], d_t_ps[0:D, 0:n]).then_inc(d_copied.sem, 1)

            def score_edges(i, k, T, rows):
                g = i * GR + k
                dve.wait_ge(q_copied.sem, q_copied.done(g))
                dve.wait_ge(scored.sem, scored.free(g, 1))
                nc.vector.tensor_tensor(flat(qk[0:rows, 0:T, :]), flat(q[0:rows, 0:T, :]), k_ps[0:rows, 0:T * D],
                                        ALU.mult).then_inc(qk_made.sem, 1)
                dve.wait_ge(qk_made.sem, qk_made.done(g))
                dve.wait_ge(weighed.sem, weighed.free(g, 1))
                nc.vector.tensor_reduce(score[0:rows, 0:T * HEADS],
                                        flat(qk[0:rows, 0:T, :]).rearrange("p (h f) -> p h f", f=DH), AX.X, ALU.add)\
                    .then_inc(scored.sem, 1)
                dve.wait_ge(scored.sem, scored.done(g))
                nc.vector.tensor_scalar(score[0:rows, 0:T * HEADS], score[0:rows, 0:T * HEADS], -10.0, 10.0,
                                        ALU.max, ALU.min).then_inc(clipped.sem, 1)

            def pay_edges(i, k, T, rows):
                g = i * GR + k
                dve.wait_ge(weighed.sem, weighed.done(g))
                dve.wait_ge(totalled.sem, totalled.free(g, 2))
                w = weight[0:rows, k % 2, 0:T * HEADS]
                nc.vector.tensor_copy(pay[0:rows, k % 2, 0:T, D:M], w.rearrange("p (t h) -> p t h", h=HEADS))
                for j in range(T):
                    last = nc.vector.tensor_tensor(
                        pay[0:rows, k % 2, j, 0:D].rearrange("p (h f) -> p h f", f=DH),
                        v_ps[0:rows, j * D:(j + 1) * D].rearrange("p (h f) -> p h f", f=DH),
                        w[:, j * HEADS:(j + 1) * HEADS].rearrange("p (h o) -> p h o", o=1).to_broadcast([rows, HEADS, DH]),
                        ALU.mult)
                last.then_inc(paid.sem, 1)

            def count(i, k, T, rows):
                edge_norm.count(dve, i, k, T, rows)
            nc.vector.memset(before[:], 0.0)
            edge_norm.set_up(ready)
            laps(nc.vector, [(3, match), (3, copy_d), (2, score_edges), (2, pay_edges), (0, count)])
            edge_norm.fold_on_vector(dve)


def attention_nodes(nc, c, x, x_out):
    with Phase(nc) as ctx:
        def sb(name, shape, dt=F32):
            return ctx.sbuf(name, shape, dt)

        att_in = sb("att_in", [P, GR, GT, M])
        att_in2 = sb("att_in2", [P, GR, GT, M])
        x_in = sb("x_in", [P, GR, GT, D])
        share = sb("share", [P, 2, GT, HEADS])
        seen = sb("seen", [P, 2, GT, D])
        z = sb("z", [P, 2, GT, D])
        res = sb("res", [P, RING, GT, D])
        x_t = sb("x_t", [D, 2, GT * P])
        f = sb("f", [D, 2, GT * P])
        x_t_ps = ctx.psum("x_t_ps", [P, 2, 512], F32)
        f_ps = ctx.psum("f_ps", [P, 2, 512], F32)
        ready = ctx.semaphore("ready")
        loaded = DmaRing(ctx, nc, "loaded", 3, ring=GR)
        att_whole = Count(ctx, nc, "att_whole")
        stored = DmaRing(ctx, nc, "stored")
        floored = Count(ctx, nc, "floored")
        shared = Count(ctx, nc, "shared")
        seen_made = Count(ctx, nc, "seen_made")
        z_made = Count(ctx, nc, "z_made")
        res_made = Count(ctx, nc, "res_made")
        turned = Count(ctx, nc, "turned")
        copied = Count(ctx, nc, "copied")
        projected = Count(ctx, nc, "projected")
        rectified = Count(ctx, nc, "rectified")
        counted = Count(ctx, nc, "counted")
        norm = RowNorm(ctx, nc, c, "norm", ready)
        block = ctx.enter_context(nc.Block())

        @block.sync
        def _(sp):
            def load(i, k, T, rows):
                g = i * GR + k
                wait_apart(nc.sync, ready, (z_made.sem, z_made.free(g, GR)))
                for h, to in enumerate((att_in, att_in2)):
                    sp.dma_start(to[0:rows, k % GR, 0:T, :], packed_rows(c.att[h], g, T, rows)).then_inc(loaded.sem(k), 16)
                sp.dma_start(x_in[0:rows, k % GR, 0:T, :], packed_rows(x, g, T, rows)).then_inc(loaded.sem(k), 16)
            sp.wait_ge(ready, 1)
            laps(nc.sync, [(0, load)])
            wait_stores(sp, stored)

        @block.tensor
        def _(pe):
            def turn(i, k, T, rows):
                g = i * GR + k
                pe.wait_ge(res_made.sem, res_made.done(g))
                pe.wait_ge(copied.sem, copied.free(g, 2))
                transposed(nc, x_t_ps[:, k % 2, :], T, rows, D, lambda j: res[0:rows, k % RING, j, :], c.ident)\
                    .then_inc(turned.sem, 1)

            def project(i, k, T, rows):
                g = i * GR + k
                pe.wait_ge(copied.sem, copied.done(g))
                pe.wait_ge(rectified.sem, rectified.free(g, 2))
                nc.tensor.matmul(f_ps[0:D, k % 2, 0:T * rows], c.w_node[:], x_t[:, k % 2, 0:T * rows],
                                 start=True, stop=True).then_inc(projected.sem, 1)
            laps(nc.tensor, [(2, turn), (0, project)])

        @block.scalar
        def _(act):
            def normalise(i, k, T, rows):
                g = i * GR + k
                act.wait_ge(stored.sem(k), stored.free(i, k))
                act.wait_ge(turned.sem, turned.free(g, RING))
                norm.apply(act, g, k % 2, T, rows, lambda j: z[0:rows, k % 2, j, :],
                           lambda j: res[0:rows, k % RING, j, :]).then_inc(res_made.sem, 1)

            def copy_x(i, k, T, rows):
                g = i * GR + k
                act.wait_ge(turned.sem, turned.done(g))
                act.wait_ge(projected.sem, projected.free(g, 2))
                nc.scalar.copy(x_t[:, k % 2, 0:T * rows], x_t_ps[0:D, k % 2, 0:T * rows]).then_inc(copied.sem, 1)

            def rectify(i, k, T, rows):
                g = i * GR + k
                act.wait_ge(projected.sem, projected.done(g))
                act.wait_ge(counted.sem, counted.free(g, 2))
                nc.scalar.activation(f[:, k % 2, 0:T * rows], f_ps[0:D, k % 2, 0:T * rows], ACT.Relu,
                                     bias=column(c, "b_node")).then_inc(rectified.sem, 1)
            def store(i, k, T, rows):
                g = i * GR + k
                act.wait_ge(res_made.sem, res_made.done(g))
                nc.scalar.dma_start(packed_rows(x_out, g, T, rows), res[0:rows, k % RING, 0:T, :])\
                    .then_inc(stored.sem(k), 16)

            def deviate(i, k, T, rows):
                norm.deviate(act, i * GR + k, k % 2, T, rows)

            laps(nc.scalar, [(4, normalise), (2, copy_x), (0, rectify), (5, deviate), (4, store)])

        @block.gpsimd
        def _(pool):
            def see(i, k, T, rows):
                g = i * GR + k
                pool.wait_ge(shared.sem, shared.done(g))
                pool.wait_ge(z_made.sem, z_made.free(g, 2))
                for j in range(T):
                    last = nc.gpsimd.tensor_tensor(
                        seen[0:rows, k % 2, j, :].rearrange("p (h f) -> p h f", f=DH),
                        att_in[0:rows, k % GR, j, 0:D].rearrange("p (h f) -> p h f", f=DH),
                        share[0:rows, k % 2, j, :].rearrange("p (h o) -> p h o", o=1).to_broadcast([rows, HEADS, DH]),
                        ALU.mult)
                last.then_inc(seen_made.sem, 1)
            laps(nc.gpsimd, [(0, see)])

        @block.vector
        def _(dve):
            nc.vector.memset(share[:], 0.0).then_inc(ready, 1)

            def add_up(i, k, T, rows):
                g = i * GR + k
                dve.wait_ge(loaded.sem(k), loaded.done(i, k))
                whole = flat(att_in[0:rows, k % GR, 0:T, :])
                nc.vector.tensor_tensor(whole, whole, flat(att_in2[0:rows, k % GR, 0:T, :]), ALU.add)\
                    .then_inc(att_whole.sem, 1)

            def put_floor(i, k, T, rows):
                g = i * GR + k
                dve.wait_ge(att_whole.sem, att_whole.done(g))
                dve.wait_ge(seen_made.sem, seen_made.free(g, 2))
                at = share[0:rows, k % 2, 0:T, :]
                nc.vector.tensor_scalar(at, att_in[0:rows, k % GR, 0:T, D:M], 1e-8, None, ALU.add)\
                    .then_inc(floored.sem, 1)

            def divide(i, k, T, rows):
                g = i * GR + k
                at = share[0:rows, k % 2, 0:T, :]
                dve.wait_ge(floored.sem, floored.done(g))
                nc.vector.reciprocal(at, at).then_inc(shared.sem, 1)

            def join(i, k, T, rows):
                g = i * GR + k
                dve.wait_ge(seen_made.sem, seen_made.done(g))
                dve.wait_ge(res_made.sem, res_made.free(g, 2))
                nc.vector.scalar_tensor_tensor(flat(z[0:rows, k % 2, 0:T, :]), flat(x_in[0:rows, k % GR, 0:T, :]), 2.0,
                                               flat(seen[0:rows, k % 2, 0:T, :]), ALU.mult, ALU.add)\
                    .then_inc(z_made.sem, 1)

            def record_z(i, k, T, rows):
                g = i * GR + k
                dve.wait_ge(z_made.sem, z_made.done(g))
                norm.records(g, k % 2, T, rows, lambda j: z[0:rows, k % 2, j, :])

            def moments(i, k, T, rows):
                norm.moments(i * GR + k, k % 2, T, rows)

            def invert(i, k, T, rows):
                norm.invert(dve, i * GR + k, k % 2, T, rows)

            def make_bias(i, k, T, rows):
                norm.make_bias(dve, i * GR + k, k % 2, T, rows)

            def count(i, k, T, rows):
                g = i * GR + k
                dve.wait_ge(rectified.sem, rectified.done(g))
                nc.vector.bn_stats(record(c.stat, g), f[:, k % 2, 0:T * rows]).then_inc(counted.sem, 1)
            laps(nc.vector, [(5, invert), (9, add_up), (5, make_bias), (6, join), (8, put_floor), (6, record_z),
                             (8, divide), (6, moments), (0, count)])


def message_edges(nc, c, x, edge4_t):
    with Phase(nc) as ctx:
        def sb(name, shape, dt=F32):
            return ctx.sbuf(name, shape, dt)

        idx = sb("idx", [P, GR, 2, GT], I32)
        rows_s = sb("rows_s", [P, RING, GT, D])
        rows_d = sb("rows_d", [P, RING, GT, D])
        feats = sb("feats", [5, RING, GT * P])
        s_t = sb("s_t", [W, 2, GT * P])
        d_t = sb("d_t", [D, 2, GT * P])
        f_t = sb("f_t", [D, 2, GT * P])
        m_t = sb("m_t", [D, 2, GT * P])
        msg = sb("msg", [P, 2, GT, W])
        s_t_ps, d_t_ps, f_t_ps, m_t_ps, msg_ps = (ctx.psum(n, [P, 512], F32)
                                                  for n in ("s_t_ps", "d_t_ps", "f_t_ps", "m_t_ps", "msg_ps"))
        ready = ctx.semaphore("ready")
        idx_in = DmaRing(ctx, nc, "idx_in", 2, ring=GR)
        feats_in = DmaRing(ctx, nc, "feats_in")
        gathered = DmaRing(ctx, nc, "gathered", 2 * GT, pool=True)
        turned = Count(ctx, nc, "turned")
        s_copied = Count(ctx, nc, "s_copied")
        d_copied = Count(ctx, nc, "d_copied")
        f_made = Count(ctx, nc, "f_made")
        multiplied = Count(ctx, nc, "multiplied")
        m_made = Count(ctx, nc, "m_made")
        counted = Count(ctx, nc, "counted")
        turned_back = Count(ctx, nc, "turned_back")
        msg_made = Count(ctx, nc, "msg_made")
        node_sum = NodeSum(ctx, nc, c, 2)
        block = ctx.enter_context(nc.Block())

        @block.sync
        def _(sp):
            def load(i, k, T, rows):
                g = i * GR + k
                wait_apart(nc.sync, ready, (turned.sem, turned.free(g, GR)))
                sp.dma_start(idx[0:rows, k % GR, 0, 0:T], idx_cols(c.src_cols, c.src, g, rows))\
                    .then_inc(idx_in.sem(k), 16)
                sp.dma_start(idx[0:rows, k % GR, 1, 0:T], idx_cols(c.dst_cols, c.dst, g, rows))\
                    .then_inc(idx_in.sem(k), 16)

            def load_feats(i, k, T, rows):
                g = i * GR + k
                wait_apart(nc.sync, ready, (turned.sem, turned.free(g, RING)))
                sp.dma_start(feats[0:4, k % RING, 0:T * rows], group_cols(edge4_t, g, rows)).then_inc(feats_in.sem(k), 16)
            sp.wait_ge(ready, 1)
            laps(nc.sync, [(3, load), (0, load_feats)])

        @block.gpsimd
        def _(pool):
            take = PoolTakes(nc, ctx.tag)
            idx_at = take.ring(idx_in.done(0, 0), idx_in)
            turned_at = take.counter(turned.free(0, RING), 1)

            def gather(i, k, T, rows):
                take.next_group(k, [turned_at])
                idx_value, turned_value = take.value(idx_at), take.value(turned_at)
                pool.wait_ge(ready, 1)
                pool.wait_ge(idx_in.sem(k), idx_value)
                pool.wait_ge(turned.sem, turned_value)
                for side, to in enumerate((rows_s, rows_d)):
                    for j in range(T):
                        gather_tile(nc, to[0:rows, k % RING, j, :], x, idx[0:rows, k % GR, side, j:j + 1])\
                            .then_inc(gathered.sem(k), 16 * GT if T == 1 else 16)
            laps(nc.gpsimd, [(0, gather)])

        @block.tensor
        def _(pe):
            def turn(i, k, T, rows):
                g = i * GR + k
                pe.wait_ge(feats_in.sem(k), feats_in.done(i, k))
                pe.wait_ge(f_made.sem, f_made.free(g, 1))
                nc.tensor.matmul(f_t_ps[0:D, 0:T * rows], c.w_edge4[:], feats[:, k % RING, 0:T * rows],
                                 start=True, stop=True)
                pe.wait_ge(gathered.sem(k), gathered.done(i, k))
                pe.wait_ge(s_copied.sem, s_copied.free(g, 1))
                transposed(nc, s_t_ps, T, rows, D, lambda j: rows_s[0:rows, k % RING, j, :], c.ident)
                pe.wait_ge(d_copied.sem, d_copied.free(g, 1))
                transposed(nc, d_t_ps, T, rows, D, lambda j: rows_d[0:rows, k % RING, j, :], c.ident)\
                    .then_inc(turned.sem, 1)

            def multiply(i, k, T, rows):
                g = i * GR + k
                pe.wait_ge(s_copied.sem, s_copied.done(g))
                pe.wait_ge(d_copied.sem, d_copied.done(g))
                pe.wait_ge(f_made.sem, f_made.done(g))
                pe.wait_ge(m_made.sem, m_made.free(g, 1))
                n = T * rows
                to = m_t_ps[0:D, 0:n]
                nc.tensor.matmul(to, c.w_src[:], s_t[:, k % 2, 0:n], start=True, stop=False)
                nc.tensor.matmul(to, c.w_dst[:], d_t[:, k % 2, 0:n], start=False, stop=False)
                nc.tensor.matmul(to, c.w_feat[:], f_t[:, k % 2, 0:n], start=False, stop=True).then_inc(multiplied.sem, 1)

            def turn_back(i, k, T, rows):
                g = i * GR + k
                pe.wait_ge(m_made.sem, m_made.done(g))
                pe.wait_ge(msg_made.sem, msg_made.free(g, 1))
                for j in range(T):
                    last = nc.tensor.transpose(msg_ps[0:rows, j * D:(j + 1) * D], m_t[:, k % 2, j * P:j * P + rows],
                                               c.ident[0:D, 0:D])
                last.then_inc(turned_back.sem, 1)
            add_up = node_sum.on_tensor(pe, lambda k, j, rows: msg[0:rows, k % 2, j, :],
                                        lambda i, k: pe.wait_ge(msg_made.sem, msg_made.done(i * GR + k)))
            pe.wait_ge(ready, 1)
            laps(nc.tensor, [(3, turn), (2, multiply), (1, turn_back), (0, add_up)])

        @block.scalar
        def _(act):
            def copy_s(i, k, T, rows):
                g = i * GR + k
                act.wait_ge(turned.sem, turned.done(g))
                act.wait_ge(multiplied.sem, multiplied.free(g, 2))
                nc.scalar.copy(s_t[0:D, k % 2, 0:T * rows], s_t_ps[0:D, 0:T * rows]).then_inc(s_copied.sem, 1)
                nc.scalar.activation(f_t[:, k % 2, 0:T * rows], f_t_ps[0:D, 0:T * rows], ACT.Relu).then_inc(f_made.sem, 1)

            def rectify(i, k, T, rows):
                g = i * GR + k
                act.wait_ge(multiplied.sem, multiplied.done(g))
                act.wait_ge(counted.sem, counted.free(g, 2))
                act.wait_ge(turned_back.sem, turned_back.free(g, 2))
                nc.scalar.activation(m_t[:, k % 2, 0:T * rows], m_t_ps[0:D, 0:T * rows], ACT.Relu).then_inc(m_made.sem, 1)

            def copy_back(i, k, T, rows):
                g = i * GR + k
                act.wait_ge(turned_back.sem, turned_back.done(g))
                act.wait_ge(node_sum.summed.sem, node_sum.summed.free(g * GT + GT - 1, 2 * GT))
                nc.scalar.copy(msg[0:rows, k % 2, 0:T, 0:D],
                               msg_ps[0:rows, 0:T * D].rearrange("p (a b) -> p a b", a=T)).then_inc(msg_made.sem, 1)
            laps(nc.scalar, [(3, copy_s), (2, rectify), (1, copy_back)])

        @block.vector
        def _(dve):
            nc.vector.memset(feats[:], 1.0)
            nc.vector.memset(s_t[D:W, :, :], 1.0)
            nc.vector.memset(msg[:, :, :, D:W], 1.0).then_inc(ready, 1)

            def copy_d(i, k, T, rows):
                g = i * GR + k
                dve.wait_ge(turned.sem, turned.done(g))
                dve.wait_ge(multiplied.sem, multiplied.free(g, 2))
                nc.vector.tensor_copy(d_t[:, k % 2, 0:T * rows], d_t_ps[0:D, 0:T * rows]).then_inc(d_copied.sem, 1)

            def count(i, k, T, rows):
                g = i * GR + k
                dve.wait_ge(m_made.sem, m_made.done(g))
                nc.vector.bn_stats(record(c.stat_msg, g), m_t[:, k % 2, 0:T * rows]).then_inc(counted.sem, 1)
            laps(nc.vector, [(3, copy_d), (2, count), *node_sum.on_vector(dve)])


def message_nodes(nc, c, x, x_out):
    with Phase(nc) as ctx:
        def sb(name, shape, dt=F32):
            return ctx.sbuf(name, shape, dt)

        x_in = sb("x_in", [P, GR, GT, D])
        z = sb("z", [P, 2, GT, D])
        sums = sb("sums", [P, 2, GT, W])
        x_t = sb("x_t", [D, 2, GT * P])
        s_t = sb("s_t", [W, 2, GT * P])
        f_t = sb("f_t", [W, 2, GT * P])
        res = sb("res", [P, RING, GT, D])
        terms_n = sb("terms_n", [D, 2])
        terms_m = sb("terms_m", [D, 2])
        left_n = sb("left_n", [D, W])
        left_m = sb("left_m", [D, W])
        scale_m = sb("scale_m", [W, D])
        scale_n = sb("scale_n", [W, D])
        x_t_ps = ctx.psum("x_t_ps", [P, 2, 512], F32)
        s_t_ps = ctx.psum("s_t_ps", [P, 2, 512], F32)
        f_t_ps = ctx.psum("f_t_ps", [P, 512], F32)
        z_ps = ctx.psum("z_ps", [P, 2, 512], F32)
        small_ps = ctx.psum("small_ps", [P, 512], F32)
        ready = ctx.semaphore("ready")
        folding = ctx.semaphore("folding")
        folded = ctx.semaphore("folded")
        constants = ctx.semaphore("constants")
        norm_n = Norm(ctx, nc, "nodes")
        norm_m = Norm(ctx, nc, "messages")
        loaded = DmaRing(ctx, nc, "loaded", ring=GR)
        stored = DmaRing(ctx, nc, "stored")
        taken = Count(ctx, nc, "taken")
        x_turned = Count(ctx, nc, "x_turned")
        s_turned = Count(ctx, nc, "s_turned")
        x_copied = Count(ctx, nc, "x_copied")
        s_copied = Count(ctx, nc, "s_copied")
        projected = Count(ctx, nc, "projected")
        f_made = Count(ctx, nc, "f_made")
        joined = Count(ctx, nc, "joined")
        z_made = Count(ctx, nc, "z_made")
        res_made = Count(ctx, nc, "res_made")
        norm = RowNorm(ctx, nc, c, "norm", ready)
        block = ctx.enter_context(nc.Block())

        @block.sync
        def _(sp):
            def load(i, k, T, rows):
                g = i * GR + k
                wait_apart(nc.sync, ready, (z_made.sem, z_made.free(g, GR)))
                sp.dma_start(x_in[0:rows, k % GR, 0:T, :], group_rows(x, g, T, rows)).then_inc(loaded.sem(k), 16)
            sp.wait_ge(ready, 1)
            laps(nc.sync, [(0, load)])
            wait_stores(sp, stored)

        @block.gpsimd
        def _(pool):
            def take(i, k, T, rows):
                take_sums(nc, c, ready, taken, s_turned, sums, i * GR + k, k, T)
            laps(nc.gpsimd, [(0, take)])

        @block.tensor
        def _(pe):
            pe.wait_ge(folding, 2)
            nc.tensor.matmul(small_ps[0:W, 0:D], left_n[:], c.ident[0:D, 0:D], start=True, stop=True)
            nc.tensor.matmul(small_ps[0:W, D:2 * D], left_m[:], c.ident[0:D, 0:D], start=True, stop=True)\
                .then_inc(folded, 1)
            pe.wait_ge(constants, 2)
            pe.wait_ge(ready, 1)

            def turn_x(i, k, T, rows):
                g = i * GR + k
                pe.wait_ge(loaded.sem(k), loaded.done(i, k))
                pe.wait_ge(x_copied.sem, x_copied.free(g, 2))
                transposed(nc, x_t_ps[:, k % 2, :], T, rows, D, lambda j: x_in[0:rows, k % GR, j, :], c.ident)\
                    .then_inc(x_turned.sem, 1)

            def turn_s(i, k, T, rows):
                g = i * GR + k
                pe.wait_ge(taken.sem, taken.done(g))
                pe.wait_ge(s_copied.sem, s_copied.free(g, 2))
                transposed(nc, s_t_ps[:, k % 2, :], T, rows, W, lambda j: sums[0:rows, k % 2, j, :], c.ident)\
                    .then_inc(s_turned.sem, 1)

            def project(i, k, T, rows):
                g = i * GR + k
                pe.wait_ge(x_copied.sem, x_copied.done(g))
                pe.wait_ge(f_made.sem, f_made.free(g, 1))
                nc.tensor.matmul(f_t_ps[0:D, 0:T * rows], c.w_node[:], x_t[:, k % 2, 0:T * rows],
                                 start=True, stop=True).then_inc(projected.sem, 1)

            def join(i, k, T, rows):
                g = i * GR + k
                pe.wait_ge(s_copied.sem, s_copied.done(g))
                pe.wait_ge(f_made.sem, f_made.done(g))
                pe.wait_ge(z_made.sem, z_made.free(g, 2))
                for j in range(T):
                    to = z_ps[0:rows, k % 2, j * D:(j + 1) * D]
                    at = slice(j * P, j * P + rows)
                    nc.tensor.matmul(to, s_t[:, k % 2, at], scale_m[:], start=True, stop=False)
                    last = nc.tensor.matmul(to, f_t[:, k % 2, at], scale_n[:], start=False, stop=True)
                last.then_inc(joined.sem, 1)
            laps(nc.tensor, [(3, turn_x), (2, turn_s), (1, project), (0, join)])

        @block.scalar
        def _(act):
            norm_n.on_scalar(act)
            norm_m.on_scalar(act)

            def copy_x(i, k, T, rows):
                g = i * GR + k
                act.wait_ge(x_turned.sem, x_turned.done(g))
                act.wait_ge(projected.sem, projected.free(g, 2))
                nc.scalar.copy(x_t[:, k % 2, 0:T * rows], x_t_ps[0:D, k % 2, 0:T * rows]).then_inc(x_copied.sem, 1)

            def rectify(i, k, T, rows):
                g = i * GR + k
                act.wait_ge(projected.sem, projected.done(g))
                act.wait_ge(joined.sem, joined.free(g, 2))
                nc.scalar.activation(f_t[0:D, k % 2, 0:T * rows], f_t_ps[0:D, 0:T * rows], ACT.Relu,
                                     bias=column(c, "b_node")).then_inc(f_made.sem, 1)

            def normalise(i, k, T, rows):
                g = i * GR + k
                act.wait_ge(stored.sem(k), stored.free(i, k))
                norm.apply(act, g, k % 2, T, rows, lambda j: z[0:rows, k % 2, j, :],
                           lambda j: res[0:rows, k % RING, j, :]).then_inc(res_made.sem, 1)
            def store(i, k, T, rows):
                g = i * GR + k
                act.wait_ge(res_made.sem, res_made.done(g))
                nc.scalar.dma_start(group_rows(x_out, g, T, rows), res[0:rows, k % RING, 0:T, :])\
                    .then_inc(stored.sem(k), 16)

            def deviate(i, k, T, rows):
                norm.deviate(act, i * GR + k, k % 2, T, rows)

            laps(nc.scalar, [(2, rectify), (0, normalise), (4, copy_x), (1, deviate), (0, store)])

        @block.vector
        def _(dve):
            nc.vector.memset(f_t[D:W, :, :], 1.0).then_inc(ready, 1)
            norm_n.on_vector(dve, c.stat, column(c, "g_node"), column(c, "beta_node"), terms_n)
            norm_m.on_vector(dve, c.stat_msg, column(c, "g_msg"), column(c, "beta_msg"), terms_m)
            eye = c.ident[0:D, 0:D]
            nc.vector.tensor_scalar(left_n[:, 0:D], eye, terms_n[:, 0:1], None, ALU.mult)
            nc.vector.tensor_copy(left_n[:, D:W], terms_n[:, 1:2]).then_inc(folding, 1)
            nc.vector.tensor_scalar(left_m[:, 0:D], eye, terms_m[:, 0:1], None, ALU.mult)
            nc.vector.tensor_copy(left_m[:, D:W], terms_m[:, 1:2]).then_inc(folding, 1)
            dve.wait_ge(folded, 1)
            nc.vector.tensor_copy(scale_n[:], small_ps[0:W, 0:D]).then_inc(constants, 1)
            nc.vector.tensor_copy(scale_m[:], small_ps[0:W, D:2 * D]).then_inc(constants, 1)

            def copy_s(i, k, T, rows):
                g = i * GR + k
                dve.wait_ge(s_turned.sem, s_turned.done(g))
                dve.wait_ge(joined.sem, joined.free(g, 2))
                nc.vector.tensor_copy(s_t[:, k % 2, 0:T * rows], s_t_ps[0:W, k % 2, 0:T * rows]).then_inc(s_copied.sem, 1)

            def join(i, k, T, rows):
                g = i * GR + k
                dve.wait_ge(joined.sem, joined.done(g))
                dve.wait_ge(loaded.sem(k), loaded.done(i, k))
                dve.wait_ge(res_made.sem, res_made.free(g, 2))
                nc.vector.tensor_tensor(flat(z[0:rows, k % 2, 0:T, :]), flat(x_in[0:rows, k % GR, 0:T, :]),
                                        z_ps[0:rows, k % 2, 0:T * D], ALU.add).then_inc(z_made.sem, 1)

            def record_z(i, k, T, rows):
                g = i * GR + k
                dve.wait_ge(z_made.sem, z_made.done(g))
                norm.records(g, k % 2, T, rows, lambda j: z[0:rows, k % 2, j, :])

            def moments(i, k, T, rows):
                norm.moments(i * GR + k, k % 2, T, rows)

            def invert(i, k, T, rows):
                norm.invert(dve, i * GR + k, k % 2, T, rows)

            def make_bias(i, k, T, rows):
                norm.make_bias(dve, i * GR + k, k % 2, T, rows)

            laps(nc.vector, [(0, invert), (3, copy_s), (0, make_bias), (1, join), (1, record_z), (1, moments)])


def mlp_nodes(nc, c, x):
    with Phase(nc) as ctx:
        def sb(name, shape, dt=F32):
            return ctx.sbuf(name, shape, dt)

        x_in = sb("x_in", [P, RING, GT, D])
        h = sb("h", [P, 2, GT, D])
        h_t = sb("h_t", [D, 2, GT * P])
        r_t = sb("r_t", [W, 2, GT * P])
        h_t_ps = ctx.psum("h_t_ps", [P, 2, 512], F32)
        r_t_ps = ctx.psum("r_t_ps", [P, 2, 512], F32)
        h2_t_ps = ctx.psum("h2_t_ps", [P, 512], F32)
        h2_ps = ctx.psum("h2_ps", [P, 2, 512], F32)
        ready = ctx.semaphore("ready")
        loaded = DmaRing(ctx, nc, "loaded")
        h_made = Count(ctx, nc, "h_made")
        turned = Count(ctx, nc, "turned")
        copied = Count(ctx, nc, "copied")
        first = Count(ctx, nc, "first")
        rectified = Count(ctx, nc, "rectified")
        second_t = Count(ctx, nc, "second_t")
        second = Count(ctx, nc, "second")
        counted = Count(ctx, nc, "counted")
        kept = Count(ctx, nc, "kept")
        block = ctx.enter_context(nc.Block())

        @block.sync
        def _(sp):
            def load(i, k, T, rows):
                g = i * GR + k
                wait_apart(nc.sync, ready, (h_made.sem, h_made.free(g, RING)))
                sp.dma_start(x_in[0:rows, k % RING, 0:T, :], group_rows(x, g, T, rows)).then_inc(loaded.sem(k), 16)
            sp.wait_ge(ready, 1)
            laps(nc.sync, [(0, load)])

        @block.gpsimd
        def _(pool):
            def join(i, k, T, rows):
                g = i * GR + k
                wait_apart(nc.gpsimd, ready, (loaded.sem(k), loaded.done(i, k)), (turned.sem, turned.free(g, 2)))
                nc.gpsimd.tensor_tensor(h[0:rows, k % 2, 0:T, :], x_in[0:rows, k % RING, 0:T, :],
                                        c.node_tab[0:rows, bass.ds(g * GT, T), 0:D], ALU.add).then_inc(h_made.sem, 1)
            laps(nc.gpsimd, [(0, join)])

        @block.tensor
        def _(pe):
            def turn(i, k, T, rows):
                g = i * GR + k
                pe.wait_ge(h_made.sem, h_made.done(g))
                pe.wait_ge(copied.sem, copied.free(g, 2))
                transposed(nc, h_t_ps[:, k % 2, :], T, rows, D, lambda j: h[0:rows, k % 2, j, :], c.ident)\
                    .then_inc(turned.sem, 1)

            def one(i, k, T, rows):
                g = i * GR + k
                pe.wait_ge(copied.sem, copied.done(g))
                pe.wait_ge(rectified.sem, rectified.free(g, 2))
                nc.tensor.matmul(r_t_ps[0:D, k % 2, 0:T * rows], c.w1[:], h_t[:, k % 2, 0:T * rows],
                                 start=True, stop=True).then_inc(first.sem, 1)

            def two(i, k, T, rows):
                g = i * GR + k
                pe.wait_ge(rectified.sem, rectified.done(g))
                pe.wait_ge(counted.sem, counted.free(g, 1))
                nc.tensor.matmul(h2_t_ps[0:D, 0:T * rows], c.w2[:], r_t[:, k % 2, 0:T * rows],
                                 start=True, stop=True).then_inc(second_t.sem, 1)
                pe.wait_ge(kept.sem, kept.free(g, 2))
                for j in range(T):
                    last = nc.tensor.matmul(h2_ps[0:rows, k % 2, j * D:(j + 1) * D], r_t[:, k % 2, j * P:j * P + rows],
                                            c.w2[:], start=True, stop=True)
                last.then_inc(second.sem, 1)
            pe.wait_ge(ready, 1)
            laps(nc.tensor, [(2, turn), (1, one), (0, two)])

        @block.scalar
        def _(act):
            def copy_h(i, k, T, rows):
                g = i * GR + k
                act.wait_ge(turned.sem, turned.done(g))
                act.wait_ge(first.sem, first.free(g, 2))
                nc.scalar.copy(h_t[:, k % 2, 0:T * rows], h_t_ps[0:D, k % 2, 0:T * rows]).then_inc(copied.sem, 1)

            def rectify(i, k, T, rows):
                g = i * GR + k
                act.wait_ge(first.sem, first.done(g))
                act.wait_ge(second.sem, second.free(g, 2))
                nc.scalar.activation(r_t[0:D, k % 2, 0:T * rows], r_t_ps[0:D, k % 2, 0:T * rows], ACT.Relu,
                                     bias=column(c, "b1")).then_inc(rectified.sem, 1)
            laps(nc.scalar, [(1, copy_h), (0, rectify)])

        @block.vector
        def _(dve):
            nc.vector.memset(r_t[D:W, :, :], 1.0).then_inc(ready, 1)

            def count(i, k, T, rows):
                g = i * GR + k
                dve.wait_ge(second_t.sem, second_t.done(g))
                nc.vector.bn_stats(record(c.stat, g), h2_t_ps[0:D, 0:T * rows]).then_inc(counted.sem, 1)

            def keep(i, k, T, rows):
                g = i * GR + k
                dve.wait_ge(second.sem, second.done(g))
                dve.wait_ge(h_made.sem, h_made.done(g))
                nc.vector.tensor_copy(c.node_tab[0:rows, bass.ds(g * GT, T), 0:D],
                                      h2_ps[0:rows, k % 2, 0:T * D].rearrange("p (a b) -> p a b", a=T))\
                    .then_inc(kept.sem, 1)
            laps(nc.vector, [(0, count), (0, keep)])


def out_nodes(nc, c, x, out):
    with Phase(nc) as ctx:
        def sb(name, shape, dt=F32):
            return ctx.sbuf(name, shape, dt)

        x_in = sb("x_in", [P, RING, GT, D])
        scaled = sb("scaled", [P, 2, GT, D])
        z = sb("z", [P, 2, GT, D])
        res = sb("res", [P, RING, GT, D])
        terms = sb("terms", [D, 2])
        diag = sb("diag", [D, 2, D])
        scale = sb("scale", [P, GT, D])
        shift = sb("shift", [P, GT, D])
        rows_ps = ctx.psum("rows_ps", [P, 512], F32)
        ready = ctx.semaphore("ready")
        diag_made = ctx.semaphore("diag_made")
        spread_out = ctx.semaphore("spread_out")
        norm_h = Norm(ctx, nc, "h2")
        loaded = DmaRing(ctx, nc, "loaded")
        stored = DmaRing(ctx, nc, "stored")
        scaled_made = Count(ctx, nc, "scaled_made")
        shifted = Count(ctx, nc, "shifted")
        z_made = Count(ctx, nc, "z_made")
        res_made = Count(ctx, nc, "res_made")
        norm = RowNorm(ctx, nc, c, "norm", ready)
        block = ctx.enter_context(nc.Block())

        @block.sync
        def _(sp):
            def load(i, k, T, rows):
                g = i * GR + k
                wait_apart(nc.sync, ready, (z_made.sem, z_made.free(g, RING)))
                sp.dma_start(x_in[0:rows, k % RING, 0:T, :], group_rows(x, g, T, rows)).then_inc(loaded.sem(k), 16)
            sp.wait_ge(ready, 1)
            laps(nc.sync, [(0, load)])
            wait_stores(sp, stored)

        @block.tensor
        def _(pe):
            pe.wait_ge(diag_made, 2)
            for n in range(2):
                last = nc.tensor.matmul(rows_ps[:, n * D:(n + 1) * D], c.ones[0:D, :], diag[:, n, :], start=True, stop=True)
            last.then_inc(spread_out, 1)

        @block.gpsimd
        def _(pool):
            def multiply(i, k, T, rows):
                g = i * GR + k
                wait_apart(nc.gpsimd, ready, (z_made.sem, z_made.free(g, 2)))
                nc.gpsimd.tensor_tensor(scaled[0:rows, k % 2, 0:T, :], c.node_tab[0:rows, bass.ds(g * GT, T), 0:D],
                                        scale[0:rows, 0:T, :], ALU.mult).then_inc(scaled_made.sem, 1)
            pool.wait_ge(ready, 1)
            laps(nc.gpsimd, [(0, multiply)])

        @block.scalar
        def _(act):
            norm_h.on_scalar(act)

            def normalise(i, k, T, rows):
                g = i * GR + k
                act.wait_ge(stored.sem(k), stored.free(i, k))
                norm.apply(act, g, k % 2, T, rows, lambda j: z[0:rows, k % 2, j, :],
                           lambda j: res[0:rows, k % RING, j, :]).then_inc(res_made.sem, 1)
            def store(i, k, T, rows):
                g = i * GR + k
                act.wait_ge(res_made.sem, res_made.done(g))
                nc.scalar.dma_start(group_rows(out, g, T, rows), res[0:rows, k % RING, 0:T, :])\
                    .then_inc(stored.sem(k), 16)

            def deviate(i, k, T, rows):
                norm.deviate(act, i * GR + k, k % 2, T, rows)

            laps(nc.scalar, [(1, normalise), (2, deviate), (0, store)])

        @block.vector
        def _(dve):
            norm_h.on_vector(dve, c.stat, column(c, "gamma"), column(c, "beta"), terms)
            for n in range(2):
                nc.vector.tensor_scalar(diag[:, n, :], c.ident[0:D, 0:D], terms[:, n:n + 1], None, ALU.mult)\
                    .then_inc(diag_made, 1)
            dve.wait_ge(spread_out, 1)
            for n, to in enumerate((scale, shift)):
                for j in range(GT):
                    last = nc.vector.tensor_copy(to[:, j, :], rows_ps[:, n * D:(n + 1) * D])
            last.then_inc(ready, 1)

            def add_shift(i, k, T, rows):
                g = i * GR + k
                dve.wait_ge(scaled_made.sem, scaled_made.done(g))
                u = flat(scaled[0:rows, k % 2, 0:T, :])
                nc.vector.tensor_tensor(u, u, flat(shift[0:rows, 0:T, :]), ALU.add).then_inc(shifted.sem, 1)

            def join(i, k, T, rows):
                g = i * GR + k
                dve.wait_ge(shifted.sem, shifted.done(g))
                dve.wait_ge(loaded.sem(k), loaded.done(i, k))
                dve.wait_ge(res_made.sem, res_made.free(g, 2))
                nc.vector.scalar_tensor_tensor(flat(z[0:rows, k % 2, 0:T, :]), flat(scaled[0:rows, k % 2, 0:T, :]), 0.0,
                                               flat(x_in[0:rows, k % RING, 0:T, :]), ALU.max, ALU.add)\
                    .then_inc(z_made.sem, 1)

            def record_z(i, k, T, rows):
                g = i * GR + k
                dve.wait_ge(z_made.sem, z_made.done(g))
                norm.records(g, k % 2, T, rows, lambda j: z[0:rows, k % 2, j, :])

            def moments(i, k, T, rows):
                norm.moments(i * GR + k, k % 2, T, rows)

            def invert(i, k, T, rows):
                norm.invert(dve, i * GR + k, k % 2, T, rows)

            def make_bias(i, k, T, rows):
                norm.make_bias(dve, i * GR + k, k % 2, T, rows)

            dve.wait_ge(ready, 1)
            laps(nc.vector, [(0, invert), (0, make_bias), (1, join), (1, record_z), (2, add_shift), (1, moments)])


def wait_stores(sp, stored):
    for k in range(RING):
        last = max(g for g in range(GROUPS + 1) if g % RING == k)
        sp.wait_ge(stored.sem(k), stored.done(last // GR, last % GR))


def given_arrays(np, inputs):
    a = {k: np.asarray(v) for k, v in inputs.items()}
    out = {"x": a["x"], "x_t": a["x"].T, "src": a["src"], "dst": a["dst"],
           "src_cols": a["src"][:TILES * P].reshape(TILES, P).T,
           "dst_cols": a["dst"][:TILES * P].reshape(TILES, P).T,
           "edge4_t": a["edge_attr_4"].T, "edge32_t": a["edge_attr_32"].T}
    unit = np.zeros((1, W), np.float32)
    unit[0, D] = 1
    for l in range(2):
        w0, b0 = a["L0_gnn_W0"][l], a["L0_gnn_b0"][l]
        w1, b1 = a["L0_gnn_W1"][l], a["L0_gnn_b1"][l]
        w2, b2 = a["L0_gnn_W2"][l], a["L0_gnn_b2"][l]
        out[f"self_t{l}"] = np.concatenate([np.concatenate([w1, b1[None]]).T, unit])
        out[f"near_t{l}"] = np.concatenate([w0, b0[None]]).T
        out[f"w2_self{l}"] = np.concatenate([w2[:D], b2[None]])
        out[f"w2_near{l}"] = w2[D:]
    wm = a["L2_gnn_W_msg"]
    out["w_src"] = np.concatenate([wm[:D], a["L2_gnn_b_msg"][None]])
    out["w_dst"] = wm[D:2 * D]
    out["w_feat"] = wm[2 * D:]
    out["w_edge4"] = np.concatenate([a["L2_gnn_W_edge"], a["L2_gnn_b_edge"][None]])
    out["qkv"] = np.concatenate([a["L1_gnn_qW"], a["L1_gnn_kW"], a["L1_gnn_vW"]], axis=1)
    out["w_node"] = a["L2_gnn_W_node"]
    out["w_edge32"] = np.concatenate([a["L3_gnn_We"], a["L3_gnn_be"][None]])
    out["w1"] = a["L3_gnn_W1"]
    out["w2"] = np.concatenate([a["L3_gnn_W2"], a["L3_gnn_b2"][None]])
    out["cols"] = np.stack([a["L2_gnn_b_node"], a["L2_gnn_g_node"], a["L2_gnn_beta_node"], a["L2_gnn_g_edge"],
                            a["L2_gnn_beta_edge"], a["L2_gnn_g_msg"], a["L2_gnn_beta_msg"], a["L3_gnn_b1"],
                            a["L3_gnn_gamma"], a["L3_gnn_beta"]], axis=1)
    return {k: np.ascontiguousarray(v) for k, v in out.items()}


def kernel(**inputs):
    import numpy as np
    import concourse.bacc as bacc
    from concourse.bass_utils import run_bass_kernel_spmd as run

    nc = bacc.Bacc("TRN2", target_bir_lowering=False, num_devices=1)
    arrays = given_arrays(np, inputs)
    given = {k: nc.dram_tensor(f"in_{k}", a.shape, mybir.dt.from_np(a.dtype), kind="ExternalInput").ap()
             for k, a in arrays.items()}
    out = nc.dram_tensor("out", (N, D), F32, kind="ExternalOutput").ap()
    gnn(nc, given, out)
    r = run(nc, [{f"in_{k}": a for k, a in arrays.items()}], core_ids=[0])
    return r.results[0]["out"]
```
